# Optimizing a Trainium2 kernel written in Bass

```python
import numpy as np
import jax
import jax.numpy as jnp

def _softmax(x, axis=-1):
    return jax.nn.softmax(x, axis=axis)

def _gelu(x):
    return jax.nn.gelu(x, approximate=True)

def _silu(x):
    return jax.nn.silu(x)

def _sigmoid(x):
    return jax.nn.sigmoid(x)

def _layernorm(x, axis=-1, eps=1e-05):
    m = jnp.mean(x, axis=axis, keepdims=True)
    v = jnp.var(x, axis=axis, keepdims=True)
    return (x - m) / jnp.sqrt(v + eps)

def _scatter_add(tgt, idx, src, axis=0):
    return tgt.at[idx].add(src)

def _segment_sum(src, seg, n):
    return jax.ops.segment_sum(src, seg, n)
kernel_name = 'mk_sandwich_d4_jaxref_r8_8b810b'

def setup_inputs(seed: int=0):
    np.random.seed(seed)
    _w = jnp.asarray

    def _L0_attn_setup():
        import jax, jax.numpy as jnp
        from jax import lax
        import numpy as np
        D_MODEL = 128
        K = 32
        K_Q = 4
        N_ANCHOR = 4
        N_DECAY = K - N_ANCHOR
        M = 8
        KS = 4
        H = D_MODEL // K
        N_REP = K // K_Q
        DIM_K = D_MODEL
        DIM_DECAY = K
        DIM_Q = K_Q * H * M * 2
        TOTAL = DIM_K + DIM_DECAY + DIM_Q
        B, L = (2, 256)
        key = jax.random.key(seed)
        ks = jax.random.split(key, 8)
        x = jax.random.normal(ks[0], (B, L, D_MODEL), jnp.float32)
        W_in = jax.random.normal(ks[1], (D_MODEL, TOTAL), jnp.float32) * D_MODEL ** (-0.5)
        conv_k = jax.random.normal(ks[2], (KS, 1, DIM_K + DIM_DECAY), jnp.float32) * 0.3
        grid = np.linspace(-np.pi / 3, np.pi / 3, M)
        theta = jnp.asarray(np.tile(grid.reshape(1, 1, 1, 1, M), (1, 1, K, H, 1)), jnp.float32)
        decay_slopes = jnp.log(jnp.exp(jnp.asarray(np.geomspace(0.001, 0.1, N_DECAY), jnp.float32)) - 1.0)
        anchor_slopes = jnp.log(jnp.exp(jnp.asarray(np.geomspace(0.01, 0.1, N_ANCHOR), jnp.float32)) - 1.0)
        score_scale = jnp.ones((K,), jnp.float32)
        lim = float(np.sqrt(6.0 / (H + H)))
        W_re = jax.random.uniform(ks[3], (H, H), jnp.float32, -lim, lim)
        W_im = jax.random.uniform(ks[4], (H, H), jnp.float32, -lim, lim)
        norm_scale = jnp.ones((2 * H,), jnp.float32)
        W_out = jax.random.normal(ks[5], (D_MODEL, D_MODEL), jnp.float32) * D_MODEL ** (-0.5)
        return dict(x=x, W_in=W_in, conv_k=conv_k, theta=theta, decay_slopes=decay_slopes, anchor_slopes=anchor_slopes, score_scale=score_scale, W_re=W_re, W_im=W_im, norm_scale=norm_scale, W_out=W_out)
    _L0_attn_in = _L0_attn_setup()

    def _L0_ffn_setup():
        import jax, jax.numpy as jnp
        import numpy as np
        HIDDEN = 128
        INTER = 256
        NUM_EXPERTS = 8
        TOPK = 2
        STD = 0.02
        key = jax.random.key(seed)
        k1, k2, k3, k4 = jax.random.split(key, 4)
        return {'hidden_states': jax.random.normal(k1, (1, 256, HIDDEN), dtype=jnp.float32), 'w1': jax.random.normal(k2, (NUM_EXPERTS, 2 * INTER, HIDDEN), dtype=jnp.float32) * STD, 'w2': jax.random.normal(k3, (NUM_EXPERTS, HIDDEN, INTER), dtype=jnp.float32) * STD, 'router_w': jax.random.normal(k4, (NUM_EXPERTS, HIDDEN), dtype=jnp.float32) * STD}
    _L0_ffn_in = _L0_ffn_setup()

    def _L1_attn_setup():
        import jax, jax.numpy as jnp
        import numpy as np
        D_MODEL = 128
        NHEAD = 16
        BATCH = 2
        SEQ = 256
        key = jax.random.key(seed)
        ks = jax.random.split(key, 5)
        s = 0.02
        return {'x': jax.random.normal(ks[0], (BATCH, SEQ, D_MODEL), dtype=jnp.float32), 'Wqkv': jax.random.normal(ks[1], (3 * D_MODEL, D_MODEL), dtype=jnp.float32) * s, 'bqkv': jax.random.normal(ks[2], (3 * D_MODEL,), dtype=jnp.float32) * s, 'Wout': jax.random.normal(ks[3], (D_MODEL, D_MODEL), dtype=jnp.float32) * s, 'bout': jax.random.normal(ks[4], (D_MODEL,), dtype=jnp.float32) * s}
    _L1_attn_in = _L1_attn_setup()

    def _L1_ffn_setup():
        import jax, jax.numpy as jnp
        import numpy as np
        E = 8
        key = jax.random.key(seed)
        k0, k1, k2, k3 = jax.random.split(key, 4)
        B, S, H, F = (4, 512, 128, 512)
        x = jax.random.normal(k0, (B, S, H), jnp.float32)
        Wr = jax.random.normal(k1, (E, H), jnp.float32) * 0.02
        W1 = jax.random.normal(k2, (E, H, F), jnp.float32) * 0.02
        b1 = jnp.zeros((E, F), jnp.float32)
        W2 = jax.random.normal(k3, (E, F, H), jnp.float32) * 0.02
        b2 = jnp.zeros((E, H), jnp.float32)
        return {'x': x, 'Wr': Wr, 'W1': W1, 'b1': b1, 'W2': W2, 'b2': b2}
    _L1_ffn_in = _L1_ffn_setup()

    def _L2_attn_setup():
        import math
        import jax, jax.numpy as jnp
        import numpy as np
        N_HEAD = 16
        X_INT = -100.0
        Y_INT = 1.0
        POWER = 2
        DIVISOR = 1000.0

        def polymax(x):
            m = Y_INT / X_INT
            lin_cond = (x >= X_INT) & (x <= 0)
            x_lin = jnp.where(lin_cond, x, 0.0)
            lin = jnp.where(lin_cond, m * x_lin + Y_INT, 0.0)
            pos_cond = x > 0
            x_pos = jnp.where(pos_cond, x, 0.0)
            poly = jnp.where(pos_cond, x_pos ** POWER + Y_INT, 0.0)
            return (poly + lin) / DIVISOR
        key = jax.random.key(seed)
        k1, k2, k3 = jax.random.split(key, 3)
        B, T, C = (2, 256, 128)
        x = jax.random.normal(k1, (B, T, C), dtype=jnp.float32)
        W_attn = jax.random.normal(k2, (C, 3 * C), dtype=jnp.float32) * (1.0 / math.sqrt(C))
        W_proj = jax.random.normal(k3, (C, C), dtype=jnp.float32) * (1.0 / math.sqrt(C))
        return {'x': x, 'W_attn': W_attn, 'W_proj': W_proj}
    _L2_attn_in = _L2_attn_setup()

    def _L2_ffn_setup():
        import jax, jax.numpy as jnp
        import numpy as np
        NH, NKV, E, K = (16, 4, 8, 2)
        CAP_FACTOR = 1.25
        LN_EPS = 1e-05

        def _layer_norm(x, w, b):
            mu = jnp.mean(x, axis=-1, keepdims=True)
            var = jnp.mean(jnp.square(x - mu), axis=-1, keepdims=True)
            return (x - mu) * jax.lax.rsqrt(var + LN_EPS) * w + b
        key = jax.random.key(seed)
        ks = jax.random.split(key, 6)
        S, B, H, F = (256, 1, 128, 256)
        HD = H // NH
        qkv_out = NKV * (NH // NKV + 2) * HD
        f32 = jnp.float32
        return {'hidden_states': jax.random.normal(ks[0], (S, B, H), f32), 'ln1_weight': jnp.ones((H,), f32), 'ln1_bias': jnp.zeros((H,), f32), 'ln2_weight': jnp.ones((H,), f32), 'ln2_bias': jnp.zeros((H,), f32), 'qkv_weight': jax.random.normal(ks[1], (qkv_out, H), f32) * 0.02, 'proj_weight': jax.random.normal(ks[2], (H, H), f32) * 0.02, 'router_weight': jax.random.normal(ks[3], (H, E), f32) * 0.02, 'moe_w1': jax.random.normal(ks[4], (E, H, F), f32) * 0.02, 'moe_w2': jax.random.normal(ks[5], (F and E, F, H), f32)[:E] * 0.02 if False else jax.random.normal(ks[5], (E, F, H), f32) * 0.02}
    _L2_ffn_in = _L2_ffn_setup()

    def _L3_attn_setup():
        import jax, jax.numpy as jnp
        import numpy as np
        N_EMBD = 128
        N_HEAD = 16
        HEAD_DIM = N_EMBD // N_HEAD
        LATENT_DIM = N_EMBD // 2
        B, T = (4, 256)
        key = jax.random.key(seed)
        ks = jax.random.split(key, 5)

        def init(k, fan_in, fan_out):
            bound = 1.0 / np.sqrt(fan_in)
            return jax.random.uniform(k, (fan_in, fan_out), jnp.float32, -bound, bound)
        return {'x': jax.random.normal(ks[0], (B, T, N_EMBD), jnp.float32), 'Wc_down': init(ks[1], N_EMBD, LATENT_DIM), 'Wq_up': init(ks[2], LATENT_DIM, N_EMBD), 'Wkv_up': init(ks[3], LATENT_DIM, 2 * HEAD_DIM), 'Wc_proj': init(ks[4], N_EMBD, N_EMBD)}
    _L3_attn_in = _L3_attn_setup()

    def _L3_ffn_setup():
        import jax, jax.numpy as jnp
        import numpy as np
        B, S, H = (2, 128, 128)
        E, F = (16, 64)
        G, TOPK_G, TOPK = (4, 2, 4)
        N_SHARED = 2
        ROUTE_SCALE = 1.0
        FS = N_SHARED * F

        def _gate(x, w_gate):
            T = x.shape[0]
            scores = jax.nn.sigmoid(x @ w_gate.T)
            sv = scores.reshape(T, G, E // G)
            group_scores = jax.lax.top_k(sv, 2)[0].sum(-1)
            top_groups = jax.lax.top_k(group_scores, TOPK_G)[1]
            allowed = jnp.zeros((T, G), dtype=bool).at[jnp.arange(T)[:, None], top_groups].set(True)
            masked = jnp.where(allowed[:, :, None], sv, -jnp.inf).reshape(T, E)
            _, idx = jax.lax.top_k(masked, TOPK)
            w = jnp.take_along_axis(scores, idx, axis=1)
            w = w / (w.sum(-1, keepdims=True) + 1e-06) * ROUTE_SCALE
            return (w, idx)

        def _swiglu(x, w1, w3, w2):
            return jax.nn.silu(x @ w1.T) * (x @ w3.T) @ w2.T
        key = jax.random.key(seed)
        ks = jax.random.split(key, 8)
        scale = 0.02
        return {'hidden_states': jax.random.normal(ks[0], (B, S, H), dtype=jnp.float32), 'w_gate': jax.random.normal(ks[1], (E, H), dtype=jnp.float32) * scale, 'w1_e': jax.random.normal(ks[2], (E, F, H), dtype=jnp.float32) * scale, 'w3_e': jax.random.normal(ks[3], (E, F, H), dtype=jnp.float32) * scale, 'w2_e': jax.random.normal(ks[4], (E, H, F), dtype=jnp.float32) * scale, 'w1_s': jax.random.normal(ks[5], (FS, H), dtype=jnp.float32) * scale, 'w3_s': jax.random.normal(ks[6], (FS, H), dtype=jnp.float32) * scale, 'w2_s': jax.random.normal(ks[7], (H, FS), dtype=jnp.float32) * scale}
    _L3_ffn_in = _L3_ffn_setup()
    _d = {'L0_attn_x': _L0_attn_in['x'], 'L0_attn_W_in': _L0_attn_in['W_in'], 'L0_attn_conv_k': _L0_attn_in['conv_k'], 'L0_attn_theta': _L0_attn_in['theta'], 'L0_attn_decay_slopes': _L0_attn_in['decay_slopes'], 'L0_attn_anchor_slopes': _L0_attn_in['anchor_slopes'], 'L0_attn_score_scale': _L0_attn_in['score_scale'], 'L0_attn_W_re': _L0_attn_in['W_re'], 'L0_attn_W_im': _L0_attn_in['W_im'], 'L0_attn_norm_scale': _L0_attn_in['norm_scale'], 'L0_attn_W_out': _L0_attn_in['W_out'], 'L0_ffn_w1': _L0_ffn_in['w1'], 'L0_ffn_w2': _L0_ffn_in['w2'], 'L0_ffn_router_w': _L0_ffn_in['router_w'], 'L1_attn_Wqkv': _L1_attn_in['Wqkv'], 'L1_attn_bqkv': _L1_attn_in['bqkv'], 'L1_attn_Wout': _L1_attn_in['Wout'], 'L1_attn_bout': _L1_attn_in['bout'], 'L1_ffn_Wr': _L1_ffn_in['Wr'], 'L1_ffn_W1': _L1_ffn_in['W1'], 'L1_ffn_b1': _L1_ffn_in['b1'], 'L1_ffn_W2': _L1_ffn_in['W2'], 'L1_ffn_b2': _L1_ffn_in['b2'], 'L2_attn_W_attn': _L2_attn_in['W_attn'], 'L2_attn_W_proj': _L2_attn_in['W_proj'], 'L2_ffn_ln1_weight': _L2_ffn_in['ln1_weight'], 'L2_ffn_ln1_bias': _L2_ffn_in['ln1_bias'], 'L2_ffn_ln2_weight': _L2_ffn_in['ln2_weight'], 'L2_ffn_ln2_bias': _L2_ffn_in['ln2_bias'], 'L2_ffn_qkv_weight': _L2_ffn_in['qkv_weight'], 'L2_ffn_proj_weight': _L2_ffn_in['proj_weight'], 'L2_ffn_router_weight': _L2_ffn_in['router_weight'], 'L2_ffn_moe_w1': _L2_ffn_in['moe_w1'], 'L2_ffn_moe_w2': _L2_ffn_in['moe_w2'], 'L3_attn_Wc_down': _L3_attn_in['Wc_down'], 'L3_attn_Wq_up': _L3_attn_in['Wq_up'], 'L3_attn_Wkv_up': _L3_attn_in['Wkv_up'], 'L3_attn_Wc_proj': _L3_attn_in['Wc_proj'], 'L3_ffn_w_gate': _L3_ffn_in['w_gate'], 'L3_ffn_w1_e': _L3_ffn_in['w1_e'], 'L3_ffn_w3_e': _L3_ffn_in['w3_e'], 'L3_ffn_w2_e': _L3_ffn_in['w2_e'], 'L3_ffn_w1_s': _L3_ffn_in['w1_s'], 'L3_ffn_w3_s': _L3_ffn_in['w3_s'], 'L3_ffn_w2_s': _L3_ffn_in['w2_s']}
    _x0 = _d['L0_attn_x']
    _d['L0_attn_x'] = jax.random.normal(jax.random.fold_in(jax.random.key(seed), 1), (8, 256, 128), dtype=_x0.dtype)
    del _x0
    return _d

def reference(L0_attn_x, L0_attn_W_in, L0_attn_conv_k, L0_attn_theta, L0_attn_decay_slopes, L0_attn_anchor_slopes, L0_attn_score_scale, L0_attn_W_re, L0_attn_W_im, L0_attn_norm_scale, L0_attn_W_out, L0_ffn_w1, L0_ffn_w2, L0_ffn_router_w, L1_attn_Wqkv, L1_attn_bqkv, L1_attn_Wout, L1_attn_bout, L1_ffn_Wr, L1_ffn_W1, L1_ffn_b1, L1_ffn_W2, L1_ffn_b2, L2_attn_W_attn, L2_attn_W_proj, L2_ffn_ln1_weight, L2_ffn_ln1_bias, L2_ffn_ln2_weight, L2_ffn_ln2_bias, L2_ffn_qkv_weight, L2_ffn_proj_weight, L2_ffn_router_weight, L2_ffn_moe_w1, L2_ffn_moe_w2, L3_attn_Wc_down, L3_attn_Wq_up, L3_attn_Wkv_up, L3_attn_Wc_proj, L3_ffn_w_gate, L3_ffn_w1_e, L3_ffn_w3_e, L3_ffn_w2_e, L3_ffn_w1_s, L3_ffn_w3_s, L3_ffn_w2_s):

    def _L0_attn_ref(x, W_in, conv_k, theta, decay_slopes, anchor_slopes, score_scale, W_re, W_im, norm_scale, W_out):
        import jax, jax.numpy as jnp
        from jax import lax
        import numpy as np
        D_MODEL = 128
        K = 32
        K_Q = 4
        N_ANCHOR = 4
        N_DECAY = K - N_ANCHOR
        M = 8
        KS = 4
        H = D_MODEL // K
        N_REP = K // K_Q
        DIM_K = D_MODEL
        DIM_DECAY = K
        DIM_Q = K_Q * H * M * 2
        TOTAL = DIM_K + DIM_DECAY + DIM_Q
        B, L = (2, 256)
        b, l, _ = x.shape
        z = x @ W_in
        z_mem = z[..., :DIM_K + DIM_DECAY]
        q_raw = z[..., DIM_K + DIM_DECAY:]
        zp = jnp.pad(z_mem, ((0, 0), (KS - 1, 0), (0, 0)))
        z_mem = lax.conv_general_dilated(zp, conv_k, window_strides=(1,), padding='VALID', dimension_numbers=('NWC', 'WIO', 'NWC'), feature_group_count=DIM_K + DIM_DECAY)
        k_val = z_mem[..., :DIM_K].reshape(b, l, K, H)
        s_raw = z_mem[..., -K:].reshape(b, l, K, 1)
        q = q_raw.reshape(b, l, K_Q, H, M, 2)
        q_re, q_im = (q[..., 0], q[..., 1])
        pos = jnp.arange(l, dtype=jnp.float32)
        slopes_d = jax.nn.softplus(decay_slopes).reshape(1, 1, N_DECAY, 1)
        dist = jnp.maximum(jnp.float32(l - 1) - pos, 0.0)
        lw_d = -slopes_d * dist[None, :, None, None]
        slopes_a = jax.nn.softplus(anchor_slopes).reshape(1, 1, N_ANCHOR, 1)
        lw_a = -slopes_a * pos[None, :, None, None]
        log_tw = jnp.concatenate([lw_d, lw_a], axis=2)
        log_p = jnp.clip(score_scale[None, None, :, None] * s_raw, -20.0, 20.0)
        p_w = jnp.exp(log_p + log_tw)
        phi = k_val[..., None] * theta
        re_k = jnp.cos(phi)
        im_k = jnp.sin(phi)
        den = jnp.cumsum(p_w[..., 0], axis=1)
        pwb = p_w[..., None]
        num_re = jnp.cumsum(pwb * re_k, axis=1)
        num_im = jnp.cumsum(pwb * im_k, axis=1)
        inv = lax.rsqrt(jnp.maximum(den, 0.0001))
        inv = (inv * inv)[..., None, None]
        s_re = (num_re * inv).reshape(b, l, K_Q, N_REP, H, M)
        s_im = (num_im * inv).reshape(b, l, K_Q, N_REP, H, M)
        qr = q_re.reshape(b, l, K_Q, 1, H, M)
        qi = q_im.reshape(b, l, K_Q, 1, H, M)
        out_re = jnp.sum(s_re * qr + s_im * qi, axis=-1).reshape(b, l, K, H)
        out_im = jnp.sum(s_im * qr - s_re * qi, axis=-1).reshape(b, l, K, H)
        y_re = out_re * norm_scale[:H] * jnp.diagonal(W_re)
        y_im = out_im * norm_scale[H:] * jnp.diagonal(W_im)
        y = jax.nn.silu((y_re + y_im).reshape(b, l, DIM_K))
        return y @ W_out

    def _L0_ffn_ref(hidden_states, w1, w2, router_w):
        import jax, jax.numpy as jnp
        import numpy as np
        HIDDEN = 128
        INTER = 256
        NUM_EXPERTS = 8
        TOPK = 2
        STD = 0.02
        orig_shape = hidden_states.shape
        dtype = hidden_states.dtype
        x = hidden_states.reshape(-1, orig_shape[-1])
        E = w1.shape[0]
        gating = x @ router_w.T
        probs = jax.nn.softmax(gating.astype(jnp.float32), axis=-1)
        topk_w, sel = jax.lax.top_k(probs, TOPK)
        topk_w = topk_w.astype(dtype)
        combine = (jax.nn.one_hot(sel, E, dtype=dtype) * topk_w[..., None]).sum(axis=1)
        h = jnp.einsum('td,eid->tei', x, w1)
        gate = jax.nn.silu(h[..., :INTER])
        y = h[..., INTER:] * gate
        out = jnp.einsum('tei,ehi,te->th', y, w2, combine)
        return out.reshape(orig_shape)

    def _L1_attn_ref(x, Wqkv, bqkv, Wout, bout):
        import jax, jax.numpy as jnp
        import numpy as np
        D_MODEL = 128
        NHEAD = 16
        BATCH = 2
        SEQ = 256
        B, S, D = x.shape
        H = NHEAD
        dk = D // H
        qkv = x @ Wqkv.T + bqkv
        qkv = qkv.reshape(B, S, H, 3 * dk).transpose(2, 0, 1, 3)
        q, k, v = jnp.split(qkv, 3, axis=-1)
        scale = 1.0 / jnp.sqrt(jnp.asarray(dk, dtype=x.dtype))
        scores = jnp.einsum('hbqd,hbkd->hbqk', q, k) * scale
        attn = jax.nn.softmax(scores, axis=-1)
        o = jnp.einsum('hbqk,hbkd->hbqd', attn, v)
        o = o.transpose(1, 2, 0, 3).reshape(B, S, D)
        return o @ Wout.T + bout

    def _L1_ffn_ref(x, Wr, W1, b1, W2, b2):
        import jax, jax.numpy as jnp
        import numpy as np
        E = 8
        B, S, H = x.shape
        xf = x.reshape(-1, H)
        probs = jax.nn.softmax(xf @ Wr.T, axis=-1)
        eid = E - 1
        h = jax.nn.gelu(xf @ W1[eid] + b1[eid], approximate=False)
        y = (h @ W2[eid] + b2[eid]) * probs[:, eid:eid + 1]
        return y.reshape(B, S, H)

    def _L2_attn_ref(x, W_attn, W_proj):
        import math
        import jax, jax.numpy as jnp
        import numpy as np
        N_HEAD = 16
        X_INT = -100.0
        Y_INT = 1.0
        POWER = 2
        DIVISOR = 1000.0

        def polymax(x):
            m = Y_INT / X_INT
            lin_cond = (x >= X_INT) & (x <= 0)
            x_lin = jnp.where(lin_cond, x, 0.0)
            lin = jnp.where(lin_cond, m * x_lin + Y_INT, 0.0)
            pos_cond = x > 0
            x_pos = jnp.where(pos_cond, x, 0.0)
            poly = jnp.where(pos_cond, x_pos ** POWER + Y_INT, 0.0)
            return (poly + lin) / DIVISOR
        B, T, C = x.shape
        H = N_HEAD
        hd = C // H
        qkv = x @ W_attn
        q, k, v = jnp.split(qkv, 3, axis=-1)
        q = q.reshape(B, T, H, hd).transpose(0, 2, 1, 3)
        k = k.reshape(B, T, H, hd).transpose(0, 2, 1, 3)
        v = v.reshape(B, T, H, hd).transpose(0, 2, 1, 3)
        att = jnp.einsum('bhid,bhjd->bhij', q, k) * (1.0 / math.sqrt(hd))
        causal = jnp.tril(jnp.ones((T, T), dtype=bool))
        att = jnp.where(causal[None, None], att, -jnp.inf)
        att = polymax(att)
        y = jnp.einsum('bhij,bhjd->bhid', att, v)
        y = y.transpose(0, 2, 1, 3).reshape(B, T, C)
        return y @ W_proj

    def _L2_ffn_ref(hidden_states, ln1_weight, ln1_bias, ln2_weight, ln2_bias, qkv_weight, proj_weight, router_weight, moe_w1, moe_w2):
        import jax, jax.numpy as jnp
        import numpy as np
        NH, NKV, E, K = (16, 4, 8, 2)
        CAP_FACTOR = 1.25
        LN_EPS = 1e-05

        def _layer_norm(x, w, b):
            mu = jnp.mean(x, axis=-1, keepdims=True)
            var = jnp.mean(jnp.square(x - mu), axis=-1, keepdims=True)
            return (x - mu) * jax.lax.rsqrt(var + LN_EPS) * w + b
        S, B, H = hidden_states.shape
        HD = H // NH
        q_per_kv = NH // NKV
        ln1 = _layer_norm(hidden_states, ln1_weight, ln1_bias)
        qkv = jnp.einsum('sbh,oh->sbo', ln1, qkv_weight)
        qkv = qkv.reshape(S, B, NKV, (q_per_kv + 2) * HD)
        q = qkv[..., :q_per_kv * HD].reshape(S, B, NH, HD)
        k = qkv[..., q_per_kv * HD:(q_per_kv + 1) * HD]
        v = qkv[..., (q_per_kv + 1) * HD:]
        qb = jnp.transpose(q, (1, 2, 0, 3)).reshape(B, NKV, q_per_kv, S, HD)
        kb = jnp.transpose(k, (1, 2, 0, 3))
        vb = jnp.transpose(v, (1, 2, 0, 3))
        scale = 1.0 / np.sqrt(HD).astype(np.float32)
        scores = jnp.einsum('bgqsd,bgtd->bgqst', qb, kb) * scale
        causal = jnp.tril(jnp.ones((S, S), bool))
        scores = jnp.where(causal, scores, jnp.finfo(scores.dtype).min)
        attn = jax.nn.softmax(scores, axis=-1)
        ao = jnp.einsum('bgqst,bgtd->bgqsd', attn, vb)
        ao = ao.reshape(B, NH, S, HD)
        ao = jnp.transpose(ao, (2, 0, 1, 3)).reshape(S, B, H)
        proj = jnp.einsum('sbh,oh->sbo', ao, proj_weight)
        h1 = hidden_states + proj
        ln2 = _layer_norm(h1, ln2_weight, ln2_bias)
        x = ln2.reshape(-1, H)
        N = x.shape[0]
        logits = x @ router_weight
        probs = jax.nn.softmax(logits, axis=-1)
        top_p, top_i = jax.lax.top_k(probs, K)
        top_p = top_p / jnp.sum(top_p, axis=-1, keepdims=True)
        exp_idx = top_i.reshape(-1)
        exp_p = top_p.reshape(-1)
        order = jnp.argsort(exp_idx, stable=True)
        sorted_exp = exp_idx[order]
        counts = jnp.bincount(exp_idx, length=E)
        offsets = jnp.concatenate([jnp.zeros((1,), counts.dtype), jnp.cumsum(counts)[:-1]])
        within = jnp.arange(N * K) - offsets[sorted_exp]
        cap = int(np.ceil(N * K / E * CAP_FACTOR))
        T = E * cap
        valid = within < cap
        dst = jnp.where(valid, sorted_exp * cap + within, T)
        padded_tokens = jnp.zeros((T, H), x.dtype).at[dst].set(x[order // K], mode='drop')
        padded_probs = jnp.zeros((T,), exp_p.dtype).at[dst].set(exp_p[order], mode='drop')
        padded_tid = jnp.zeros((T,), jnp.int32).at[dst].set((order // K).astype(jnp.int32), mode='drop')
        xt = padded_tokens.reshape(E, cap, H)
        fc1 = jax.nn.gelu(jnp.einsum('ech,ehf->ecf', xt, moe_w1))
        fc2 = jnp.einsum('ecf,efh->ech', fc1, moe_w2).reshape(T, H)
        weighted = fc2 * padded_probs[:, None]
        moe_out = jnp.zeros((N, H), hidden_states.dtype).at[padded_tid].add(weighted)
        return h1 + moe_out.reshape(S, B, H)

    def _L3_attn_ref(x, Wc_down, Wq_up, Wkv_up, Wc_proj):
        import jax, jax.numpy as jnp
        import numpy as np
        N_EMBD = 128
        N_HEAD = 16
        HEAD_DIM = N_EMBD // N_HEAD
        LATENT_DIM = N_EMBD // 2
        B, T = (4, 256)
        Bsz, Tlen, C = x.shape
        latent = x @ Wc_down
        q = (latent @ Wq_up).reshape(Bsz, Tlen, N_HEAD, HEAD_DIM)
        kv = latent @ Wkv_up
        k, v = (kv[..., :HEAD_DIM], kv[..., HEAD_DIM:])
        scale = 1.0 / np.sqrt(HEAD_DIM)
        att = jnp.einsum('bthd,bsd->bhts', q, k) * scale
        causal = jnp.tril(jnp.ones((Tlen, Tlen), dtype=bool))
        att = jnp.where(causal[None, None], att, -jnp.inf)
        att = jax.nn.softmax(att, axis=-1)
        y = jnp.einsum('bhts,bsd->bthd', att, v).reshape(Bsz, Tlen, C)
        return y @ Wc_proj

    def _L3_ffn_ref(hidden_states, w_gate, w1_e, w3_e, w2_e, w1_s, w3_s, w2_s):
        import jax, jax.numpy as jnp
        import numpy as np
        B, S, H = (2, 128, 128)
        E, F = (16, 64)
        G, TOPK_G, TOPK = (4, 2, 4)
        N_SHARED = 2
        ROUTE_SCALE = 1.0
        FS = N_SHARED * F

        def _gate(x, w_gate):
            T = x.shape[0]
            scores = jax.nn.sigmoid(x @ w_gate.T)
            sv = scores.reshape(T, G, E // G)
            group_scores = jax.lax.top_k(sv, 2)[0].sum(-1)
            top_groups = jax.lax.top_k(group_scores, TOPK_G)[1]
            allowed = jnp.zeros((T, G), dtype=bool).at[jnp.arange(T)[:, None], top_groups].set(True)
            masked = jnp.where(allowed[:, :, None], sv, -jnp.inf).reshape(T, E)
            _, idx = jax.lax.top_k(masked, TOPK)
            w = jnp.take_along_axis(scores, idx, axis=1)
            w = w / (w.sum(-1, keepdims=True) + 1e-06) * ROUTE_SCALE
            return (w, idx)

        def _swiglu(x, w1, w3, w2):
            return jax.nn.silu(x @ w1.T) * (x @ w3.T) @ w2.T
        shape = hidden_states.shape
        x = hidden_states.reshape(-1, H)
        weights, idx = _gate(x, w_gate)
        combine = (jax.nn.one_hot(idx, E, dtype=x.dtype) * weights[..., None]).sum(1)
        g = jax.nn.silu(jnp.einsum('th,efh->tef', x, w1_e))
        u = jnp.einsum('th,efh->tef', x, w3_e)
        routed = jnp.einsum('tef,ehf,te->th', g * u, w2_e, combine)
        shared = _swiglu(x, w1_s, w3_s, w2_s)
        return (routed + shared).reshape(shape)
    x = L0_attn_x
    x = x + _layernorm(_L0_attn_ref(_layernorm(x, axis=-1), L0_attn_W_in, L0_attn_conv_k, L0_attn_theta, L0_attn_decay_slopes, L0_attn_anchor_slopes, L0_attn_score_scale, L0_attn_W_re, L0_attn_W_im, L0_attn_norm_scale, L0_attn_W_out), axis=-1)
    x = x + _layernorm(_L0_ffn_ref(_layernorm(x, axis=-1), L0_ffn_w1, L0_ffn_w2, L0_ffn_router_w), axis=-1)
    x = x + _layernorm(_L1_attn_ref(_layernorm(x, axis=-1), L1_attn_Wqkv, L1_attn_bqkv, L1_attn_Wout, L1_attn_bout), axis=-1)
    x = x + _layernorm(_L1_ffn_ref(_layernorm(x, axis=-1), L1_ffn_Wr, L1_ffn_W1, L1_ffn_b1, L1_ffn_W2, L1_ffn_b2), axis=-1)
    x = x + _layernorm(_L2_attn_ref(_layernorm(x, axis=-1), L2_attn_W_attn, L2_attn_W_proj), axis=-1)
    x = x + _layernorm(_L2_ffn_ref(_layernorm(x, axis=-1), L2_ffn_ln1_weight, L2_ffn_ln1_bias, L2_ffn_ln2_weight, L2_ffn_ln2_bias, L2_ffn_qkv_weight, L2_ffn_proj_weight, L2_ffn_router_weight, L2_ffn_moe_w1, L2_ffn_moe_w2), axis=-1)
    x = x + _layernorm(_L3_attn_ref(_layernorm(x, axis=-1), L3_attn_Wc_down, L3_attn_Wq_up, L3_attn_Wkv_up, L3_attn_Wc_proj), axis=-1)
    x = x + _layernorm(_L3_ffn_ref(_layernorm(x, axis=-1), L3_ffn_w_gate, L3_ffn_w1_e, L3_ffn_w3_e, L3_ffn_w2_e, L3_ffn_w1_s, L3_ffn_w3_s, L3_ffn_w2_s), axis=-1)
    return x

_drawn_inputs = setup_inputs


def setup_inputs(seed=0):
    import zlib

    import numpy as np

    out = dict(_drawn_inputs(seed))
    spreads = {'L0_attn_score_scale': (1.0, 0.6),
     'L0_attn_norm_scale': (1.0, 0.2),
     'L1_ffn_b1': (0.0, 0.1),
     'L1_ffn_b2': (0.0, 0.1),
     'L2_ffn_ln1_weight': (1.0, 0.6),
     'L2_ffn_ln1_bias': (0.0, 0.8),
     'L2_ffn_ln2_weight': (1.0, 0.6),
     'L2_ffn_ln2_bias': (0.0, 0.8)}
    factors = {'L0_attn_anchor_slopes': 16.446,
     'L1_ffn_Wr': 8.0,
     'L2_ffn_qkv_weight': 3.109,
     'L2_ffn_proj_weight': 2.826,
     'L2_ffn_router_weight': 7.944,
     'L2_ffn_moe_w1': 7.184,
     'L2_ffn_moe_w2': 6.459,
     'L3_attn_Wq_up': 6.934}
    for name, (base, spread) in spreads.items():
        noise = np.random.default_rng([zlib.crc32(name.encode()), seed]).standard_normal(out[name].shape)
        drawn = base * np.exp(spread * noise) if base else spread * noise
        out[name] = jnp.asarray(drawn.astype(out[name].dtype))
    for name, factor in factors.items():
        out[name] = (out[name] * factor).astype(out[name].dtype)
    return out
```

```python
from contextlib import ExitStack

import numpy as np

import concourse.bass as bass
from concourse import mybir

ALU = mybir.AluOpType
ACT = mybir.ActivationFunctionType
AX = mybir.AxisListType
F32 = mybir.dt.float32
BF16 = mybir.dt.bfloat16

P = 128
NB, L = 8, 256
T = L // P
D = 128
EPS = 1e-5

(L0_ATTN, L0_FFN, L1_ATTN, L1_FFN, L2_ATTN, L2_MIX, L2_MOE, L3_ATTN, L3_FFN) = range(9)
RUN = tuple(range(9))

KCH, HC, NM = 32, 4, 8
KQ = 4
TAPS = 4
CHUNK_M = 2
CHUNKS = NM // CHUNK_M
MAGIC = float(1.5 * 2 ** 23)
TWO_PI_LOW = 6.283185

NH, HD = 16, 8
SM_SCALE = 1.0 / float(np.sqrt(np.float32(HD)))
PARTS = 7 * HD
AUG = 3
SLOT = 64
VW = HD + 1
NEG = -1e30

E8, F8 = 8, 256
FD1 = 512
E16, F16 = 16, 64
NSH = 128
CAP = 640
NG = 4


class Pack:

    def __init__(self, fields):
        self.at, n = {}, 0
        for name, width in fields:
            self.at[name] = (n, width)
            n += width
        self.width = n


PACKS = {
    "const": Pack([("ident", P), ("rank8", 64), ("rank16", 256), ("rank4", 16), ("causal8", 64), ("decay_pos", L)]),
    "l0a": Pack([("wk", D), ("ws", D), ("wq_re", P), ("wq_im", P), ("wout", D), ("conv_k", TAPS * D),
                 ("conv_s", TAPS * D), ("norm_re", P), ("norm_im", P), ("diag_re", P), ("diag_im", P),
                 ("theta", NM), ("slope", 1), ("score", 1)]),
    "l0f": Pack([("router", E8), ("w1", E8 * 2 * F8), ("w2", E8 * 2 * D)]),
    "l1a": Pack([("wqkv", 3 * D), ("bqkv", 3 * D), ("wout", D), ("bout", D)]),
    "l1f": Pack([("router", E8), ("w1", FD1), ("b1", 4), ("w2", 4 * D), ("b2", D)]),
    "l2a": Pack([("wqkv", 3 * D), ("wout", D)]),
    "l2f": Pack([("ln1w", 1), ("ln1b", 1), ("ln2w", 1), ("ln2b", 1), ("qkv", 192), ("proj", D),
                 ("router", E8), ("w1", E8 * F8), ("w2", E8 * 2 * D)]),
    "l3a": Pack([("down", 64), ("up", D + 2 * HD), ("wout", D)]),
    "l3f": Pack([("router", E16), ("w1", E16 * F16), ("w3", E16 * F16), ("w2", 8 * D), ("w1s", NSH),
                 ("w3s", NSH), ("w2s", D)]),
}
PACKS_BF = {"cbf": Pack([("ident", P), ("mask_q", 2 * L), ("mask_k", 384), ("before", P), ("ones", P)])}


def block_program(nc, x, packs, packs_bf, out):
    ctx = ExitStack()
    with ctx:
        def sb(name, shape, dt=F32):
            return ctx.enter_context(nc.sbuf_tensor(name, shape, dt))

        def sem(name):
            return ctx.enter_context(nc.semaphore(name))

        W = {n: sb("w_" + n, [P, pk.width]) for n, pk in PACKS.items()}
        W["cbf"] = sb("w_cbf", [P, PACKS_BF["cbf"].width], BF16)

        def w(pack, name):
            a, n = (PACKS.get(pack) or PACKS_BF[pack]).at[name]
            return W[pack][:, a:a + n]

        X = sb("X", [P, NB * T, D])
        H1 = sb("H1", [P, NB * T, D])
        h = sb("h", [P, T, D])
        hT = sb("hT", [P, L])
        hst, hmv, hve, hrs = (sb("hst", [P, T, 6]), sb("hmv", [P, T, 2]), sb("hve", [P, T]), sb("hrs", [P, T]))
        tst, tmv, tve, trs = (sb("tst", [P, T, 6]), sb("tmv", [P, T, 2]), sb("tve", [P, T]), sb("trs", [P, T]))
        tn = sb("tn", [P, T, D])
        mhalf = sb("mhalf", [P, T])
        eps = sb("eps", [P, T])
        warm_t = sb("warm_t", [P, 1])
        half_pi = sb("half_pi", [P, 1])
        one_c = sb("one_c", [P, 1])
        wkc, wsc = sb("wkc", [P, TAPS, D]), sb("wsc", [P, TAPS, D])
        wab = sb("wab", [P, 2, P])
        wtmp = sb("wtmp", [P, 2, P])
        coef = sb("coef", [P, 2, P])
        wA, wB = sb("wA", [P, NM, D]), sb("wB", [P, NM, D])
        slope = sb("slope", [P, 4])
        logw = sb("logw", [P, L])
        theta = sb("theta", [P, NM])
        carry = sb("carry", [P, CHUNK_M, L])
        la, pw, den = sb("la", [P, L]), sb("pw", [P, L]), sb("den", [P, L])
        inv, arg, yT = sb("inv", [P, L]), sb("arg", [P, L]), sb("yT", [P, L])
        cb = sb("cb", [P, CHUNKS, CHUNK_M, L])
        sbuf = sb("sbuf", [P, CHUNKS, CHUNK_M, L])
        qkv = sb("qkv", [P, T, 3 * D])
        rest = sb("rest", [P, T * NH, HD])
        QS, KS = sb("QS", [P, T * NH, SLOT], BF16), sb("KS", [P, T * NH, SLOT], BF16)
        QT, KT = sb("QT", [P, NH // 2, L], BF16), sb("KT", [P, NH // 2, L], BF16)
        VA = sb("VA", [P, T, NH, VW])
        mx = sb("mx", [P, NH, T])
        mr = sb("mr", [P, T, NH])
        PT = sb("PT", [P, 4, 2 * L])
        PG = cb[:].rearrange("p c m t -> p c (m t)")
        PN = sbuf[:].rearrange("p c m t -> p c (m t)")
        PG2 = sb("PG2", [P, 2, 384])
        rsum = sb("rsum", [P, T, NH])
        osb = sb("osb", [P, T, D])
        oT = sb("oT", [P, L])
        latT = sb("latT", [64, L])
        cbf_f = PT[:].rearrange("p a b -> p (a b)")
        cwx = PT[:].rearrange("p a b -> p (a b)").rearrange("p (t e f) -> p t e f", t=T, e=E16)
        sg, y = sb("sg", [P, 2, 2 * L]), sb("y", [P, 2, 2 * L])
        acc = sb("acc", [P, T, D])
        lg, ex = sb("lg", [P, T, E16]), sb("ex", [P, T, E16])
        gmx, gsm = sb("gmx", [P, T]), sb("gsm", [P, T])
        gtb, eqb = sb("gtb", [P, T, E16 * E16]), sb("eqb", [P, T, E16 * E16])
        rank = sb("rank", [P, T, E16])
        cw = sb("cw", [P, T, E16])
        hilo = sb("hilo", [P, 4, T * NG, 2])
        gsc, gal = sb("gsc", [P, T, NG]), sb("gal", [P, T, NG])
        msk = sb("msk", [P, T, E16])
        mbf, cum = sb("mbf", [P, T, E8], BF16), sb("cum", [P, E8], BF16)
        cum1 = sb("cum1", [P, E8], BF16)
        n1, n1T = sb("n1", [P, T, D]), sb("n1T", [P, L])
        q2 = sb("q2", [P, T, NG, 4, HD])
        KC, VC = sb("KC", [P, T, NG, NB, HD]), sb("VC", [P, T, NG, HD, NB])
        prod = PT[:].rearrange("p a b -> p (a b)").rearrange("p (a b) -> p a b", a=T * NG)
        sc2 = sb("sc2", [P, T * NH, NB])
        ex2 = sb("ex2", [P, T * NH, NB])
        mx2, sm2 = sb("mx2", [P, T * NH]), sb("sm2", [P, T * NH])
        ao, aoT = sb("ao", [P, T * NH, HD]), sb("aoT", [P, L])

        PS = ctx.enter_context(nc.psum_tensor("PS", [P, 8, 512], F32))
        PSB = PS[:].bitcast(BF16)
        Y = PS[:, 6, 0:L].rearrange("p (t d) -> p t d", t=T)
        TR = PS[:, 7, 0:L]
        GATES = {l: PS[:, b, 0:T * E16].rearrange("p (t e) -> p t e", t=T)
                 for l, b in ((L0_FFN, 6), (L1_FFN, 4), (L2_MOE, 6), (L3_FFN, 5))}

        x_in, w_in, wb_in, st_out = sem("x_in"), {n: sem("in_" + n) for n in PACKS}, sem("in_cbf"), sem("st_out")
        consts, cbf_ready = sem("consts"), sem("cbf_ready")
        hd_stat, hd_rstd, hd_h, hd_tr, hd_hT = (sem("hd_" + n) for n in ("stat", "rstd", "h", "tr", "hT"))
        tl_stat, tl_rstd = sem("tl_stat"), sem("tl_rstd")
        y_ready, x_done = sem("y_ready"), sem("x_done")
        h1_done = sem("h1_done")
        a_w, a_soft, a_z, a_lg, a_p, a_u, a_red, a_trig, a_pp, a_ab, a_pr, a_sum, a_arg, a_yT = (
            sem("a_" + n) for n in "w soft z lg p u red trig pp ab pr sum arg yT".split())
        t_qkv, t_split, t_tr, t_ev, t_s, t_mx, t_m, t_st, t_pt, t_pv, t_o, t_oT, t_oTs, t_lat, t_lats, t_pn, t_pg, t_m2 = (
            sem("t_" + n) for n in "qkv split tr ev s mx m st pt pv o oT oTs lat lats pn pg m2".split())
        FF = {l: {n: sem(f"f{l}_{n}") for n in "gate ge gx g sg y o oc c cT rk".split()}
              for l in (L0_FFN, L1_FFN, L2_MOE, L3_FFN)}
        m_st, m_rs, m_n1, m_tr, m_n1T, m_qkv, m_sc, m_ex, m_ao, m_aT, m_aTs, m_y = (
            sem("m_" + n) for n in "st rs n1 tr n1T qkv sc ex ao aT aTs y".split())

        run = RUN
        order = {l: n for n, l in enumerate(run)}
        head0, k = {}, 0
        for n, l in enumerate(run):
            if n == 0 or l in (L2_MOE,) or run[n - 1] == L2_MOE:
                k += 1
            head0[l] = k - 1
            k += NB
        tail0, k = {}, 0
        for l in run:
            tail0[l] = k
            k += NB if l != L2_MIX else 0
        tails = k
        res0 = {l: NB * n for n, l in enumerate([a for a in run if a in (L0_ATTN, L1_ATTN, L2_ATTN, L3_ATTN)])}
        att0 = {l: NB * n for n, l in enumerate([a for a in run if a in (L1_ATTN, L2_ATTN, L3_ATTN)])}

        att_pt, k = {}, 0
        for l in run:
            att_pt[l] = k
            k += NB * NH if l in att0 else 0
        att_tr, att_s, k, ks = {}, {}, 0, 0
        for l in run:
            att_tr[l], att_s[l] = k, ks
            if l in att0:
                k += NB * (4 if l == L2_ATTN else (5 if l == L3_ATTN else 6))
                ks += 0 if l == L2_ATTN else NB * (NH // 2)
        att_m = {L1_ATTN: 0, L3_ATTN: NB if L1_ATTN in run else 0}

        def own_head(l):
            n = order[l]
            return n == 0 or l == L2_MOE or run[n - 1] == L2_MOE

        block = ctx.enter_context(nc.Block())

        @block.sync
        def _(sp):
            xt = x.rearrange("b (t p) d -> p (b t) d", p=P)
            sp.dma_start(X[:], xt).then_inc(x_in, 16)
            for n in PACKS:
                sp.dma_start(W[n][:], packs[n]).then_inc(w_in[n], 16)
                if n == "const":
                    sp.dma_start(cbf_f[:, 0:PACKS_BF["cbf"].width], packs_bf["cbf"]).then_inc(wb_in, 16)
            sp.wait_ge(x_done, 1 + tails)
            sp.dma_start(out.rearrange("b (t p) d -> p (b t) d", p=P), X[:]).then_inc(st_out, 16)
            sp.wait_ge(st_out, 16)

        @block.gpsimd
        def _(pool):
            def rstd(stat, ready, count, mv, ve, rs):
                pool.wait_ge(stat, count)
                pool.tensor_tensor(ve[:], mv[:, :, 1], eps[:], ALU.add)
                pool.drain()
                pool.tensor_tensor(rs[:], ve[:], mhalf[:], ALU.pow).then_inc(ready, 1)

            def head_rstd(count):
                rstd(hd_stat, hd_rstd, count, hmv, hve, hrs)

            def tail_rstd(count):
                rstd(tl_stat, tl_rstd, count, tmv, tve, trs)

            pool.memset(mhalf[:], -0.5)
            pool.memset(eps[:], EPS)
            pool.memset(half_pi[:], float(np.pi / 2))
            pool.memset(one_c[:], 1.0)
            pool.memset(carry[:], 1.0)
            pool.memset(QS[:], 0.0)
            pool.memset(KS[:], 0.0)
            pool.memset(VA[:], 1.0)
            pool.memset(KC[:], 0.0)
            pool.memset(VC[:], 0.0)
            pool.memset(cum[:], 0.0)
            pool.drain()
            pool.memset(carry[:, :, 0:1], 0.0)
            pool.memset(KS[:, :, PARTS:PARTS + AUG], 1.0)
            pool.drain().then_inc(consts, 1)

            for l in run:
                if own_head(l):
                    head_rstd(head0[l] + 1)
                with pool.Fori(0, NB) as i:
                    head_rstd(i + (head0[l] + 2))
                    if l == L0_ATTN:
                        for c in range(CHUNKS):
                            pool.wait_ge(a_trig, i * CHUNKS + (c + 1))
                            if c == 0:
                                pool.wait_ge(a_p, i + 1)
                            for b in (cb, sbuf):
                                ins = pool.tensor_tensor(b[:, c], b[:, c],
                                                         pw[:].unsqueeze(1).to_broadcast([P, CHUNK_M, L]), ALU.mult)
                            ins.then_inc(a_pp, 1)
                    if l == L2_MIX:
                        pool.wait_ge(m_st, i + 1)
                        pool.tensor_tensor(tve[:], tmv[:, :, 1], eps[:], ALU.add)
                        pool.drain()
                        pool.tensor_tensor(trs[:], tve[:], mhalf[:], ALU.pow).then_inc(m_rs, 1)
                    if l == L2_ATTN:
                        for hh in range(NH):
                            pool.wait_ge(t_pt, i * NH + (att_pt[l] + hh + 1))
                            pool.tensor_tensor(PG[:, hh % 4, 0:384], PT[:, hh % 4, 0:384],
                                               PT[:, hh % 4, 0:384], ALU.mult).then_inc(t_pg, 1)
                    if l != L2_MIX:
                        tail_rstd(i + (tail0[l] + 1))

        @block.scalar
        def _(act):
            def warm(func):
                act.activation(warm_t[:], one_c[:], func)

            def head_copy(l, count):
                act.wait_ge(hd_tr, count)
                if l == L2_MOE:
                    act.activation(hT[:], TR, ACT.Identity, scale=w("l2f", "ln2w"),
                                   bias=w("l2f", "ln2b")).then_inc(hd_hT, 1)
                else:
                    act.activation(hT[:], TR, ACT.Copy).then_inc(hd_hT, 1)

            act.wait_ge(consts, 1)
            for l in run:
                if own_head(l):
                    if l == L2_MOE:
                        act.wait_ge(w_in["l2f"], 16)
                    head_copy(l, head0[l] + 1)
                if l == L0_ATTN:
                    act.wait_ge(w_in["l0a"], 16)
                    act.activation(slope[:, 0:1], w("l0a", "slope"), ACT.Abs)
                    act.drain()
                    act.activation(slope[:, 1:2], slope[:, 0:1], ACT.Exp, scale=-1.0)
                    act.drain()
                    act.activation(slope[:, 2:3], slope[:, 1:2], ACT.Ln, bias=one_c[:], scale=1.0)
                    act.activation(slope[:, 3:4], w("l0a", "slope"), ACT.Relu)
                    act.drain().then_inc(a_soft, 1)
                    act.wait_ge(a_w, 1)
                    act.sem_inc(a_sum, CHUNKS)
                    warm(ACT.Silu)
                    with act.Fori(0, NB) as i:
                        act.wait_ge(a_z, i + 1)

                        def turns(c):
                            act.wait_ge(a_sum, i * CHUNKS + (c + 1))
                            for m in range(CHUNK_M):
                                j = c * CHUNK_M + m
                                ins = act.activation(cb[:, c, m], PS[:, 0, 0:L], ACT.Identity,
                                                     scale=theta[:, j:j + 1])
                            ins.then_inc(a_u, 1)

                        def trig(c):
                            act.wait_ge(a_red, i * CHUNKS + (c + 1))
                            act.activation(cb[:, c], sbuf[:, c], ACT.Abs)
                            act.drain()
                            act.activation(cb[:, c], cb[:, c], ACT.Sin, scale=-TWO_PI_LOW, bias=half_pi[:])
                            act.activation(sbuf[:, c], sbuf[:, c], ACT.Sin, scale=-TWO_PI_LOW).then_inc(a_trig, 1)

                        turns(0)
                        turns(1)
                        act.wait_ge(a_lg, i + 1)
                        act.activation(pw[:], la[:], ACT.Exp).then_inc(a_p, 1)
                        trig(0)
                        turns(2)
                        trig(1)
                        turns(3)
                        trig(2)
                        trig(3)
                        act.wait_ge(a_arg, i + 2)
                        act.activation(yT[:], arg[:], ACT.Silu).then_inc(a_yT, 1)
                        head_copy(l, i + (head0[l] + 2))
                elif l in (L1_ATTN, L2_ATTN, L3_ATTN):
                    causal = l != L1_ATTN
                    width = 384 if causal else 2 * L
                    ntr = {L1_ATTN: 6, L2_ATTN: 4, L3_ATTN: 5}[l]
                    warm(ACT.Exp)
                    with act.Fori(0, NB) as i:
                        if l == L3_ATTN:
                            act.wait_ge(t_lat, i + 1)
                            act.activation(latT[:], PS[0:64, 4, 0:L], ACT.Copy).then_inc(t_lats, 1)
                            act.wait_ge(t_tr, i * ntr + (att_tr[l] + 1))
                            act.activation(KT[:, 0, :], PSB[:, 4, 0:L], ACT.Copy).then_inc(t_ev, 1)
                            todo = [(1, QT, 0), (2, QT, 1)]
                        else:
                            todo = [(0, KT, 0), (1, KT, 1), (2, QT, 0), (3, QT, 1)]
                        again = [] if l == L2_ATTN else [(ntr - 2, QT, 0), (ntr - 1, QT, 1)]
                        for part in (todo, again):
                            for n, dst, t in part:
                                act.wait_ge(t_tr, i * ntr + (att_tr[l] + n + 1))
                                act.activation(dst[:, :, t * P:(t + 1) * P],
                                               PSB[:, 4 + n % 2, :].rearrange("p (a b) -> p a b", b=P),
                                               ACT.Copy).then_inc(t_ev, 1)
                        for hh in range(NH):
                            act.wait_ge(t_st, i * NH + (att_pt[l] + hh + 1))
                            src = PS[:, hh % 4, 0:width]
                            act.wait_ge(t_pv, i * NH + (att_pt[l] + hh + 1))
                            if l == L2_ATTN:
                                act.activation(PN[:, hh % 4, 0:width], src, ACT.Relu,
                                               scale=-0.01 * SM_SCALE).then_inc(t_pn, 1)
                                act.activation(PT[:, hh % 4, 0:width], src, ACT.Relu,
                                               scale=SM_SCALE).then_inc(t_pt, 1)
                            else:
                                act.activation(PT[:, hh % 4, 0:width], src, ACT.Exp,
                                               scale=SM_SCALE).then_inc(t_pt, 1)
                        act.wait_ge(t_oT, i + (att0[l] + 1))
                        act.activation(oT[:], PS[:, 4, 0:L], ACT.Copy).then_inc(t_oTs, 1)
                        head_copy(l, i + (head0[l] + 2))
                elif l == L2_MIX:
                    act.wait_ge(w_in["l2f"], 16)
                    warm(ACT.Exp)
                    with act.Fori(0, NB) as i:
                        act.wait_ge(m_tr, i + 1)
                        act.activation(n1T[:], PS[:, 0, 0:L], ACT.Identity, scale=w("l2f", "ln1w"),
                                       bias=w("l2f", "ln1b")).then_inc(m_n1T, 1)
                        act.wait_ge(m_sc, i + 1)
                        act.activation(ex2[:], sc2[:], ACT.Exp).then_inc(m_ex, 1)
                        act.wait_ge(m_aT, i + 1)
                        act.activation(aoT[:], PS[:, 2, 0:L], ACT.Copy).then_inc(m_aTs, 1)
                        head_copy(l, i + (head0[l] + 2))
                else:
                    f, GATE = FF[l], GATES[l]
                    func = {L0_FFN: ACT.Silu, L3_FFN: ACT.Silu, L1_FFN: ACT.Gelu, L2_MOE: ACT.Gelu_apprx_tanh}[l]
                    n_chunks = {L0_FFN: 8, L1_FFN: 2, L2_MOE: 8, L3_FFN: 5}[l]
                    ne = E16 if l == L3_FFN else E8
                    if l in (L1_FFN, L3_FFN):
                        act.wait_ge(w_in["l1f" if l == L1_FFN else "l3f"], 16)
                    warm(func)
                    with act.Fori(0, NB) as i:
                        act.wait_ge(f["ge"], i + 1)
                        act.activation(ex[:, :, 0:ne], lg[:, :, 0:ne], ACT.Exp, scale=-1.0 if l == L3_FFN else 1.0).then_inc(f["gx"], 1)
                        for c in range(n_chunks):
                            cols = 2 * L if not (l == L3_FFN and c == 4) else L
                            gate = PS[:, 2 * (c % 2), 0:cols]
                            act.wait_ge(f["g"], i * n_chunks + (c + 1))
                            if l in (L0_FFN, L3_FFN):
                                act.activation(sg[:, c % 2, 0:cols], gate, func).then_inc(f["sg"], 1)
                            else:
                                act.wait_ge(f["o"], i * n_chunks + (c + 1))
                                if l == L1_FFN:
                                    for b in range(2):
                                        j = 2 * c + b
                                        ins = act.activation(y[:, c % 2, b * L:(b + 1) * L],
                                                             PS[:, 2 * (c % 2), b * L:(b + 1) * L], func,
                                                             bias=w("l1f", "b1")[:, j:j + 1])
                                else:
                                    ins = act.activation(y[:, c % 2, :], gate, func)
                                ins.then_inc(f["y"], 1)
                        head_copy(l, i + (head0[l] + 2))

        @block.tensor
        def _(pe):
            ident = w("const", "ident")
            identb = w("cbf", "ident")

            def head_transpose(l, i):
                pe.wait_ge(hd_h, i + (head0[l] + 2))
                for t in range(T):
                    ins = pe.transpose(TR[:, t * P:(t + 1) * P], h[:, t, :], ident)
                ins.then_inc(hd_tr, 1)

            pe.wait_ge(w_in["const"], 16)
            pe.wait_ge(cbf_ready, 1)
            pe.sem_inc(x_done, 1)
            for l in run:
                if own_head(l):
                    pe.wait_ge(hd_h, head0[l] + 1)
                    if head0[l]:
                        pe.wait_ge(hd_hT, head0[l])
                    for t in range(T):
                        ins = pe.transpose(TR[:, t * P:(t + 1) * P], h[:, t, :], ident)
                    ins.then_inc(hd_tr, 1)
                if order[l]:
                    pe.wait_ge(x_done, 1 + tail0[l])
                if l == L2_MOE:
                    pe.wait_ge(h1_done, NB)

                def unit_ready(i):
                    pe.wait_ge(hd_hT, i + (head0[l] + 1))

                def y_free(i):
                    pe.wait_ge(x_done, i + (tail0[l] + 1))

                if l == L0_ATTN:
                    pe.wait_ge(w_in["l0a"], 16)
                    pe.wait_ge(a_w, 1)
                    pe.sem_inc(a_pr, 2)
                    pe.sem_inc(a_arg, 1)
                    with pe.Fori(0, NB) as i:
                        unit_ready(i)
                        pe.wait_ge(a_arg, i + 1)
                        for g, wt in ((0, wkc), (1, wsc)):
                            for j in range(TAPS - 1, -1, -1):
                                back = TAPS - 1 - j
                                ins = pe.matmul(PS[:, 5 * g, g * L + back:(g + 1) * L], wt[:, j, :], hT[:, 0:L - back],
                                                start=back == 0, stop=back == TAPS - 1)
                        ins.then_inc(a_z, 1)

                        def factors(c):
                            pe.wait_ge(a_pr, i * CHUNKS + (c + 1))
                            for g, wt in ((0, wA), (1, wB)):
                                for m in range(CHUNK_M):
                                    ins = pe.matmul(PS[:, 1 + 2 * (c % 2) + g, m * L:(m + 1) * L],
                                                    wt[:, c * CHUNK_M + m, :], hT[:], start=True, stop=True)
                            ins.then_inc(a_ab, 1)

                        def sums(c):
                            pe.wait_ge(a_pr, i * CHUNKS + (c + 3))
                            for b in (cb, sbuf):
                                for m in range(CHUNK_M):
                                    first = c == 0 and m == 0 and b is cb
                                    last = c == CHUNKS - 1 and m == CHUNK_M - 1 and b is sbuf
                                    ins = pe.matmul(PS[:, 5, 0:L], ident, b[:, c, m], start=first, stop=last)
                            ins.then_inc(a_sum, 1)

                        factors(0)
                        factors(1)
                        sums(0)
                        factors(2)
                        sums(1)
                        factors(3)
                        sums(2)
                        head_transpose(l, i)
                        sums(3)
                        pe.wait_ge(a_yT, i + 1)
                        y_free(i)
                        for t in range(T):
                            ins = pe.matmul(Y[:, t, :], yT[:, t * P:(t + 1) * P], w("l0a", "wout"), start=True, stop=True)
                        ins.then_inc(y_ready, 1)
                elif l in (L1_ATTN, L2_ATTN, L3_ATTN):
                    name = {L1_ATTN: "l1a", L2_ATTN: "l2a", L3_ATTN: "l3a"}[l]
                    causal = l != L1_ATTN
                    ntr = {L1_ATTN: 6, L2_ATTN: 4, L3_ATTN: 5}[l]
                    pe.wait_ge(w_in[name], 16)
                    if att0[l] == 0:
                        pe.sem_inc(t_pv, 4)
                    with pe.Fori(0, NB) as i:
                        unit_ready(i)
                        if l == L3_ATTN:
                            pe.matmul(PS[0:64, 4, 0:L], w(name, "down"), hT[:], start=True, stop=True).then_inc(t_lat, 1)
                            pe.wait_ge(t_lats, i + 1)
                            for t in range(T):
                                ins = pe.matmul(PS[:, 4 + t, 0:D + 2 * HD], latT[:, t * P:(t + 1) * P],
                                                w(name, "up")[0:64], start=True, stop=True)
                        else:
                            for t in range(T):
                                ins = pe.matmul(PS[:, 4 + t, 0:3 * D], hT[:, t * P:(t + 1) * P], w(name, "wqkv"),
                                                start=True, stop=True)
                        ins.then_inc(t_qkv, 1)
                        head_transpose(l, i)

                        def parts_transpose(n, src, t):
                            if n >= 2:
                                pe.wait_ge(t_ev, i * ntr + (att_tr[l] + n - 1))
                            for a in range(NH // 2):
                                ins = pe.transpose(
                                    PSB[:, 4 + n % 2, a * P:(a + 1) * P],
                                    src[:, t * NH + 2 * a:t * NH + 2 * a + 2, :].rearrange("p a b -> p (a b)"), identb)
                            ins.then_inc(t_tr, 1)

                        pe.wait_ge(t_split, i + (att0[l] + 1))
                        if l == L3_ATTN:
                            for t in range(T):
                                ins = pe.transpose(PSB[:, 4, t * P:(t + 1) * P],
                                                   KS[:, t * NH:t * NH + 2, :].rearrange("p a b -> p (a b)"), identb)
                            ins.then_inc(t_tr, 1)
                            parts_transpose(1, QS, 0)
                            parts_transpose(2, QS, 1)
                        else:
                            for n, (src, t) in enumerate(((KS, 0), (KS, 1), (QS, 0), (QS, 1))):
                                parts_transpose(n, src, t)
                        first = ntr if l == L2_ATTN else ntr - 2
                        pe.wait_ge(t_ev, i * ntr + (att_tr[l] + first))

                        if l != L2_ATTN:
                            for pair in range(NH // 2):
                                if pair >= 2:
                                    pe.wait_ge(t_mx, i * (NH // 2) + (att_s[l] + pair - 1))
                                for hh in (2 * pair, 2 * pair + 1):
                                    b = 2 * (pair % 2) + hh % 2
                                    r = 64 * (hh % 2)
                                    if causal:
                                        pe.matmul(PS[:, b, :], identb, w("cbf", "mask_q"), start=True, stop=False,
                                                  skip_group_check=True)
                                    for t in range(T):
                                        ins = pe.matmul(PS[:, b, t * L:(t + 1) * L],
                                                        QT[r:r + PARTS, hh // 2, t * P:(t + 1) * P],
                                                        KT[r:r + PARTS, 0 if l == L3_ATTN else hh // 2, :],
                                                        start=not causal, stop=True, skip_group_check=causal)
                                ins.then_inc(t_s, 1)
                            pe.wait_ge(t_m, i + (att_m[l] + 1))
                            parts_transpose(ntr - 2, QS, 0)
                            parts_transpose(ntr - 1, QS, 1)
                            pe.wait_ge(t_ev, i * ntr + (att_tr[l] + ntr))
                            rows = PARTS + AUG
                        else:
                            rows = PARTS

                        def scores(hh):
                            r, kh = 64 * (hh % 2), 0 if l == L3_ATTN else hh // 2
                            if hh >= 4:
                                pe.wait_ge(t_pt, i * NH + (att_pt[l] + hh - 3))
                            if causal:
                                pe.matmul(PS[:, hh % 4, 0:384], identb, w("cbf", "mask_k"), start=True, stop=False,
                                          skip_group_check=True)
                                pe.matmul(PS[:, hh % 4, 0:L], KT[r:r + rows, kh, 0:P], QT[r:r + rows, hh // 2, :],
                                          start=False, stop=True, skip_group_check=True)
                                ins = pe.matmul(PS[:, hh % 4, L:384], KT[r:r + rows, kh, P:L],
                                                QT[r:r + rows, hh // 2, P:L], start=False, stop=True,
                                                skip_group_check=True)
                            else:
                                for t in range(T):
                                    ins = pe.matmul(PS[:, hh % 4, t * L:(t + 1) * L],
                                                    KT[r:r + rows, kh, t * P:(t + 1) * P],
                                                    QT[r:r + rows, hh // 2, :], start=True, stop=True)
                            ins.then_inc(t_st, 1)

                        def values(hh):
                            vh = 0 if l == L3_ATTN else hh
                            if l == L2_ATTN:
                                pe.wait_ge(t_pg, i * NH + (hh + 1))
                                pe.wait_ge(t_m2, i * NH + (hh + 1))
                                srcs = (PG, PN)
                            else:
                                pe.wait_ge(t_pt, i * NH + (att_pt[l] + hh + 1))
                                srcs = (PT,)
                            if causal:
                                blocks = (((0, 0),), ((0, P), (1, L)))
                            else:
                                blocks = (((0, 0), (1, L)), ((0, P), (1, L + P)))
                            for t in range(T):
                                terms = [(s, kk, at) for s in srcs for kk, at in blocks[t]]
                                for n, (s, kk, at) in enumerate(terms):
                                    ins = pe.matmul(PS[:, 5, (t * NH + hh) * VW:(t * NH + hh + 1) * VW],
                                                    s[:, hh % 4, at:at + P], VA[:, kk, vh, :],
                                                    start=n == 0, stop=n == len(terms) - 1)
                            ins.then_inc(t_pv, 1)

                        lead = 3
                        for hh in range(NH + lead):
                            if hh < NH:
                                scores(hh)
                            if hh >= lead:
                                values(hh - lead)
                        pe.wait_ge(t_o, i + (att0[l] + 1))
                        for t in range(T):
                            ins = pe.transpose(PS[:, 4, t * P:(t + 1) * P], osb[:, t, :], ident)
                        ins.then_inc(t_oT, 1)
                        pe.wait_ge(t_oTs, i + (att0[l] + 1))
                        y_free(i)
                        for t in range(T):
                            ins = pe.matmul(Y[:, t, :], oT[:, t * P:(t + 1) * P], w(name, "wout"), start=True, stop=True)
                        ins.then_inc(y_ready, 1)
                elif l == L2_MIX:
                    pe.wait_ge(w_in["l2f"], 16)
                    with pe.Fori(0, NB) as i:
                        unit_ready(i)
                        pe.wait_ge(m_n1, i + 1)
                        for t in range(T):
                            ins = pe.transpose(PS[:, 0, t * P:(t + 1) * P], n1[:, t, :], ident)
                        ins.then_inc(m_tr, 1)
                        head_transpose(l, i)
                        pe.wait_ge(m_n1T, i + 1)
                        for t in range(T):
                            ins = pe.matmul(PS[:, 1, t * 192:(t + 1) * 192], n1T[:, t * P:(t + 1) * P],
                                            w("l2f", "qkv"), start=True, stop=True)
                        ins.then_inc(m_qkv, 1)
                        pe.wait_ge(m_ao, i + 1)
                        for t in range(T):
                            ins = pe.transpose(PS[:, 2, t * P:(t + 1) * P],
                                               ao[:, t * NH:(t + 1) * NH, :].rearrange("p a b -> p (a b)"), ident)
                        ins.then_inc(m_aT, 1)
                        pe.wait_ge(m_aTs, i + 1)
                        for t in range(T):
                            ins = pe.matmul(PS[:, 3, t * P:(t + 1) * P], aoT[:, t * P:(t + 1) * P],
                                            w("l2f", "proj"), start=True, stop=True)
                        ins.then_inc(m_y, 1)
                else:
                    f, GATE = FF[l], GATES[l]
                    name = {L0_FFN: "l0f", L1_FFN: "l1f", L2_MOE: "l2f", L3_FFN: "l3f"}[l]
                    n_chunks = {L0_FFN: 8, L1_FFN: 2, L2_MOE: 8, L3_FFN: 5}[l]
                    experts = E16 if l == L3_FFN else E8
                    pe.wait_ge(w_in[name], 16)
                    pe.sem_inc(f["y"], 2)
                    pe.sem_inc(f["o"], 2)
                    pe.sem_inc(f["oc"], 2)
                    with pe.Fori(0, NB) as i:
                        unit_ready(i)
                        for t in range(T):
                            ins = pe.matmul(GATE[:, t, 0:experts], hT[:, t * P:(t + 1) * P], w(name, "router"),
                                            start=True, stop=True)
                        ins.then_inc(f["gate"], 1)
                        if l == L2_MOE:
                            pe.wait_ge(f["rk"], i + 1)
                            for t in range(T):
                                pe.matmul(GATE[:, t, 8:16], w("cbf", "before"), mbf[:, t, :], start=True, stop=False)
                                ins = pe.matmul(GATE[:, t, 8:16], w("cbf", "ones"), (cum if t == 0 else cum1)[:],
                                                start=False, stop=True)
                            ins.then_inc(f["c"], 1)

                        def up(c):
                            pe.wait_ge(f["y"], i * n_chunks + (2 if l == L3_FFN and c == 0 else c + 1))
                            if l == L0_FFN:
                                srcs = [(g, w(name, "w1")[:, ((c * 2 + g) * 2 + b) * P:((c * 2 + g) * 2 + b + 1) * P], b)
                                        for g in range(2) for b in range(2)]
                            elif l == L3_FFN and c < 4:
                                srcs = [(g, w(name, n)[:, (2 * c + b) * P:(2 * c + b + 1) * P], b)
                                        for g, n in ((0, "w1"), (1, "w3")) for b in range(2)]
                            elif l == L3_FFN:
                                srcs = [(0, w(name, "w1s"), 0), (1, w(name, "w3s"), 0)]
                            else:
                                srcs = [(0, w(name, "w1")[:, (2 * c + b) * P:(2 * c + b + 1) * P], b) for b in range(2)]
                            for g, wt, b in srcs:
                                ins = pe.matmul(PS[:, 2 * (c % 2) + g, b * L:(b + 1) * L], wt, hT[:], start=True, stop=True)
                            ins.then_inc(f["g"], 1)

                        def share(c):
                            if c == 0:
                                pe.wait_ge(f["c"], i + 1)
                            for b in range(2):
                                for t in range(T):
                                    e = 2 * (2 * c + b)
                                    ins = pe.transpose(
                                        PS[:, 4 + c % 2, b * L + t * P:b * L + (t + 1) * P],
                                        cwx[:, t, e:e + 2, :].rearrange("p e f -> p (e f)"), ident)
                            ins.then_inc(f["cT"], 1)

                        def down(c):
                            pe.wait_ge(f["y"], i * n_chunks + (c + 3))
                            if l in (L0_FFN, L2_MOE):
                                pe.wait_ge(f["oc"], i * n_chunks + (c + 1))
                                for t in range(T):
                                    for b in range(2):
                                        ins = pe.matmul(
                                            PS[:, 4 + c % 2, t * P:(t + 1) * P],
                                            y[:, c % 2, b * L + t * P:b * L + (t + 1) * P],
                                            w(name, "w2")[:, (2 * c + b) * D:(2 * c + b + 1) * D],
                                            start=b == 0, stop=b == 1)
                            else:
                                if c == 0:
                                    y_free(i)
                                nb = 1 if l == L3_FFN and c == 4 else 2
                                for b in range(nb):
                                    for t in range(T):
                                        w2 = (w(name, "w2s") if nb == 1 else
                                              w(name, "w2")[:, (2 * c + b) * D:(2 * c + b + 1) * D])
                                        ins = pe.matmul(Y[:, t, :], y[:, c % 2, b * L + t * P:b * L + (t + 1) * P], w2,
                                                        start=c == 0 and b == 0 and t == 0,
                                                        stop=c == n_chunks - 1 and b == nb - 1,
                                                        skip_group_check=True)
                            ins.then_inc(f["o"], 1)

                        for c in range(n_chunks + 1):
                            if c < n_chunks:
                                up(c)
                            if l == L3_FFN and 1 <= c <= 4:
                                share(c - 1)
                            if c == n_chunks - 1:
                                head_transpose(l, i)
                            if c >= 1:
                                down(c - 1)

        @block.vector
        def _(dve):
            def head_stats(src, u):
                for t in range(T):
                    dve.bn_stats(hst[:, t, :], src[:, bass.ds(u * T + t, 1), :].rearrange("p a b -> p (a b)"))
                dve.drain()
                for t in range(T):
                    ins = dve.bn_aggr(hmv[:, t, :], hst[:, t, :])
                ins.then_inc(hd_stat, 1)

            def head_norm(src, u, count):
                dve.wait_ge(hd_tr, count - 1)
                dve.wait_ge(hd_rstd, count)
                for t in range(T):
                    ins = dve.tensor_scalar(h[:, t, :], src[:, bass.ds(u * T + t, 1), :].rearrange("p a b -> p (a b)"),
                                            hmv[:, t, 0:1], hrs[:, t:t + 1], ALU.subtract, ALU.mult)
                ins.then_inc(hd_h, 1)

            def tail(l, i, src):
                for t in range(T):
                    dve.bn_stats(tst[:, t, :], src[:, t, :])
                dve.drain()
                for t in range(T):
                    ins = dve.bn_aggr(tmv[:, t, :], tst[:, t, :])
                ins.then_inc(tl_stat, 1)
                dve.wait_ge(tl_rstd, i + (tail0[l] + 1))
                for t in range(T):
                    dve.tensor_scalar(tn[:, t, :], src[:, t, :], tmv[:, t, 0:1], trs[:, t:t + 1],
                                      ALU.subtract, ALU.mult)
                dve.drain()
                dve.tensor_tensor(X[:, bass.ds(i * T, T), :], X[:, bass.ds(i * T, T), :], tn[:], ALU.add)\
                   .then_inc(x_done, 1)
                dve.drain()

            def top(p, n, k, weighted, scratch_rank, lower):
                gt = gtb[:, :, 0:n * n].rearrange("p t (j i) -> p t j i", i=n)
                eq = eqb[:, :, 0:n * n].rearrange("p t (j i) -> p t j i", i=n)
                other = p.unsqueeze(2).to_broadcast([P, T, n, n])
                own = p.unsqueeze(3).to_broadcast([P, T, n, n])
                dve.tensor_tensor(gt, other, own, ALU.is_gt)
                dve.tensor_tensor(eq, other, own, ALU.is_equal)
                dve.drain()
                dve.tensor_tensor(eq, eq, lower.rearrange("p (a j i) -> p a j i", a=1, i=n).to_broadcast([P, T, n, n]),
                                  ALU.mult)
                dve.drain()
                dve.tensor_tensor(gt, gt, eq, ALU.add)
                dve.drain()
                dve.tensor_reduce(scratch_rank, gt, AX.X, ALU.add)
                dve.drain()
                if weighted is not None:
                    dve.scalar_tensor_tensor(weighted, scratch_rank, float(k), p, ALU.is_lt, ALU.mult)
                    dve.drain()

            dve.wait_ge(x_in, 16)
            dve.wait_ge(consts, 1)
            dve.wait_ge(w_in["const"], 16)
            dve.wait_ge(wb_in, 16)
            dve.tensor_copy(W["cbf"][:], cbf_f[:, 0:PACKS_BF["cbf"].width]).then_inc(cbf_ready, 1)
            for l in run:
                src_h = H1 if l == L2_MOE else X
                if own_head(l):
                    head_stats(src_h, 0)
                    dve.wait_ge(hd_rstd, head0[l] + 1)
                    if head0[l]:
                        dve.wait_ge(hd_tr, head0[l])
                    for t in range(T):
                        ins = dve.tensor_scalar(h[:, t, :], src_h[:, t, :], hmv[:, t, 0:1], hrs[:, t:t + 1],
                                                ALU.subtract, ALU.mult)
                    ins.then_inc(hd_h, 1)
                    dve.drain()

                if l == L0_ATTN:
                    dve.wait_ge(w_in["l0a"], 16)
                    for dst, wt, cv in ((wkc, "wk", "conv_k"), (wsc, "ws", "conv_s")):
                        dve.tensor_tensor(dst[:], w("l0a", wt).unsqueeze(1).to_broadcast([P, TAPS, D]),
                                          w("l0a", cv).rearrange("p (j d) -> p j d", j=TAPS), ALU.mult)
                    dve.tensor_tensor(coef[:, 0, :], w("l0a", "norm_re"), w("l0a", "diag_re"), ALU.mult)
                    dve.tensor_tensor(coef[:, 1, :], w("l0a", "norm_im"), w("l0a", "diag_im"), ALU.mult)
                    dve.drain()
                    dve.tensor_tensor(wab[:, 0, :], w("l0a", "wq_re"), coef[:, 0, :], ALU.mult)
                    dve.tensor_tensor(wab[:, 1, :], w("l0a", "wq_im"), coef[:, 0, :], ALU.mult)
                    dve.tensor_tensor(wtmp[:, 0, :], w("l0a", "wq_im"), coef[:, 1, :], ALU.mult)
                    dve.tensor_tensor(wtmp[:, 1, :], w("l0a", "wq_re"), coef[:, 1, :], ALU.mult)
                    dve.drain()
                    dve.tensor_tensor(wab[:, 0, :], wab[:, 0, :], wtmp[:, 0, :], ALU.subtract)
                    dve.tensor_tensor(wab[:, 1, :], wab[:, 1, :], wtmp[:, 1, :], ALU.add)
                    dve.drain()
                    rep = KCH // KQ
                    for g, dst in ((0, wA), (1, wB)):
                        for m in range(NM):
                            dve.tensor_copy(
                                dst[:, m, :].rearrange("p (q r h) -> p q r h", q=KQ, r=rep),
                                wab[:, g, :].rearrange("p (q a h m) -> p q a h m", q=KQ, a=1, h=HC)[:, :, :, :, m]
                                .to_broadcast([P, KQ, rep, HC]))
                    dve.tensor_scalar(theta[:], w("l0a", "theta"), float(1.0 / (2 * np.pi)), None, ALU.mult)
                    dve.wait_ge(a_soft, 1)
                    dve.tensor_tensor(slope[:, 0:1], slope[:, 2:3], slope[:, 3:4], ALU.add)
                    dve.drain()
                    dve.tensor_scalar(logw[:], w("const", "decay_pos"), slope[:, 0:1], None, ALU.mult)
                    dve.drain().then_inc(a_w, 1)
                    with dve.Fori(0, NB) as i:
                        nxt = (i + 1) % NB
                        head_stats(X, nxt)
                        dve.wait_ge(a_z, i + 1)
                        dve.tensor_scalar(la[:], PS[:, 5, L:2 * L], w("l0a", "score"), 20.0, ALU.mult, ALU.min)
                        dve.drain()
                        dve.scalar_tensor_tensor(la[:], la[:], -20.0, logw[:], ALU.max, ALU.add).then_inc(a_lg, 1)

                        def reduce_turns(c):
                            dve.wait_ge(a_u, i * CHUNKS + (c + 1))
                            dve.tensor_scalar(sbuf[:, c], cb[:, c], MAGIC, None, ALU.add)
                            dve.drain()
                            dve.scalar_tensor_tensor(sbuf[:, c], sbuf[:, c], MAGIC, cb[:, c],
                                                     ALU.subtract, ALU.subtract).then_inc(a_red, 1)

                        def cumulate(c):
                            dve.wait_ge(a_pp, i * CHUNKS + (c + 1))
                            cf = carry[:].rearrange("p m t -> p (m t)")
                            for b in (cb, sbuf):
                                flat = b[:, c].rearrange("p m t -> p (m t)")
                                dve.tensor_tensor_scan(flat, cf, flat, 0.0, ALU.mult, ALU.add)
                            dve.drain()
                            dve.wait_ge(a_ab, i * CHUNKS + (c + 1))
                            for g, b in ((0, cb), (1, sbuf)):
                                flat = b[:, c].rearrange("p m t -> p (m t)")
                                ins = dve.tensor_tensor(flat, flat, PS[:, 1 + 2 * (c % 2) + g, :], ALU.mult)
                            ins.then_inc(a_pr, 1)

                        reduce_turns(0)
                        reduce_turns(1)
                        dve.wait_ge(a_p, i + 1)
                        dve.tensor_tensor_scan(den[:], one_c[:].to_broadcast([P, L]), pw[:], 0.0, ALU.mult, ALU.add)
                        dve.drain()
                        dve.tensor_scalar(den[:], den[:], 1e-4, None, ALU.max)
                        dve.drain()
                        dve.reciprocal(inv[:], den[:])
                        reduce_turns(2)
                        cumulate(0)
                        reduce_turns(3)
                        head_norm(X, nxt, i + (head0[l] + 2))
                        cumulate(1)
                        cumulate(2)
                        cumulate(3)
                        dve.wait_ge(a_sum, i * CHUNKS + 2 * CHUNKS)
                        dve.tensor_tensor(arg[:], inv[:], PS[:, 5, 0:L], ALU.mult).then_inc(a_arg, 1)
                        dve.wait_ge(y_ready, i + (res0[l] + 1))
                        tail(l, i, Y)
                elif l in (L1_ATTN, L2_ATTN, L3_ATTN):
                    name = {L1_ATTN: "l1a", L2_ATTN: "l2a", L3_ATTN: "l3a"}[l]
                    dve.wait_ge(w_in[name], 16)
                    nk = 1 if l == L3_ATTN else NH
                    with dve.Fori(0, NB) as i:
                        nxt = (i + 1) % NB
                        head_stats(X, nxt)
                        dve.wait_ge(t_qkv, i + (att0[l] + 1))
                        used = D + 2 * HD if l == L3_ATTN else 3 * D
                        if l == L1_ATTN:
                            dve.tensor_tensor(qkv[:], PS[:, 4:6, 0:3 * D],
                                              w(name, "bqkv").unsqueeze(1).to_broadcast([P, T, 3 * D]), ALU.add)
                        else:
                            dve.tensor_copy(qkv[:, :, 0:used], PS[:, 4:6, 0:used])
                        dve.drain()
                        q4 = qkv[:, :, 0:D].rearrange("p t (a d) -> p t a d", d=HD)
                        vsrc = qkv[:, :, used - nk * HD:used].rearrange("p t (a d) -> p t a d", d=HD)
                        dve.tensor_scalar(VA[:, :, 0:nk, 0:HD], vsrc, 1e-3 if l == L2_ATTN else 1.0, None, ALU.mult)
                        QSv = QS[:].rearrange("p (t a) (s d) -> p t a s d", t=T, d=HD)
                        KSv = KS[:].rearrange("p (t a) (s d) -> p t a s d", t=T, d=HD)
                        restv = rest[:].rearrange("p (t a) d -> p t a d", t=T)

                        def split(src, dst, n, slots, t):
                            cur = src[:, t]
                            for part in range(3):
                                a, b, st = slots[part]
                                cnt = len(range(a, b, st))
                                dve.tensor_copy(dst[:, t, 0:n, a:b:st, :],
                                                cur.unsqueeze(2).to_broadcast([P, n, cnt, HD]))
                                dve.drain()
                                if part < 2:
                                    dve.tensor_tensor(restv[:, t, 0:n, :], cur, dst[:, t, 0:n, a, :], ALU.subtract)
                                    dve.drain()
                                    cur = restv[:, t, 0:n, :]

                        if l == L3_ATTN:
                            k4 = qkv[:, :, D:D + HD].rearrange("p t (a d) -> p t a d", d=HD)
                        else:
                            k4 = qkv[:, :, D:2 * D].rearrange("p t (a d) -> p t a d", d=HD)
                        for t in range(T):
                            split(k4, KSv, nk, ((0, 3, 1), (3, 6, 1), (6, 7, 1)), t)
                            split(q4, QSv, NH, ((0, 7, 3), (1, 6, 3), (2, 6, 3)), t)
                            if l == L3_ATTN:
                                dve.tensor_copy(KS[:, t * NH + 1, 0:PARTS], KS[:, t * NH, 0:PARTS])
                        dve.drain().then_inc(t_split, 1)
                        head_norm(X, nxt, i + (head0[l] + 2))
                        if l != L2_ATTN:
                            for pair in range(NH // 2):
                                dve.wait_ge(t_s, i * (NH // 2) + (att_s[l] + pair + 1))
                                b = 2 * (pair % 2)
                                dve.tensor_reduce(mx[:, 2 * pair:2 * pair + 2, :],
                                                  PS[:, b:b + 2, :].rearrange("p a (t k) -> p a t k", t=T),
                                                  AX.X, ALU.max).then_inc(t_mx, 1)
                            dve.drain()
                            dve.tensor_scalar(mr[:], mx[:].rearrange("p a t -> p t a"), -1.0, None, ALU.mult)
                            dve.drain()
                            QM = QS[:].rearrange("p (t a) c -> p t a c", t=T)
                            for part in range(AUG):
                                dve.tensor_copy(QM[:, :, :, PARTS + part], mr[:])
                                dve.drain()
                                if part < AUG - 1:
                                    dve.tensor_tensor(mr[:], mr[:], QM[:, :, :, PARTS + part], ALU.subtract)
                                    dve.drain()
                            dve.drain().then_inc(t_m, 1)
                        else:
                            for hh in range(NH):
                                s = hh % 4
                                dve.wait_ge(t_pn, i * NH + (hh + 1))
                                dve.tensor_scalar(PG2[:, hh % 2, :], PN[:, s, 0:384], 1.0, None, ALU.add)
                                dve.drain()
                                dve.scalar_tensor_tensor(PN[:, s, 0:384], PN[:, s, 0:384], 1.0, PG2[:, hh % 2, :],
                                                         ALU.is_le, ALU.mult).then_inc(t_m2, 1)
                        dve.wait_ge(t_pv, i * NH + (att_pt[l] + NH + 4))
                        O = PS[:, 5, 0:T * NH * VW].rearrange("p (t a c) -> p t a c", t=T, c=VW)
                        ov = osb[:].rearrange("p t (a d) -> p t a d", d=HD)
                        if l == L2_ATTN:
                            dve.tensor_copy(ov, O[:, :, :, 0:HD]).then_inc(t_o, 1)
                        else:
                            dve.reciprocal(rsum[:], O[:, :, :, HD])
                            dve.drain()
                            dve.tensor_tensor(ov, O[:, :, :, 0:HD],
                                              rsum[:].unsqueeze(3).to_broadcast([P, T, NH, HD]),
                                              ALU.mult).then_inc(t_o, 1)
                        dve.wait_ge(y_ready, i + (res0[l] + 1))
                        if l == L1_ATTN:
                            dve.tensor_tensor(acc[:], Y, w(name, "bout").unsqueeze(1).to_broadcast([P, T, D]), ALU.add)
                            dve.drain()
                            tail(l, i, acc)
                        else:
                            tail(l, i, Y)
                elif l == L2_MIX:
                    with dve.Fori(0, NB) as i:
                        nxt = (i + 1) % NB
                        for t in range(T):
                            dve.bn_stats(tst[:, t, :], h[:, t, :])
                        dve.drain()
                        for t in range(T):
                            ins = dve.bn_aggr(tmv[:, t, :], tst[:, t, :])
                        ins.then_inc(m_st, 1)
                        dve.tensor_copy(H1[:, bass.ds(i * T, T), :], h[:])
                        head_stats(X, nxt)
                        dve.wait_ge(m_rs, i + 1)
                        for t in range(T):
                            ins = dve.tensor_scalar(n1[:, t, :], h[:, t, :], tmv[:, t, 0:1], trs[:, t:t + 1],
                                                    ALU.subtract, ALU.mult)
                        ins.then_inc(m_n1, 1)
                        dve.drain()
                        head_norm(X, nxt, i + (head0[l] + 2))
                        dve.wait_ge(m_qkv, i + 1)
                        src = PS[:, 1, 0:T * 192].rearrange("p (t g c) -> p t g c", t=T, g=NG)
                        dve.tensor_copy(q2[:].rearrange("p t g q d -> p t g (q d)"), src[:, :, :, 0:32])
                        for t in range(T):
                            dve.tensor_copy(KC[:, t, :, bass.ds(i, 1), :].rearrange("p g a d -> p g (a d)"),
                                            src[:, t, :, 32:40])
                            dve.tensor_copy(VC[:, t, :, :, bass.ds(i, 1)].rearrange("p g d a -> p g (d a)"),
                                            src[:, t, :, 40:48])
                        dve.drain()
                        for t in range(T):
                            for g in range(NG):
                                dve.tensor_tensor(
                                    prod[:, t * NG + g, :].rearrange("p (q s d) -> p q s d", q=4, s=NB),
                                    q2[:, t, g].unsqueeze(2).to_broadcast([P, 4, NB, HD]),
                                    KC[:, t, g].unsqueeze(1).to_broadcast([P, 4, NB, HD]), ALU.mult)
                        dve.drain()
                        dve.tensor_reduce(sc2[:].rearrange("p a s -> p (a s)"),
                                          prod.rearrange("p a (b d) -> p (a b) d", d=HD), AX.X, ALU.add)
                        dve.drain()
                        crow = w("const", "causal8").rearrange("p (a b) -> p a b", b=NB)
                        dve.tensor_scalar(sc2[:], sc2[:], SM_SCALE, None, ALU.mult)
                        dve.drain()
                        dve.tensor_tensor(sc2[:], sc2[:], crow[:, bass.ds(i, 1), :].to_broadcast([P, T * NH, NB]),
                                          ALU.add)
                        dve.drain()
                        dve.tensor_reduce(mx2[:], sc2[:], AX.X, ALU.max)
                        dve.drain()
                        dve.tensor_tensor(sc2[:], sc2[:], mx2[:].unsqueeze(2).to_broadcast([P, T * NH, NB]),
                                          ALU.subtract).then_inc(m_sc, 1)
                        dve.wait_ge(m_ex, i + 1)
                        dve.tensor_reduce(sm2[:], ex2[:], AX.X, ALU.add)
                        for t in range(T):
                            for g in range(NG):
                                a = (t * NG + g) * 4
                                dve.tensor_tensor(
                                    prod[:, t * NG + g, :].rearrange("p (q d s) -> p q d s", q=4, s=NB),
                                    ex2[:, a:a + 4, :].unsqueeze(2).to_broadcast([P, 4, HD, NB]),
                                    VC[:, t, g].unsqueeze(1).to_broadcast([P, 4, HD, NB]), ALU.mult)
                        dve.drain()
                        dve.tensor_reduce(ao[:].rearrange("p a d -> p (a d)"),
                                          prod.rearrange("p a (b s) -> p (a b) s", s=NB), AX.X, ALU.add)
                        dve.reciprocal(sm2[:], sm2[:])
                        dve.drain()
                        dve.tensor_tensor(ao[:], ao[:], sm2[:].unsqueeze(2).to_broadcast([P, T * NH, HD]),
                                          ALU.mult).then_inc(m_ao, 1)
                        dve.wait_ge(m_y, i + 1)
                        dve.tensor_tensor(H1[:, bass.ds(i * T, T), :], H1[:, bass.ds(i * T, T), :],
                                          PS[:, 3, 0:L].rearrange("p (t d) -> p t d", t=T), ALU.add).then_inc(h1_done, 1)
                        dve.drain()
                else:
                    f, GATE = FF[l], GATES[l]
                    n_chunks = {L0_FFN: 8, L1_FFN: 2, L2_MOE: 8, L3_FFN: 5}[l]
                    ne = E16 if l == L3_FFN else E8
                    with dve.Fori(0, NB) as i:
                        nxt = (i + 1) % NB
                        head_stats(src_h, nxt)
                        dve.wait_ge(f["gate"], i + 1)
                        if l == L3_FFN:
                            dve.tensor_scalar(lg[:], GATE, -80.0, None, ALU.max).then_inc(f["ge"], 1)
                            dve.wait_ge(f["gx"], i + 1)
                            dve.tensor_scalar(ex[:], ex[:], 1.0, None, ALU.add)
                            dve.drain()
                            dve.reciprocal(ex[:], ex[:])
                            dve.drain()
                            v = ex[:].rearrange("p t (g c) -> p (t g) c", c=4)
                            dve.tensor_tensor(hilo[:, 0], v[:, :, 0:2], v[:, :, 2:4], ALU.max)
                            dve.tensor_tensor(hilo[:, 1], v[:, :, 0:2], v[:, :, 2:4], ALU.min)
                            dve.drain()
                            dve.tensor_tensor(hilo[:, 2, :, 0], hilo[:, 0, :, 0], hilo[:, 0, :, 1], ALU.max)
                            dve.tensor_tensor(hilo[:, 2, :, 1], hilo[:, 0, :, 0], hilo[:, 0, :, 1], ALU.min)
                            dve.tensor_tensor(hilo[:, 3, :, 0], hilo[:, 1, :, 0], hilo[:, 1, :, 1], ALU.max)
                            dve.drain()
                            dve.tensor_tensor(hilo[:, 3, :, 1], hilo[:, 2, :, 1], hilo[:, 3, :, 0], ALU.max)
                            dve.drain()
                            dve.tensor_tensor(gsc[:].rearrange("p t g -> p (t g)"), hilo[:, 2, :, 0],
                                              hilo[:, 3, :, 1], ALU.add)
                            dve.drain()
                            top(gsc[:], NG, 2, None, gal[:], w("const", "rank4"))
                            dve.tensor_scalar(gal[:], gal[:], 2.0, None, ALU.is_lt)
                            dve.drain()
                            dve.tensor_scalar(gsc[:], gal[:], -1.0, None, ALU.add)
                            ga = gal[:].unsqueeze(3).to_broadcast([P, T, NG, 4])
                            gb = gsc[:].unsqueeze(3).to_broadcast([P, T, NG, 4])
                            m4 = msk[:].rearrange("p t (g c) -> p t g c", c=4)
                            dve.tensor_tensor(m4, ex[:].rearrange("p t (g c) -> p t g c", c=4), ga, ALU.mult)
                            dve.drain()
                            dve.tensor_tensor(m4, m4, gb, ALU.add)
                            dve.drain()
                            top(msk[:], E16, 4, msk[:], rank[:], w("const", "rank16"))
                            dve.tensor_reduce(gsm[:], msk[:], AX.X, ALU.add)
                            dve.drain()
                            dve.tensor_scalar(gsm[:], gsm[:], 1e-6, None, ALU.add)
                            dve.drain()
                            dve.reciprocal(gsm[:], gsm[:])
                            dve.drain()
                            dve.tensor_tensor(cw[:], msk[:], gsm[:].unsqueeze(2).to_broadcast([P, T, E16]),
                                              ALU.mult)
                            dve.drain()
                            for t in range(T):
                                ins = dve.tensor_copy(cwx[:, t, :, :], cw[:, t].unsqueeze(2).to_broadcast([P, E16, F16]))
                            ins.then_inc(f["c"], 1)
                        else:
                            g8, e8 = GATE[:, :, 0:E8], ex[:, :, 0:E8]
                            dve.tensor_reduce(gmx[:], g8, AX.X, ALU.max)
                            dve.drain()
                            dve.tensor_tensor(lg[:, :, 0:E8], g8, gmx[:].unsqueeze(2).to_broadcast([P, T, E8]),
                                              ALU.subtract).then_inc(f["ge"], 1)
                            dve.wait_ge(f["gx"], i + 1)
                            dve.tensor_reduce(gsm[:], e8, AX.X, ALU.add)
                            dve.drain()
                            dve.reciprocal(gsm[:], gsm[:])
                            dve.drain()
                            dve.tensor_tensor(cw[:, :, 0:E8], e8, gsm[:].unsqueeze(2).to_broadcast([P, T, E8]), ALU.mult)
                            dve.drain()
                            if l != L1_FFN:
                                top(cw[:, :, 0:E8], E8, 2, cw[:, :, 0:E8], rank[:, :, 0:E8], w("const", "rank8"))
                            if l == L2_MOE:
                                dve.tensor_reduce(gsm[:], cw[:, :, 0:E8], AX.X, ALU.add)
                                dve.tensor_scalar(mbf[:], rank[:, :, 0:E8], 2.0, None, ALU.is_lt)
                                dve.drain()
                                dve.tensor_tensor(cum1[:], cum[:], mbf[:, 0, :], ALU.add)
                                dve.reciprocal(gsm[:], gsm[:])
                                dve.drain().then_inc(f["rk"], 1)
                                dve.tensor_tensor(cw[:, :, 0:E8], cw[:, :, 0:E8],
                                                  gsm[:].unsqueeze(2).to_broadcast([P, T, E8]), ALU.mult)
                                dve.drain()
                                dve.wait_ge(f["c"], i + 1)
                                dve.scalar_tensor_tensor(cw[:, :, 0:E8], GATE[:, :, 8:16], float(CAP),
                                                         cw[:, :, 0:E8], ALU.is_lt, ALU.mult)
                                dve.tensor_tensor(cum[:], cum1[:], mbf[:, 1, :], ALU.add)
                                dve.drain()
                        if l in (L1_FFN,):
                            head_norm(src_h, nxt, i + (head0[l] + 2))

                        def combine(c):
                            dve.wait_ge(f["o"], i * n_chunks + (c + 3))
                            for t in range(T):
                                src = PS[:, 4 + c % 2, t * P:(t + 1) * P]
                                if c == 0:
                                    ins = dve.tensor_scalar(acc[:, t, :], src, cw[:, t, 0:1], None, ALU.mult)
                                else:
                                    ins = dve.scalar_tensor_tensor(acc[:, t, :], src, cw[:, t, c:c + 1], acc[:, t, :],
                                                                   ALU.mult, ALU.add)
                            ins.then_inc(f["oc"], 1)

                        if l in (L0_FFN, L3_FFN):
                            for c in range(n_chunks):
                                cols = 2 * L if not (l == L3_FFN and c == 4) else L
                                dve.wait_ge(f["sg"], i * n_chunks + (c + 1))
                                dve.wait_ge(f["o"], i * n_chunks + (2 if l == L3_FFN and c == 0 else c + 1))
                                ins = dve.tensor_tensor(y[:, c % 2, 0:cols], sg[:, c % 2, 0:cols],
                                                        PS[:, 2 * (c % 2) + 1, 0:cols], ALU.mult)
                                if l == L3_FFN and c < 4:
                                    dve.drain()
                                    dve.wait_ge(f["cT"], i * 4 + (c + 1))
                                    dve.tensor_tensor(y[:, c % 2, :], y[:, c % 2, :], PS[:, 4 + c % 2, :], ALU.mult)\
                                       .then_inc(f["y"], 1)
                                else:
                                    ins.then_inc(f["y"], 1)
                                if c == 1:
                                    head_norm(src_h, nxt, i + (head0[l] + 2))
                                if l == L0_FFN and c >= 1:
                                    combine(c - 1)
                                    dve.drain()
                            if l == L0_FFN:
                                combine(n_chunks - 1)
                                dve.drain()
                        elif l == L2_MOE:
                            for c in range(n_chunks):
                                if c == 2:
                                    head_norm(src_h, nxt, i + (head0[l] + 2))
                                combine(c)
                                dve.drain()
                            dve.tensor_tensor(acc[:], acc[:], H1[:, bass.ds(i * T, T), :], ALU.add)
                            dve.drain()
                        if l in (L0_FFN, L2_MOE):
                            tail(l, i, acc)
                        else:
                            dve.wait_ge(f["o"], i * n_chunks + (n_chunks + 2))
                            if l == L1_FFN:
                                dve.tensor_tensor(acc[:], Y, w("l1f", "b2").unsqueeze(1).to_broadcast([P, T, D]), ALU.add)
                                dve.drain()
                                for t in range(T):
                                    dve.tensor_scalar(acc[:, t, :], acc[:, t, :], cw[:, t, 7:8], None, ALU.mult)
                                dve.drain()
                                tail(l, i, acc)
                            else:
                                tail(l, i, Y)


def _pack(fields, parts):
    out = []
    for name, width in fields.at.items():
        a = np.asarray(parts[name])
        a = a.reshape(1 if a.size == width[1] else a.shape[0], width[1])
        if a.shape[0] == 1:
            a = np.broadcast_to(a, (P, width[1]))
        if a.shape[0] < P:
            a = np.concatenate([a, np.zeros((P - a.shape[0], width[1]), a.dtype)])
        out.append(a)
    return np.ascontiguousarray(np.concatenate(out, axis=1), dtype=np.float32)


def _constants():
    r = np.arange(P)
    t = np.arange(L)
    lower = lambda n: (np.arange(n)[None, :] < np.arange(n)[:, None]).astype(np.float32).reshape(1, -1)
    pos = np.where((np.repeat(np.arange(KCH), HC) < KCH - HC)[:, None], -(L - 1 - t)[None, :], -t[None, :])
    causal8 = np.where(np.arange(NB)[None, :] > np.arange(NB)[:, None], NEG, 0.0).reshape(1, -1)
    const = _pack(PACKS["const"], dict(ident=np.eye(P), rank8=lower(E8), rank16=lower(E16), rank4=lower(NG),
                                       causal8=causal8, decay_pos=pos))
    mask_q = np.concatenate([np.where(t[None, :] > r[:, None] + P * j, NEG, 0.0) for j in range(T)], axis=1)
    mask_k = np.concatenate([np.where(r[:, None] > t[None, :], NEG, 0.0),
                             np.where(r[:, None] > r[None, :], NEG, 0.0)], axis=1)
    cbf = _pack(PACKS_BF["cbf"], dict(ident=np.eye(P), mask_q=mask_q, mask_k=mask_k,
                                      before=(r[:, None] < r[None, :]).astype(np.float32), ones=np.ones((P, P))))
    return const, cbf


def kernel(**inputs):
    import concourse.bacc as _bacc
    from concourse.bass_utils import run_bass_kernel_spmd as _run

    v = {k: np.asarray(a) for k, a in inputs.items()}
    W_in = v["L0_attn_W_in"]
    wq = W_in[:, D + KCH:].reshape(D, KQ, HC, NM, 2)
    conv = v["L0_attn_conv_k"][:, 0, :]
    over_q = lambda a: np.broadcast_to(a.reshape(1, 1, HC, 1), (1, KQ, HC, NM)).reshape(1, -1)
    norm = v["L0_attn_norm_scale"]
    heads = lambda a: np.ascontiguousarray(a.reshape(NH, 3, HD, -1).transpose(1, 0, 2, 3)).reshape(3 * D, -1)
    halves = lambda a: a.reshape(-1, 2, P, D).transpose(2, 0, 1, 3).reshape(P, -1)
    const, cbf = _constants()
    arrays = {
        "x": np.ascontiguousarray(v["L0_attn_x"]), "const": const, "cbf": cbf,
        "l0a": _pack(PACKS["l0a"], dict(
            wk=W_in[:, :D], ws=np.repeat(W_in[:, D:D + KCH], HC, axis=1), wq_re=wq[..., 0], wq_im=wq[..., 1],
            wout=v["L0_attn_W_out"], conv_k=conv[:, :D].reshape(1, -1),
            conv_s=np.repeat(conv[:, D:], HC, axis=1).reshape(1, -1), norm_re=over_q(norm[:HC]),
            norm_im=over_q(norm[HC:]), diag_re=over_q(np.diagonal(v["L0_attn_W_re"])),
            diag_im=over_q(np.diagonal(v["L0_attn_W_im"])), theta=v["L0_attn_theta"].reshape(P, NM),
            slope=np.repeat(np.concatenate([v["L0_attn_decay_slopes"], v["L0_attn_anchor_slopes"]]), HC)[:, None],
            score=np.repeat(v["L0_attn_score_scale"], HC)[:, None])),
        "l0f": _pack(PACKS["l0f"], dict(
            router=v["L0_ffn_router_w"].T, w1=v["L0_ffn_w1"].transpose(2, 0, 1),
            w2=halves(v["L0_ffn_w2"].transpose(0, 2, 1)))),
        "l1a": _pack(PACKS["l1a"], dict(
            wqkv=heads(v["L1_attn_Wqkv"]).T, bqkv=heads(v["L1_attn_bqkv"]).reshape(1, -1), wout=v["L1_attn_Wout"].T,
            bout=v["L1_attn_bout"].reshape(1, -1))),
        "l1f": _pack(PACKS["l1f"], dict(
            router=v["L1_ffn_Wr"].T, w1=v["L1_ffn_W1"][E8 - 1], b1=v["L1_ffn_b1"][E8 - 1].reshape(4, P).T,
            w2=v["L1_ffn_W2"][E8 - 1].reshape(4, P, D).transpose(1, 0, 2), b2=v["L1_ffn_b2"][E8 - 1].reshape(1, -1))),
        "l2a": _pack(PACKS["l2a"], dict(wqkv=v["L2_attn_W_attn"], wout=v["L2_attn_W_proj"])),
        "l2f": _pack(PACKS["l2f"], dict(
            ln1w=v["L2_ffn_ln1_weight"][:, None], ln1b=v["L2_ffn_ln1_bias"][:, None],
            ln2w=v["L2_ffn_ln2_weight"][:, None], ln2b=v["L2_ffn_ln2_bias"][:, None], qkv=v["L2_ffn_qkv_weight"].T,
            proj=v["L2_ffn_proj_weight"].T, router=v["L2_ffn_router_weight"],
            w1=v["L2_ffn_moe_w1"].transpose(1, 0, 2), w2=halves(v["L2_ffn_moe_w2"]))),
        "l3a": _pack(PACKS["l3a"], dict(
            down=v["L3_attn_Wc_down"], up=np.concatenate([v["L3_attn_Wq_up"], v["L3_attn_Wkv_up"]], axis=1),
            wout=v["L3_attn_Wc_proj"])),
        "l3f": _pack(PACKS["l3f"], dict(
            router=v["L3_ffn_w_gate"].T, w1=v["L3_ffn_w1_e"].transpose(2, 0, 1), w3=v["L3_ffn_w3_e"].transpose(2, 0, 1),
            w2=v["L3_ffn_w2_e"].transpose(0, 2, 1).reshape(8, P, D).transpose(1, 0, 2), w1s=v["L3_ffn_w1_s"].T,
            w3s=v["L3_ffn_w3_s"].T, w2s=v["L3_ffn_w2_s"].T)),
    }
    nc = _bacc.Bacc("TRN2", target_bir_lowering=False, num_devices=1)
    aps = {n: nc.dram_tensor("in_" + n, a.shape, F32, kind="ExternalInput").ap()
           for n, a in arrays.items()}
    out = nc.dram_tensor("result", (NB, L, D), F32, kind="ExternalOutput").ap()
    block_program(nc, aps["x"], {n: aps[n] for n in PACKS}, {"cbf": aps["cbf"]}, out)
    r = _run(nc, [{"in_" + n: a for n, a in arrays.items()}], core_ids=[0])
    return r.results[0]["result"]
```

```python
from contextlib import ExitStack

import numpy as np

import concourse.bass as bass
from concourse import mybir

ALU = mybir.AluOpType
ACT = mybir.ActivationFunctionType
AX = mybir.AxisListType
F32 = mybir.dt.float32
BF16 = mybir.dt.bfloat16

P = 128
NB, L = 8, 256
T = L // P
D = 128
EPS = 1e-5

(L0_ATTN, L0_FFN, L1_ATTN, L1_FFN, L2_ATTN, L2_MIX, L2_MOE, L3_ATTN, L3_FFN) = range(9)
RUN = tuple(range(9))

KCH, HC, NM = 32, 4, 8
KQ = 4
TAPS = 4
CHUNK_M = 2
CHUNKS = NM // CHUNK_M
MAGIC = float(1.5 * 2 ** 23)
TWO_PI_LOW = 6.283185

NH, HD = 16, 8
SM_SCALE = 1.0 / float(np.sqrt(np.float32(HD)))
PARTS = 7 * HD
AUG = 3
SLOT = 64
VW = 32
HG = P // VW
NEG = -1e30

E8, F8 = 8, 256
FD1 = 512
E16, F16 = 16, 64
NSH = 128
CAP = 640
NG = 4


class Pack:

    def __init__(self, fields):
        self.at, n = {}, 0
        for name, width in fields:
            self.at[name] = (n, width)
            n += width
        self.width = n


PACKS = {
    "const": Pack([("ident", P), ("rank8", 64), ("rank16", 256), ("rank4", 16), ("causal8", 64), ("decay_pos", L)]),
    "l0a": Pack([("wk", D), ("ws", D), ("wq_re", P), ("wq_im", P), ("wout", D), ("conv_k", TAPS * D),
                 ("conv_s", TAPS * D), ("norm_re", P), ("norm_im", P), ("diag_re", P), ("diag_im", P),
                 ("theta", NM), ("slope", 1), ("score", 1)]),
    "l0f": Pack([("router", E8), ("w1", E8 * 2 * F8), ("w2", E8 * 2 * D)]),
    "l1a": Pack([("wqkv", 3 * D), ("bqkv", 3 * D), ("wout", D), ("bout", D)]),
    "l1f": Pack([("router", E8), ("w1", FD1), ("b1", 4), ("w2", 4 * D), ("b2", D)]),
    "l2a": Pack([("wqkv", 3 * D), ("wout", D)]),
    "l2f": Pack([("ln1w", 1), ("ln1b", 1), ("ln2w", 1), ("ln2b", 1), ("qkv", 192), ("proj", D),
                 ("router", E8), ("w1", E8 * F8), ("w2", E8 * 2 * D)]),
    "l3a": Pack([("down", 64), ("up", D + 2 * HD), ("wout", D)]),
    "l3f": Pack([("router", E16), ("w1", E16 * F16), ("w3", E16 * F16), ("w2", 8 * D), ("w1s", NSH),
                 ("w3s", NSH), ("w2s", D)]),
}
PACKS_BF = {"cbf": Pack([("ident", P), ("mask_q", 384), ("mask_k", 384), ("before", P), ("ones", P)])}


def block_program(nc, x, packs, packs_bf, out):
    ctx = ExitStack()
    with ctx:
        def sb(name, shape, dt=F32):
            return ctx.enter_context(nc.sbuf_tensor(name, shape, dt))

        def sem(name):
            return ctx.enter_context(nc.semaphore(name))

        W = {n: sb("w_" + n, [P, pk.width]) for n, pk in PACKS.items()}
        W["cbf"] = sb("w_cbf", [P, PACKS_BF["cbf"].width], BF16)

        def w(pack, name):
            a, n = (PACKS.get(pack) or PACKS_BF[pack]).at[name]
            return W[pack][:, a:a + n]

        X = sb("X", [P, NB * T, D])
        H1 = sb("H1", [P, NB * T, D])
        h = sb("h", [P, T, D])
        hT = sb("hT", [P, L])
        hst, hmv, hve, hrs = (sb("hst", [P, T, 6]), sb("hmv", [P, T, 2]), sb("hve", [P, T]), sb("hrs", [P, T]))
        tst, tmv, tve, trs = (sb("tst", [P, T, 6]), sb("tmv", [P, T, 2]), sb("tve", [P, T]), sb("trs", [P, T]))
        tn = sb("tn", [P, T, D])
        mhalf = sb("mhalf", [P, T])
        eps = sb("eps", [P, T])
        warm_t = sb("warm_t", [P, 1])
        half_pi = sb("half_pi", [P, 1])
        one_c = sb("one_c", [P, 1])
        wkc, wsc = sb("wkc", [P, TAPS, D]), sb("wsc", [P, TAPS, D])
        wab = sb("wab", [P, 2, P])
        wtmp = sb("wtmp", [P, 2, P])
        coef = sb("coef", [P, 2, P])
        wA, wB = sb("wA", [P, NM, D]), sb("wB", [P, NM, D])
        slope = sb("slope", [P, 4])
        logw = sb("logw", [P, L])
        theta = sb("theta", [P, NM])
        carry = sb("carry", [P, CHUNK_M, L])
        la, pw, den = sb("la", [P, L]), sb("pw", [P, L]), sb("den", [P, L])
        inv, arg, yT = sb("inv", [P, L]), sb("arg", [P, L]), sb("yT", [P, L])
        cb = sb("cb", [P, CHUNKS, CHUNK_M, L])
        sbuf = sb("sbuf", [P, CHUNKS, CHUNK_M, L])
        qf, kf, vf = (sb("qf", [P, T * NH, HD]), sb("kf", [P, T * NH, HD]), sb("vf", [P, T * NH, HD]))
        QS, KS = sb("QS", [P, T * NH, SLOT], BF16), sb("KS", [P, T * NH, SLOT], BF16)
        QT, KT = sb("QT", [P, NH // 2, L], BF16), sb("KT", [P, NH // 2, L], BF16)
        VA = sb("VA", [P, T, NH, VW])
        mx = sb("mx", [P, NH, 3])
        PT = sb("PT", [P, 4, 2 * L])
        PG = cb[:].rearrange("p c m t -> p c (m t)")
        PN = sbuf[:].rearrange("p c m t -> p c (m t)")
        lin1 = sb("lin1", [P, 2, 384])
        rsum = sb("rsum", [P, T, NH])
        osb = sb("osb", [P, T, D])
        oT = sb("oT", [P, L])
        latT = sb("latT", [64, L])
        cbf_f = PT[:].rearrange("p a b -> p (a b)")
        cwx = PT[:].rearrange("p a b -> p (a b)").rearrange("p (t e f) -> p t e f", t=T, e=E16)
        sg, y = sb("sg", [P, 2, 2 * L]), sb("y", [P, 2, 2 * L])
        OT = sg[:].rearrange("p a b -> p (a b)")
        acc = sb("acc", [P, T, D])
        lg, ex = sb("lg", [P, T, E16]), sb("ex", [P, T, E16])
        gmx, gsm = sb("gmx", [P, T]), sb("gsm", [P, T])
        gtb, eqb = sb("gtb", [P, T, E16 * E16]), sb("eqb", [P, T, E16 * E16])
        rank = sb("rank", [P, T, E16])
        cw = sb("cw", [P, T, E16])
        hilo = sb("hilo", [P, 4, T * NG, 2])
        gsc, gal = sb("gsc", [P, T, NG]), sb("gal", [P, T, NG])
        msk = sb("msk", [P, T, E16])
        mbf, cum = sb("mbf", [P, T, E8], BF16), sb("cum", [P, E8], BF16)
        cum1 = sb("cum1", [P, E8], BF16)
        n1, n1T = sb("n1", [P, T, D]), sb("n1T", [P, L])
        q2 = sb("q2", [P, T, NG, 4, HD])
        KC, VC = sb("KC", [P, T, NG, NB, HD]), sb("VC", [P, T, NG, HD, NB])
        prod = PT[:].rearrange("p a b -> p (a b)").rearrange("p (a b) -> p a b", a=T * NG)
        sc2 = sb("sc2", [P, T * NH, NB])
        ex2 = sb("ex2", [P, T * NH, NB])
        mx2, sm2 = sb("mx2", [P, T * NH]), sb("sm2", [P, T * NH])
        ao, aoT = sb("ao", [P, T * NH, HD]), sb("aoT", [P, L])

        PS = ctx.enter_context(nc.psum_tensor("PS", [P, 8, 512], F32))
        PSB = PS[:].bitcast(BF16)
        Y = PS[:, 6, 0:L].rearrange("p (t d) -> p t d", t=T)
        TR = PS[:, 7, 0:L]
        GATES = {l: PS[:, b, 0:T * E16].rearrange("p (t e) -> p t e", t=T)
                 for l, b in ((L0_FFN, 6), (L1_FFN, 4), (L2_MOE, 6), (L3_FFN, 5))}

        x_in, w_in, wb_in, st_out = sem("x_in"), {n: sem("in_" + n) for n in PACKS}, sem("in_cbf"), sem("st_out")
        consts, cbf_ready = sem("consts"), sem("cbf_ready")
        hd_stat, hd_rstd, hd_h, hd_tr, hd_hT = (sem("hd_" + n) for n in ("stat", "rstd", "h", "tr", "hT"))
        tl_stat, tl_rstd = sem("tl_stat"), sem("tl_rstd")
        y_ready, x_done = sem("y_ready"), sem("x_done")
        h1_done = sem("h1_done")
        a_w, a_soft, a_z, a_lg, a_p, a_u, a_red, a_trig, a_pp, a_ab, a_pr, a_sum, a_arg, a_yT = (
            sem("a_" + n) for n in "w soft z lg p u red trig pp ab pr sum arg yT".split())
        AT = {l: {n: sem(f"t{l}_{n}") for n in (own + " qkv split tr eva evd m st pt pv ot otr o oT oTs").split()}
              for l, own in ((L1_ATTN, "s mx mtr mev"), (L2_ATTN, "pn pg"), (L3_ATTN, "s mx mtr mev lat lats"))}
        FF = {l: {n: sem(f"f{l}_{n}") for n in ("gate ge gx g y o oc " + own).split()}
              for l, own in ((L0_FFN, "sg"), (L1_FFN, ""), (L2_MOE, "c rk"), (L3_FFN, "sg c cT"))}
        m_st, m_rs, m_n1, m_tr, m_n1T, m_qkv, m_sc, m_ex, m_ao, m_aT, m_aTs, m_y = (
            sem("m_" + n) for n in "st rs n1 tr n1T qkv sc ex ao aT aTs y".split())

        run = RUN
        order = {l: n for n, l in enumerate(run)}
        head0, k = {}, 0
        for n, l in enumerate(run):
            if n == 0 or l in (L2_MOE,) or run[n - 1] == L2_MOE:
                k += 1
            head0[l] = k - 1
            k += NB
        tail0, k = {}, 0
        for l in run:
            tail0[l] = k
            k += NB if l != L2_MIX else 0
        tails = k
        res0 = {l: NB * n for n, l in enumerate([a for a in run if a in (L0_ATTN, L1_ATTN, L2_ATTN, L3_ATTN)])}

        def own_head(l):
            n = order[l]
            return n == 0 or l == L2_MOE or run[n - 1] == L2_MOE

        block = ctx.enter_context(nc.Block())

        @block.sync
        def _(sp):
            xt = x.rearrange("b (t p) d -> p (b t) d", p=P)
            sp.dma_start(X[:], xt).then_inc(x_in, 16)
            for n in PACKS:
                sp.dma_start(W[n][:], packs[n]).then_inc(w_in[n], 16)
                if n == "const":
                    sp.dma_start(cbf_f[:, 0:PACKS_BF["cbf"].width], packs_bf["cbf"]).then_inc(wb_in, 16)
            sp.wait_ge(x_done, 1 + tails)
            sp.dma_start(out.rearrange("b (t p) d -> p (b t) d", p=P), X[:]).then_inc(st_out, 16)
            sp.wait_ge(st_out, 16)

        @block.gpsimd
        def _(pool):
            def rstd(stat, ready, count, mv, ve, rs):
                pool.wait_ge(stat, count)
                pool.tensor_tensor(ve[:], mv[:, :, 1], eps[:], ALU.add)
                pool.drain()
                pool.tensor_tensor(rs[:], ve[:], mhalf[:], ALU.pow).then_inc(ready, 1)

            def head_rstd(count):
                rstd(hd_stat, hd_rstd, count, hmv, hve, hrs)

            def tail_rstd(count):
                rstd(tl_stat, tl_rstd, count, tmv, tve, trs)

            pool.memset(mhalf[:], -0.5)
            pool.memset(eps[:], EPS)
            pool.memset(half_pi[:], float(np.pi / 2))
            pool.memset(one_c[:], 1.0)
            pool.memset(carry[:], 1.0)
            pool.memset(QS[:], 0.0)
            pool.memset(KS[:], 0.0)
            pool.memset(VA[:], 0.0)
            pool.memset(KC[:], 0.0)
            pool.memset(VC[:], 0.0)
            pool.memset(cum[:], 0.0)
            pool.drain()
            pool.memset(carry[:, :, 0:1], 0.0)
            pool.memset(KS[:, :, PARTS:PARTS + AUG], 1.0)
            pool.memset(VA[:, :, :, HD:HD + 1], 1.0)
            pool.drain().then_inc(consts, 1)

            for l in run:
                if own_head(l):
                    head_rstd(head0[l] + 1)
                if l in AT:
                    def squares(u):
                        if l == L2_ATTN:
                            for hh in range(NH):
                                pool.wait_ge(AT[l]["pt"], u * NH + (hh + 1))
                                pool.tensor_tensor(PG[:, hh % 4, 0:384], PT[:, hh % 4, 0:384],
                                                   PT[:, hh % 4, 0:384], ALU.mult).then_inc(AT[l]["pg"], 1)

                    head_rstd(head0[l] + 2)
                    with pool.Fori(0, NB - 1) as i:
                        head_rstd(i + (head0[l] + 3))
                        squares(i)
                        tail_rstd(i + (tail0[l] + 1))
                    squares(NB - 1)
                    tail_rstd(NB + tail0[l])
                    continue
                with pool.Fori(0, NB) as i:
                    head_rstd(i + (head0[l] + 2))
                    if l == L0_ATTN:
                        for c in range(CHUNKS):
                            pool.wait_ge(a_trig, i * CHUNKS + (c + 1))
                            if c == 0:
                                pool.wait_ge(a_p, i + 1)
                            for b in (cb, sbuf):
                                ins = pool.tensor_tensor(b[:, c], b[:, c],
                                                         pw[:].unsqueeze(1).to_broadcast([P, CHUNK_M, L]), ALU.mult)
                            ins.then_inc(a_pp, 1)
                    if l == L2_MIX:
                        pool.wait_ge(m_st, i + 1)
                        pool.tensor_tensor(tve[:], tmv[:, :, 1], eps[:], ALU.add)
                        pool.drain()
                        pool.tensor_tensor(trs[:], tve[:], mhalf[:], ALU.pow).then_inc(m_rs, 1)
                    if l != L2_MIX:
                        tail_rstd(i + (tail0[l] + 1))

        @block.scalar
        def _(act):
            def warm(func):
                act.activation(warm_t[:], one_c[:], func)

            def head_copy(l, count):
                act.wait_ge(hd_tr, count)
                if l == L2_MOE:
                    act.activation(hT[:], TR, ACT.Identity, scale=w("l2f", "ln2w"),
                                   bias=w("l2f", "ln2b")).then_inc(hd_hT, 1)
                else:
                    act.activation(hT[:], TR, ACT.Copy).then_inc(hd_hT, 1)

            act.wait_ge(consts, 1)
            for l in run:
                if own_head(l):
                    if l == L2_MOE:
                        act.wait_ge(w_in["l2f"], 16)
                    head_copy(l, head0[l] + 1)
                if l == L0_ATTN:
                    act.wait_ge(w_in["l0a"], 16)
                    act.activation(slope[:, 0:1], w("l0a", "slope"), ACT.Abs)
                    act.drain()
                    act.activation(slope[:, 1:2], slope[:, 0:1], ACT.Exp, scale=-1.0)
                    act.drain()
                    act.activation(slope[:, 2:3], slope[:, 1:2], ACT.Ln, bias=one_c[:], scale=1.0)
                    act.activation(slope[:, 3:4], w("l0a", "slope"), ACT.Relu)
                    act.drain().then_inc(a_soft, 1)
                    act.wait_ge(a_w, 1)
                    act.sem_inc(a_sum, CHUNKS)
                    warm(ACT.Silu)
                    with act.Fori(0, NB) as i:
                        act.wait_ge(a_z, i + 1)

                        def turns(c):
                            act.wait_ge(a_sum, i * CHUNKS + (c + 1))
                            for m in range(CHUNK_M):
                                j = c * CHUNK_M + m
                                ins = act.activation(cb[:, c, m], PS[:, 0, 0:L], ACT.Identity,
                                                     scale=theta[:, j:j + 1])
                            ins.then_inc(a_u, 1)

                        def trig(c):
                            act.wait_ge(a_red, i * CHUNKS + (c + 1))
                            act.activation(cb[:, c], sbuf[:, c], ACT.Abs)
                            act.drain()
                            act.activation(cb[:, c], cb[:, c], ACT.Sin, scale=-TWO_PI_LOW, bias=half_pi[:])
                            act.activation(sbuf[:, c], sbuf[:, c], ACT.Sin, scale=-TWO_PI_LOW).then_inc(a_trig, 1)

                        turns(0)
                        turns(1)
                        act.wait_ge(a_lg, i + 1)
                        act.activation(pw[:], la[:], ACT.Exp).then_inc(a_p, 1)
                        trig(0)
                        turns(2)
                        trig(1)
                        turns(3)
                        trig(2)
                        trig(3)
                        act.wait_ge(a_arg, i + 2)
                        act.activation(yT[:], arg[:], ACT.Silu).then_inc(a_yT, 1)
                        head_copy(l, i + (head0[l] + 2))
                elif l in AT:
                    a = AT[l]
                    width = 2 * L if l == L1_ATTN else 384
                    ntr = 3 if l == L3_ATTN else 4
                    half = NH // 4

                    def latent(u):
                        act.wait_ge(a["lat"], u + 1)
                        act.activation(latT[:], PS[0:64, 2, 0:L], ACT.Copy).then_inc(a["lats"], 1)

                    def parts_copy(u):
                        act.wait_ge(a["tr"], u * ntr + 1)
                        if l == L3_ATTN:
                            act.activation(KT[:, 0, :], PSB[:, 2, 0:L], ACT.Copy).then_inc(a["eva"], 1)
                        else:
                            act.activation(KT[:, :, 0:P], PSB[:, 2, :].rearrange("p (a b) -> p a b", b=P),
                                           ACT.Copy).then_inc(a["eva"], 1)
                        act.wait_ge(a["tr"], u * ntr + (ntr - 1))
                        act.activation(QT[:, :, 0:P], PSB[:, 0, :].rearrange("p (a b) -> p a b", b=P),
                                       ACT.Copy).then_inc(a["eva"], 1)

                    def maxima_copy(u, k):
                        act.wait_ge(a["mtr"], u * 2 + (k + 1))
                        act.activation(QT[:, k * half:(k + 1) * half, :],
                                       PSB[:, 7, :].rearrange("p (a b) -> p a b", b=L), ACT.Copy).then_inc(a["mev"], 1)

                    def outputs(u):
                        act.wait_ge(a["pv"], u * NH + (NH + 4))
                        act.activation(OT, PS[:, 4:6, :].rearrange("p a b -> p (a b)"), ACT.Copy).then_inc(a["ot"], 1)
                        act.wait_ge(a["oT"], u + 1)
                        act.activation(oT[:], PS[:, 6, L:2 * L], ACT.Copy).then_inc(a["oTs"], 1)

                    def exponentials(u, more):
                        for hh in range(NH):
                            act.wait_ge(a["st"], u * NH + (hh + 1))
                            act.wait_ge(a["pv"], u * NH + (hh + 1))
                            src, dst = PS[:, hh % 2, 0:width], PT[:, hh % 4, 0:width]
                            if l == L2_ATTN:
                                act.activation(PN[:, hh % 4, 0:width], src, ACT.Relu,
                                               scale=-0.01 * SM_SCALE).then_inc(a["pn"], 1)
                                act.activation(dst, src, ACT.Relu, scale=SM_SCALE).then_inc(a["pt"], 1)
                            else:
                                act.activation(dst, src, ACT.Exp, scale=SM_SCALE).then_inc(a["pt"], 1)
                            if hh == 2 and l == L3_ATTN and more:
                                latent(u + 1)
                            if hh == 3 and l != L2_ATTN:
                                maxima_copy(u, 1)

                    warm(ACT.Exp)
                    if l == L3_ATTN:
                        latent(0)
                    head_copy(l, head0[l] + 2)
                    parts_copy(0)
                    if l != L2_ATTN:
                        maxima_copy(0, 0)
                    with act.Fori(0, NB - 1) as i:
                        exponentials(i, True)
                        head_copy(l, i + (head0[l] + 3))
                        parts_copy(i + 1)
                        outputs(i)
                        if l != L2_ATTN:
                            maxima_copy(i + 1, 0)
                    exponentials(NB - 1, False)
                    outputs(NB - 1)
                elif l == L2_MIX:
                    act.wait_ge(w_in["l2f"], 16)
                    warm(ACT.Exp)
                    with act.Fori(0, NB) as i:
                        act.wait_ge(m_tr, i + 1)
                        act.activation(n1T[:], PS[:, 0, 0:L], ACT.Identity, scale=w("l2f", "ln1w"),
                                       bias=w("l2f", "ln1b")).then_inc(m_n1T, 1)
                        act.wait_ge(m_sc, i + 1)
                        act.activation(ex2[:], sc2[:], ACT.Exp).then_inc(m_ex, 1)
                        act.wait_ge(m_aT, i + 1)
                        act.activation(aoT[:], PS[:, 2, 0:L], ACT.Copy).then_inc(m_aTs, 1)
                        head_copy(l, i + (head0[l] + 2))
                else:
                    f, GATE = FF[l], GATES[l]
                    func = {L0_FFN: ACT.Silu, L3_FFN: ACT.Silu, L1_FFN: ACT.Gelu, L2_MOE: ACT.Gelu_apprx_tanh}[l]
                    n_chunks = {L0_FFN: 8, L1_FFN: 2, L2_MOE: 8, L3_FFN: 5}[l]
                    ne = E16 if l == L3_FFN else E8
                    if l in (L1_FFN, L3_FFN):
                        act.wait_ge(w_in["l1f" if l == L1_FFN else "l3f"], 16)
                    warm(func)
                    with act.Fori(0, NB) as i:
                        act.wait_ge(f["ge"], i + 1)
                        act.activation(ex[:, :, 0:ne], lg[:, :, 0:ne], ACT.Exp, scale=-1.0 if l == L3_FFN else 1.0).then_inc(f["gx"], 1)
                        for c in range(n_chunks):
                            cols = 2 * L if not (l == L3_FFN and c == 4) else L
                            gate = PS[:, 2 * (c % 2), 0:cols]
                            act.wait_ge(f["g"], i * n_chunks + (c + 1))
                            if l in (L0_FFN, L3_FFN):
                                act.activation(sg[:, c % 2, 0:cols], gate, func).then_inc(f["sg"], 1)
                            else:
                                act.wait_ge(f["o"], i * n_chunks + (c + 1))
                                if l == L1_FFN:
                                    for b in range(2):
                                        j = 2 * c + b
                                        ins = act.activation(y[:, c % 2, b * L:(b + 1) * L],
                                                             PS[:, 2 * (c % 2), b * L:(b + 1) * L], func,
                                                             bias=w("l1f", "b1")[:, j:j + 1])
                                else:
                                    ins = act.activation(y[:, c % 2, :], gate, func)
                                ins.then_inc(f["y"], 1)
                        head_copy(l, i + (head0[l] + 2))

        @block.tensor
        def _(pe):
            ident = w("const", "ident")
            identb = w("cbf", "ident")

            def head_transpose(l, i):
                pe.wait_ge(hd_h, i + (head0[l] + 2))
                for t in range(T):
                    ins = pe.transpose(TR[:, t * P:(t + 1) * P], h[:, t, :], ident)
                ins.then_inc(hd_tr, 1)

            pe.wait_ge(w_in["const"], 16)
            pe.wait_ge(cbf_ready, 1)
            pe.sem_inc(x_done, 1)
            for l in run:
                if own_head(l):
                    pe.wait_ge(hd_h, head0[l] + 1)
                    if head0[l]:
                        pe.wait_ge(hd_hT, head0[l])
                    for t in range(T):
                        ins = pe.transpose(TR[:, t * P:(t + 1) * P], h[:, t, :], ident)
                    ins.then_inc(hd_tr, 1)
                if order[l]:
                    pe.wait_ge(x_done, 1 + tail0[l])
                if l == L2_MOE:
                    pe.wait_ge(h1_done, NB)

                def unit_ready(i):
                    pe.wait_ge(hd_hT, i + (head0[l] + 1))

                def y_free(i):
                    pe.wait_ge(x_done, i + (tail0[l] + 1))

                if l == L0_ATTN:
                    pe.wait_ge(w_in["l0a"], 16)
                    pe.wait_ge(a_w, 1)
                    pe.sem_inc(a_pr, 2)
                    pe.sem_inc(a_arg, 1)
                    with pe.Fori(0, NB) as i:
                        unit_ready(i)
                        pe.wait_ge(a_arg, i + 1)
                        for g, wt in ((0, wkc), (1, wsc)):
                            for j in range(TAPS - 1, -1, -1):
                                back = TAPS - 1 - j
                                ins = pe.matmul(PS[:, 5 * g, g * L + back:(g + 1) * L], wt[:, j, :], hT[:, 0:L - back],
                                                start=back == 0, stop=back == TAPS - 1)
                        ins.then_inc(a_z, 1)

                        def factors(c):
                            pe.wait_ge(a_pr, i * CHUNKS + (c + 1))
                            for g, wt in ((0, wA), (1, wB)):
                                for m in range(CHUNK_M):
                                    ins = pe.matmul(PS[:, 1 + 2 * (c % 2) + g, m * L:(m + 1) * L],
                                                    wt[:, c * CHUNK_M + m, :], hT[:], start=True, stop=True)
                            ins.then_inc(a_ab, 1)

                        def sums(c):
                            pe.wait_ge(a_pr, i * CHUNKS + (c + 3))
                            for b in (cb, sbuf):
                                for m in range(CHUNK_M):
                                    first = c == 0 and m == 0 and b is cb
                                    last = c == CHUNKS - 1 and m == CHUNK_M - 1 and b is sbuf
                                    ins = pe.matmul(PS[:, 5, 0:L], ident, b[:, c, m], start=first, stop=last)
                            ins.then_inc(a_sum, 1)

                        factors(0)
                        factors(1)
                        sums(0)
                        factors(2)
                        sums(1)
                        factors(3)
                        sums(2)
                        head_transpose(l, i)
                        sums(3)
                        pe.wait_ge(a_yT, i + 1)
                        y_free(i)
                        for t in range(T):
                            ins = pe.matmul(Y[:, t, :], yT[:, t * P:(t + 1) * P], w("l0a", "wout"), start=True, stop=True)
                        ins.then_inc(y_ready, 1)
                elif l in AT:
                    a = AT[l]
                    name = {L1_ATTN: "l1a", L2_ATTN: "l2a", L3_ATTN: "l3a"}[l]
                    causal = l != L1_ATTN
                    ntr = 3 if l == L3_ATTN else 4
                    rows = PARTS if l == L2_ATTN else PARTS + AUG
                    lead = 2

                    def project(u):
                        pe.wait_ge(hd_hT, u + (head0[l] + 1))
                        if l == L3_ATTN:
                            pe.matmul(PS[0:64, 2, 0:L], w(name, "down"), hT[:], start=True, stop=True).then_inc(a["lat"], 1)
                        else:
                            for t in range(T):
                                ins = pe.matmul(PS[:, 2 + t, 0:3 * D], hT[:, t * P:(t + 1) * P], w(name, "wqkv"),
                                                start=True, stop=True)
                            ins.then_inc(a["qkv"], 1)

                    def project_up(u):
                        pe.wait_ge(a["lats"], u + 1)
                        for t in range(T):
                            ins = pe.matmul(PS[:, 2 + t, 0:D + 2 * HD], latT[:, t * P:(t + 1) * P],
                                            w(name, "up")[0:64], start=True, stop=True)
                        ins.then_inc(a["qkv"], 1)

                    def parts_transpose(u, last):
                        pe.wait_ge(a["split"], u + 1)
                        if l == L3_ATTN:
                            for t in range(T):
                                ins = pe.transpose(PSB[:, 2, t * P:(t + 1) * P],
                                                   KS[:, t * NH:t * NH + 2, :].rearrange("p a b -> p (a b)"), identb)
                            ins.then_inc(a["tr"], 1)
                        for src, bank in (((QS, 0),) if l == L3_ATTN else ((KS, 2), (QS, 0))):
                            if src is QS and last is not None:
                                pe.wait_ge(a["pt"], last * NH + NH)
                            for t in range(T):
                                for b in range(NH // 2):
                                    s = t * NH + 2 * b
                                    ins = pe.transpose(PSB[:, bank + t, b * P:(b + 1) * P],
                                                       src[:, s:s + 2, :].rearrange("p a b -> p (a b)"), identb)
                                ins.then_inc(a["tr"], 1)

                    def parts_ready(u):
                        pe.wait_ge(a["eva"], u * 2 + 2)
                        pe.wait_ge(a["evd"], u * (ntr - 2) + (ntr - 2))

                    def maxima_transpose(u, k):
                        pe.wait_ge(a["m"], u * 2 + (k + 1))
                        for b in range(NH // 4):
                            for t in range(T):
                                s = t * NH + k * (NH // 2) + 2 * b
                                ins = pe.transpose(PSB[:, 7, b * L + t * P:b * L + (t + 1) * P],
                                                   QS[:, s:s + 2, :].rearrange("p a b -> p (a b)"), identb)
                        ins.then_inc(a["mtr"], 1)

                    def scores_for_maxima(u, pair):
                        if pair >= 2:
                            pe.wait_ge(a["mx"], u * (NH // 2) + (pair - 1))
                        for hh in (2 * pair, 2 * pair + 1):
                            b = 2 * (pair % 2) + hh % 2
                            r = 64 * (hh % 2)
                            if causal:
                                pe.matmul(PS[:, b, 0:384], identb, w("cbf", "mask_q"), start=True, stop=False,
                                          skip_group_check=True)
                            for t in range(T):
                                o = slice(0, P) if causal and t == 0 else slice(P, 384) if causal else slice(t * L, (t + 1) * L)
                                ins = pe.matmul(PS[:, b, o], QT[r:r + PARTS, hh // 2, t * P:(t + 1) * P],
                                                KT[r:r + PARTS, 0 if l == L3_ATTN else hh // 2, 0:o.stop - o.start],
                                                start=not causal, stop=True, skip_group_check=causal)
                        ins.then_inc(a["s"], 1)

                    def scores(u, hh):
                        r, kh = 64 * (hh % 2), 0 if l == L3_ATTN else hh // 2
                        if hh >= 2:
                            pe.wait_ge(a["pt"], u * NH + (hh - 1))
                        b = hh % 2
                        if causal:
                            pe.matmul(PS[:, b, 0:384], identb, w("cbf", "mask_k"), start=True, stop=False,
                                      skip_group_check=True)
                            pe.matmul(PS[:, b, 0:L], KT[r:r + rows, kh, 0:P], QT[r:r + rows, hh // 2, :],
                                      start=False, stop=True, skip_group_check=True)
                            ins = pe.matmul(PS[:, b, L:384], KT[r:r + rows, kh, P:L],
                                            QT[r:r + rows, hh // 2, P:L], start=False, stop=True,
                                            skip_group_check=True)
                        else:
                            for t in range(T):
                                ins = pe.matmul(PS[:, b, t * L:(t + 1) * L], KT[r:r + rows, kh, t * P:(t + 1) * P],
                                                QT[r:r + rows, hh // 2, :], start=True, stop=True)
                        ins.then_inc(a["st"], 1)

                    def values(u, hh):
                        vh, j, g = 0 if l == L3_ATTN else hh, hh % HG, hh // HG
                        if l == L2_ATTN:
                            pe.wait_ge(a["pg"], u * NH + (hh + 1))
                            pe.wait_ge(a["m"], u * NH + (hh + 1))
                            srcs = (PG, PN)
                        else:
                            pe.wait_ge(a["pt"], u * NH + (hh + 1))
                            srcs = (PT,)
                        at = (g % 2) * L
                        for n, s in enumerate(srcs):
                            for kt in range(T):
                                q0 = P if causal and kt == 1 else 0
                                ins = pe.matmul(PS[j * VW:(j + 1) * VW, 4 + g // 2, at + q0:at + L], VA[:, kt, vh, :],
                                                s[:, hh % 4, kt * L:(kt + 1) * L - q0],
                                                start=n == 0 and kt == 0, stop=n == len(srcs) - 1 and kt == 1,
                                                tile_position=(0, j * VW), skip_group_check=True)
                        ins.then_inc(a["pv"], 1)

                    def outputs_transpose(u):
                        pe.wait_ge(a["ot"], u + 1)
                        for n in range(T * NH // HG):
                            ins = pe.transpose(PS[:, 4 + n // 4, (n % 4) * P:(n % 4 + 1) * P],
                                               OT[:, n * P:(n + 1) * P], ident)
                        ins.then_inc(a["otr"], 1)

                    def outputs_back(u):
                        pe.wait_ge(a["o"], u + 1)
                        y_free(u)
                        for t in range(T):
                            ins = pe.transpose(PS[:, 6, L + t * P:L + (t + 1) * P], osb[:, t, :], ident)
                        ins.then_inc(a["oT"], 1)

                    def project_out(u):
                        pe.wait_ge(a["oTs"], u + 1)
                        for t in range(T):
                            ins = pe.matmul(Y[:, t, :], oT[:, t * P:(t + 1) * P], w(name, "wout"), start=True, stop=True)
                        ins.then_inc(y_ready, 1)

                    def attend(u, more):
                        if l != L2_ATTN:
                            pe.wait_ge(a["mx"], (u + 1) * (NH // 2))
                            pe.wait_ge(a["mev"], u * 2 + 1)
                        for hh in range(NH + lead):
                            if hh == NH // 2 and l != L2_ATTN:
                                pe.wait_ge(a["mev"], u * 2 + 2)
                            if hh < NH:
                                scores(u, hh)
                            if hh == 1 and more:
                                project(u + 1)
                            if hh == 3 and l != L2_ATTN:
                                maxima_transpose(u, 1)
                            if hh == 5 and more and l == L3_ATTN:
                                project_up(u + 1)
                            if hh == NH - 1 and more:
                                head_transpose(l, u + 1)
                            if hh >= lead:
                                values(u, hh - lead)

                    def finish(u):
                        outputs_transpose(u)
                        outputs_back(u)
                        project_out(u)

                    pe.wait_ge(w_in[name], 16)
                    pe.sem_inc(a["pv"], 4)
                    project(0)
                    if l == L3_ATTN:
                        project_up(0)
                    head_transpose(l, 0)
                    parts_transpose(0, None)
                    parts_ready(0)
                    if l != L2_ATTN:
                        for pair in range(NH // 2):
                            scores_for_maxima(0, pair)
                        maxima_transpose(0, 0)
                    with pe.Fori(0, NB - 1) as i:
                        attend(i, True)
                        parts_transpose(i + 1, i)
                        if l == L2_ATTN:
                            finish(i)
                            parts_ready(i + 1)
                        else:
                            parts_ready(i + 1)
                            for pair in range(NH // 2):
                                scores_for_maxima(i + 1, pair)
                                if pair == 1:
                                    outputs_transpose(i)
                                if pair == 3:
                                    outputs_back(i)
                                if pair == 4:
                                    project_out(i)
                                if pair == 5:
                                    maxima_transpose(i + 1, 0)
                    attend(NB - 1, False)
                    finish(NB - 1)
                elif l == L2_MIX:
                    pe.wait_ge(w_in["l2f"], 16)
                    with pe.Fori(0, NB) as i:
                        unit_ready(i)
                        pe.wait_ge(m_n1, i + 1)
                        for t in range(T):
                            ins = pe.transpose(PS[:, 0, t * P:(t + 1) * P], n1[:, t, :], ident)
                        ins.then_inc(m_tr, 1)
                        head_transpose(l, i)
                        pe.wait_ge(m_n1T, i + 1)
                        for t in range(T):
                            ins = pe.matmul(PS[:, 1, t * 192:(t + 1) * 192], n1T[:, t * P:(t + 1) * P],
                                            w("l2f", "qkv"), start=True, stop=True)
                        ins.then_inc(m_qkv, 1)
                        pe.wait_ge(m_ao, i + 1)
                        for t in range(T):
                            ins = pe.transpose(PS[:, 2, t * P:(t + 1) * P],
                                               ao[:, t * NH:(t + 1) * NH, :].rearrange("p a b -> p (a b)"), ident)
                        ins.then_inc(m_aT, 1)
                        pe.wait_ge(m_aTs, i + 1)
                        for t in range(T):
                            ins = pe.matmul(PS[:, 3, t * P:(t + 1) * P], aoT[:, t * P:(t + 1) * P],
                                            w("l2f", "proj"), start=True, stop=True)
                        ins.then_inc(m_y, 1)
                else:
                    f, GATE = FF[l], GATES[l]
                    name = {L0_FFN: "l0f", L1_FFN: "l1f", L2_MOE: "l2f", L3_FFN: "l3f"}[l]
                    n_chunks = {L0_FFN: 8, L1_FFN: 2, L2_MOE: 8, L3_FFN: 5}[l]
                    experts = E16 if l == L3_FFN else E8
                    pe.wait_ge(w_in[name], 16)
                    pe.sem_inc(f["y"], 2)
                    pe.sem_inc(f["o"], 2)
                    pe.sem_inc(f["oc"], 2)
                    with pe.Fori(0, NB) as i:
                        unit_ready(i)
                        for t in range(T):
                            ins = pe.matmul(GATE[:, t, 0:experts], hT[:, t * P:(t + 1) * P], w(name, "router"),
                                            start=True, stop=True)
                        ins.then_inc(f["gate"], 1)
                        if l == L2_MOE:
                            pe.wait_ge(f["rk"], i + 1)
                            for t in range(T):
                                pe.matmul(GATE[:, t, 8:16], w("cbf", "before"), mbf[:, t, :], start=True, stop=False)
                                ins = pe.matmul(GATE[:, t, 8:16], w("cbf", "ones"), (cum if t == 0 else cum1)[:],
                                                start=False, stop=True)
                            ins.then_inc(f["c"], 1)

                        def up(c):
                            pe.wait_ge(f["y"], i * n_chunks + (2 if l == L3_FFN and c == 0 else c + 1))
                            if l == L0_FFN:
                                srcs = [(g, w(name, "w1")[:, ((c * 2 + g) * 2 + b) * P:((c * 2 + g) * 2 + b + 1) * P], b)
                                        for g in range(2) for b in range(2)]
                            elif l == L3_FFN and c < 4:
                                srcs = [(g, w(name, n)[:, (2 * c + b) * P:(2 * c + b + 1) * P], b)
                                        for g, n in ((0, "w1"), (1, "w3")) for b in range(2)]
                            elif l == L3_FFN:
                                srcs = [(0, w(name, "w1s"), 0), (1, w(name, "w3s"), 0)]
                            else:
                                srcs = [(0, w(name, "w1")[:, (2 * c + b) * P:(2 * c + b + 1) * P], b) for b in range(2)]
                            for g, wt, b in srcs:
                                ins = pe.matmul(PS[:, 2 * (c % 2) + g, b * L:(b + 1) * L], wt, hT[:], start=True, stop=True)
                            ins.then_inc(f["g"], 1)

                        def share(c):
                            if c == 0:
                                pe.wait_ge(f["c"], i + 1)
                            for b in range(2):
                                for t in range(T):
                                    e = 2 * (2 * c + b)
                                    ins = pe.transpose(
                                        PS[:, 4 + c % 2, b * L + t * P:b * L + (t + 1) * P],
                                        cwx[:, t, e:e + 2, :].rearrange("p e f -> p (e f)"), ident)
                            ins.then_inc(f["cT"], 1)

                        def down(c):
                            pe.wait_ge(f["y"], i * n_chunks + (c + 3))
                            if l in (L0_FFN, L2_MOE):
                                pe.wait_ge(f["oc"], i * n_chunks + (c + 1))
                                for t in range(T):
                                    for b in range(2):
                                        ins = pe.matmul(
                                            PS[:, 4 + c % 2, t * P:(t + 1) * P],
                                            y[:, c % 2, b * L + t * P:b * L + (t + 1) * P],
                                            w(name, "w2")[:, (2 * c + b) * D:(2 * c + b + 1) * D],
                                            start=b == 0, stop=b == 1)
                            else:
                                if c == 0:
                                    y_free(i)
                                nb = 1 if l == L3_FFN and c == 4 else 2
                                for b in range(nb):
                                    for t in range(T):
                                        w2 = (w(name, "w2s") if nb == 1 else
                                              w(name, "w2")[:, (2 * c + b) * D:(2 * c + b + 1) * D])
                                        ins = pe.matmul(Y[:, t, :], y[:, c % 2, b * L + t * P:b * L + (t + 1) * P], w2,
                                                        start=c == 0 and b == 0 and t == 0,
                                                        stop=c == n_chunks - 1 and b == nb - 1,
                                                        skip_group_check=True)
                            ins.then_inc(f["o"], 1)

                        for c in range(n_chunks + 1):
                            if c < n_chunks:
                                up(c)
                            if l == L3_FFN and 1 <= c <= 4:
                                share(c - 1)
                            if c == n_chunks - 1:
                                head_transpose(l, i)
                            if c >= 1:
                                down(c - 1)

        @block.vector
        def _(dve):
            def head_stats(src, u):
                for t in range(T):
                    dve.bn_stats(hst[:, t, :], src[:, bass.ds(u * T + t, 1), :].rearrange("p a b -> p (a b)"))
                dve.drain()
                for t in range(T):
                    ins = dve.bn_aggr(hmv[:, t, :], hst[:, t, :])
                ins.then_inc(hd_stat, 1)

            def head_norm(src, u, count):
                dve.wait_ge(hd_tr, count - 1)
                dve.wait_ge(hd_rstd, count)
                for t in range(T):
                    ins = dve.tensor_scalar(h[:, t, :], src[:, bass.ds(u * T + t, 1), :].rearrange("p a b -> p (a b)"),
                                            hmv[:, t, 0:1], hrs[:, t:t + 1], ALU.subtract, ALU.mult)
                ins.then_inc(hd_h, 1)

            def tail_stats(src):
                for t in range(T):
                    dve.bn_stats(tst[:, t, :], src[:, t, :])
                dve.drain()
                for t in range(T):
                    ins = dve.bn_aggr(tmv[:, t, :], tst[:, t, :])
                ins.then_inc(tl_stat, 1)

            def tail_add(l, i, src):
                dve.wait_ge(tl_rstd, i + (tail0[l] + 1))
                for t in range(T):
                    dve.tensor_scalar(tn[:, t, :], src[:, t, :], tmv[:, t, 0:1], trs[:, t:t + 1],
                                      ALU.subtract, ALU.mult)
                dve.drain()
                dve.tensor_tensor(X[:, bass.ds(i * T, T), :], X[:, bass.ds(i * T, T), :], tn[:], ALU.add)\
                   .then_inc(x_done, 1)
                dve.drain()

            def tail(l, i, src):
                tail_stats(src)
                tail_add(l, i, src)

            def top(p, n, k, weighted, scratch_rank, lower):
                gt = gtb[:, :, 0:n * n].rearrange("p t (j i) -> p t j i", i=n)
                eq = eqb[:, :, 0:n * n].rearrange("p t (j i) -> p t j i", i=n)
                other = p.unsqueeze(2).to_broadcast([P, T, n, n])
                own = p.unsqueeze(3).to_broadcast([P, T, n, n])
                dve.tensor_tensor(gt, other, own, ALU.is_gt)
                dve.tensor_tensor(eq, other, own, ALU.is_equal)
                dve.drain()
                dve.tensor_tensor(eq, eq, lower.rearrange("p (a j i) -> p a j i", a=1, i=n).to_broadcast([P, T, n, n]),
                                  ALU.mult)
                dve.drain()
                dve.tensor_tensor(gt, gt, eq, ALU.add)
                dve.drain()
                dve.tensor_reduce(scratch_rank, gt, AX.X, ALU.add)
                dve.drain()
                if weighted is not None:
                    dve.scalar_tensor_tensor(weighted, scratch_rank, float(k), p, ALU.is_lt, ALU.mult)
                    dve.drain()

            dve.wait_ge(x_in, 16)
            dve.wait_ge(consts, 1)
            dve.wait_ge(w_in["const"], 16)
            dve.wait_ge(wb_in, 16)
            dve.tensor_copy(W["cbf"][:], cbf_f[:, 0:PACKS_BF["cbf"].width]).then_inc(cbf_ready, 1)
            for l in run:
                src_h = H1 if l == L2_MOE else X
                if own_head(l):
                    head_stats(src_h, 0)
                    dve.wait_ge(hd_rstd, head0[l] + 1)
                    if head0[l]:
                        dve.wait_ge(hd_tr, head0[l])
                    for t in range(T):
                        ins = dve.tensor_scalar(h[:, t, :], src_h[:, t, :], hmv[:, t, 0:1], hrs[:, t:t + 1],
                                                ALU.subtract, ALU.mult)
                    ins.then_inc(hd_h, 1)
                    dve.drain()

                if l == L0_ATTN:
                    dve.wait_ge(w_in["l0a"], 16)
                    for dst, wt, cv in ((wkc, "wk", "conv_k"), (wsc, "ws", "conv_s")):
                        dve.tensor_tensor(dst[:], w("l0a", wt).unsqueeze(1).to_broadcast([P, TAPS, D]),
                                          w("l0a", cv).rearrange("p (j d) -> p j d", j=TAPS), ALU.mult)
                    dve.tensor_tensor(coef[:, 0, :], w("l0a", "norm_re"), w("l0a", "diag_re"), ALU.mult)
                    dve.tensor_tensor(coef[:, 1, :], w("l0a", "norm_im"), w("l0a", "diag_im"), ALU.mult)
                    dve.drain()
                    dve.tensor_tensor(wab[:, 0, :], w("l0a", "wq_re"), coef[:, 0, :], ALU.mult)
                    dve.tensor_tensor(wab[:, 1, :], w("l0a", "wq_im"), coef[:, 0, :], ALU.mult)
                    dve.tensor_tensor(wtmp[:, 0, :], w("l0a", "wq_im"), coef[:, 1, :], ALU.mult)
                    dve.tensor_tensor(wtmp[:, 1, :], w("l0a", "wq_re"), coef[:, 1, :], ALU.mult)
                    dve.drain()
                    dve.tensor_tensor(wab[:, 0, :], wab[:, 0, :], wtmp[:, 0, :], ALU.subtract)
                    dve.tensor_tensor(wab[:, 1, :], wab[:, 1, :], wtmp[:, 1, :], ALU.add)
                    dve.drain()
                    rep = KCH // KQ
                    for g, dst in ((0, wA), (1, wB)):
                        for m in range(NM):
                            dve.tensor_copy(
                                dst[:, m, :].rearrange("p (q r h) -> p q r h", q=KQ, r=rep),
                                wab[:, g, :].rearrange("p (q a h m) -> p q a h m", q=KQ, a=1, h=HC)[:, :, :, :, m]
                                .to_broadcast([P, KQ, rep, HC]))
                    dve.tensor_scalar(theta[:], w("l0a", "theta"), float(1.0 / (2 * np.pi)), None, ALU.mult)
                    dve.wait_ge(a_soft, 1)
                    dve.tensor_tensor(slope[:, 0:1], slope[:, 2:3], slope[:, 3:4], ALU.add)
                    dve.drain()
                    dve.tensor_scalar(logw[:], w("const", "decay_pos"), slope[:, 0:1], None, ALU.mult)
                    dve.drain().then_inc(a_w, 1)
                    with dve.Fori(0, NB) as i:
                        nxt = (i + 1) % NB
                        head_stats(X, nxt)
                        dve.wait_ge(a_z, i + 1)
                        dve.tensor_scalar(la[:], PS[:, 5, L:2 * L], w("l0a", "score"), 20.0, ALU.mult, ALU.min)
                        dve.drain()
                        dve.scalar_tensor_tensor(la[:], la[:], -20.0, logw[:], ALU.max, ALU.add).then_inc(a_lg, 1)

                        def reduce_turns(c):
                            dve.wait_ge(a_u, i * CHUNKS + (c + 1))
                            dve.tensor_scalar(sbuf[:, c], cb[:, c], MAGIC, None, ALU.add)
                            dve.drain()
                            dve.scalar_tensor_tensor(sbuf[:, c], sbuf[:, c], MAGIC, cb[:, c],
                                                     ALU.subtract, ALU.subtract).then_inc(a_red, 1)

                        def cumulate(c):
                            dve.wait_ge(a_pp, i * CHUNKS + (c + 1))
                            cf = carry[:].rearrange("p m t -> p (m t)")
                            for b in (cb, sbuf):
                                flat = b[:, c].rearrange("p m t -> p (m t)")
                                dve.tensor_tensor_scan(flat, cf, flat, 0.0, ALU.mult, ALU.add)
                            dve.drain()
                            dve.wait_ge(a_ab, i * CHUNKS + (c + 1))
                            for g, b in ((0, cb), (1, sbuf)):
                                flat = b[:, c].rearrange("p m t -> p (m t)")
                                ins = dve.tensor_tensor(flat, flat, PS[:, 1 + 2 * (c % 2) + g, :], ALU.mult)
                            ins.then_inc(a_pr, 1)

                        reduce_turns(0)
                        reduce_turns(1)
                        dve.wait_ge(a_p, i + 1)
                        dve.tensor_tensor_scan(den[:], one_c[:].to_broadcast([P, L]), pw[:], 0.0, ALU.mult, ALU.add)
                        dve.drain()
                        dve.tensor_scalar(den[:], den[:], 1e-4, None, ALU.max)
                        dve.drain()
                        dve.reciprocal(inv[:], den[:])
                        reduce_turns(2)
                        cumulate(0)
                        reduce_turns(3)
                        head_norm(X, nxt, i + (head0[l] + 2))
                        cumulate(1)
                        cumulate(2)
                        cumulate(3)
                        dve.wait_ge(a_sum, i * CHUNKS + 2 * CHUNKS)
                        dve.tensor_tensor(arg[:], inv[:], PS[:, 5, 0:L], ALU.mult).then_inc(a_arg, 1)
                        dve.wait_ge(y_ready, i + (res0[l] + 1))
                        tail(l, i, Y)
                elif l in AT:
                    a = AT[l]
                    name = {L1_ATTN: "l1a", L2_ATTN: "l2a", L3_ATTN: "l3a"}[l]
                    ntr = 3 if l == L3_ATTN else 4
                    nk = 1 if l == L3_ATTN else NH
                    nm = 2 if l == L1_ATTN else 3
                    result = acc if l == L1_ATTN else Y
                    QSv = QS[:].rearrange("p n (s d) -> p n s d", d=HD)
                    KSv = KS[:].rearrange("p n (s d) -> p n s d", d=HD)
                    kn = slice(0, T * NH, NH) if nk == 1 else slice(0, T * NH)

                    def load_qkv(u, last):
                        dve.wait_ge(a["qkv"], u + 1)
                        at = 0
                        for dst, width in ((qf, D), (kf, nk * HD), (vf, nk * HD)):
                            src = PS[:, 2:4, at:at + width]
                            dstv = dst[:].rearrange("p n d -> p (n d)")[:, 0:T * width].rearrange("p (t f) -> p t f", t=T)
                            if l == L1_ATTN:
                                dve.tensor_tensor(dstv, src, w(name, "bqkv")[:, at:at + width].unsqueeze(1)
                                                  .to_broadcast([P, T, width]), ALU.add)
                            else:
                                dve.tensor_copy(dstv, src)
                            at += width
                        dve.drain()
                        if last is not None and l != L2_ATTN:
                            dve.wait_ge(a["mtr"], last * 2 + 2)

                    def split(part):
                        for cur, dst, slots in ((qf[:], QSv, ((0, 7, 3), (1, 6, 3), (2, 6, 3))),
                                                (kf[:, 0:T * nk], KSv[:, kn], ((0, 3, 1), (3, 6, 1), (6, 7, 1)))):
                            s0, s1, st = slots[part]
                            n, cnt = cur.shape[1], len(range(s0, s1, st))
                            dve.tensor_copy(dst[:, :, s0:s1:st, :], cur.unsqueeze(2).to_broadcast([P, n, cnt, HD]))
                        dve.drain()
                        if part < 2:
                            for cur, dst, s0 in ((qf[:], QSv, part), (kf[:, 0:T * nk], KSv[:, kn], 3 * part)):
                                dve.tensor_tensor(cur, cur, dst[:, :, s0, :], ALU.subtract)
                            dve.drain()
                        elif l == L3_ATTN:
                            dve.tensor_copy(KS[:, 1:T * NH:NH, 0:PARTS], KS[:, 0:T * NH:NH, 0:PARTS])
                            dve.drain().then_inc(a["split"], 1)
                        else:
                            dve.drain().then_inc(a["split"], 1)

                    def load_values():
                        dve.tensor_scalar(VA[:, :, 0:nk, 0:HD],
                                          vf[:, 0:T * nk].rearrange("p (t a) d -> p t a d", t=T),
                                          1e-3 if l == L2_ATTN else 1.0, None, ALU.mult)

                    def parts_copy(u, last):
                        if last is not None:
                            dve.wait_ge(a["st"], last * NH + NH)
                        if l != L3_ATTN:
                            dve.wait_ge(a["tr"], u * ntr + 2)
                            dve.tensor_copy(KT[:, :, P:L], PSB[:, 3, :].rearrange("p (a b) -> p a b", b=P))\
                               .then_inc(a["evd"], 1)
                        dve.wait_ge(a["tr"], u * ntr + ntr)
                        dve.tensor_copy(QT[:, :, P:L], PSB[:, 1, :].rearrange("p (a b) -> p a b", b=P))\
                           .then_inc(a["evd"], 1)

                    def maximum(u, pair):
                        dve.wait_ge(a["s"], u * (NH // 2) + (pair + 1))
                        b = 2 * (pair % 2)
                        keys = L if l == L1_ATTN else P
                        dve.tensor_reduce(mx[:, 2 * pair:2 * pair + 2, 0:nm],
                                          PS[:, b:b + 2, 0:nm * keys].rearrange("p a (t k) -> p a t k", t=nm),
                                          AX.X, ALU.max).then_inc(a["mx"], 1)

                    def maximum_parts(k):
                        hs = slice(k * NH // 2, (k + 1) * NH // 2)
                        dve.drain()
                        dve.tensor_scalar(mx[:, hs, 0:nm], mx[:, hs, 0:nm], -1.0, None, ALU.mult)
                        dve.drain()
                        if nm == 3:
                            dve.tensor_tensor(mx[:, hs, 1], mx[:, hs, 1], mx[:, hs, 2], ALU.min)
                            dve.drain()
                        m = mx[:, hs, 0:T].rearrange("p a t -> p t a")
                        QM = QS[:].rearrange("p (t a) c -> p t a c", t=T)[:, :, hs]
                        for part in range(AUG):
                            dve.tensor_copy(QM[:, :, :, PARTS + part], m)
                            dve.drain()
                            if part < AUG - 1:
                                dve.tensor_tensor(m, m, QM[:, :, :, PARTS + part], ALU.subtract)
                                dve.drain()
                        dve.drain().then_inc(a["m"], 1)

                    def normalise(u):
                        dve.wait_ge(a["otr"], u + 1)
                        O = PS[:, 4:6, :].rearrange("p b (g t j r) -> p t (b g) j r", g=2, t=T, j=HG)
                        ov = osb[:].rearrange("p t (g j d) -> p t g j d", g=NH // HG, j=HG)
                        if l == L2_ATTN:
                            for t in range(T):
                                ins = dve.tensor_copy(ov[:, t], O[:, t, :, :, 0:HD])
                        else:
                            rv = rsum[:].rearrange("p t (g j) -> p t g j", j=HG)
                            for t in range(T):
                                dve.reciprocal(rv[:, t], O[:, t, :, :, HD])
                            dve.drain()
                            for t in range(T):
                                ins = dve.tensor_tensor(ov[:, t], O[:, t, :, :, 0:HD],
                                                        rv[:, t].unsqueeze(3).to_broadcast([P, NH // HG, HG, HD]),
                                                        ALU.mult)
                        ins.then_inc(a["o"], 1)

                    def result_stats(u):
                        dve.wait_ge(y_ready, u + (res0[l] + 1))
                        if l == L1_ATTN:
                            dve.tensor_tensor(acc[:], Y, w(name, "bout").unsqueeze(1).to_broadcast([P, T, D]), ALU.add)
                            dve.drain()
                        tail_stats(result)

                    def linear(u, hh):
                        s = hh % 4
                        dve.wait_ge(a["pn"], u * NH + (hh + 1))
                        dve.tensor_scalar(lin1[:, hh % 2, :], PN[:, s, 0:384], 1.0, None, ALU.add)
                        dve.drain()
                        dve.scalar_tensor_tensor(PN[:, s, 0:384], PN[:, s, 0:384], 1.0, lin1[:, hh % 2, :],
                                                 ALU.is_le, ALU.mult).then_inc(a["m"], 1)

                    dve.wait_ge(w_in[name], 16)
                    head_stats(X, 1)
                    load_qkv(0, None)
                    for part in range(3):
                        split(part)
                    load_values()
                    head_norm(X, 1, head0[l] + 2)
                    parts_copy(0, None)
                    if l != L2_ATTN:
                        for pair in range(NH // 2):
                            maximum(0, pair)
                            if pair == 3:
                                maximum_parts(0)
                        maximum_parts(1)
                    with dve.Fori(0, NB - 1) as i:
                        nxt = (i + 2) % NB
                        head_stats(X, nxt)
                        if l == L2_ATTN:
                            for hh in range(NH):
                                linear(i, hh)
                                if hh == 2:
                                    load_qkv(i + 1, i)
                                if hh in (4, 6, 8):
                                    split((hh - 4) // 2)
                                if hh == 10:
                                    head_norm(X, nxt, i + (head0[l] + 3))
                            parts_copy(i + 1, i)
                            normalise(i)
                            load_values()
                            result_stats(i)
                        else:
                            load_qkv(i + 1, i)
                            for part in range(3):
                                split(part)
                            head_norm(X, nxt, i + (head0[l] + 3))
                            parts_copy(i + 1, i)
                            for pair in range(NH // 2):
                                maximum(i + 1, pair)
                                if pair == 1:
                                    normalise(i)
                                    load_values()
                                if pair == 3:
                                    maximum_parts(0)
                                if pair == 5:
                                    result_stats(i)
                            maximum_parts(1)
                        tail_add(l, i, result)
                    if l == L2_ATTN:
                        for hh in range(NH):
                            linear(NB - 1, hh)
                    normalise(NB - 1)
                    result_stats(NB - 1)
                    tail_add(l, NB - 1, result)
                elif l == L2_MIX:
                    with dve.Fori(0, NB) as i:
                        nxt = (i + 1) % NB
                        for t in range(T):
                            dve.bn_stats(tst[:, t, :], h[:, t, :])
                        dve.drain()
                        for t in range(T):
                            ins = dve.bn_aggr(tmv[:, t, :], tst[:, t, :])
                        ins.then_inc(m_st, 1)
                        dve.tensor_copy(H1[:, bass.ds(i * T, T), :], h[:])
                        head_stats(X, nxt)
                        dve.wait_ge(m_rs, i + 1)
                        for t in range(T):
                            ins = dve.tensor_scalar(n1[:, t, :], h[:, t, :], tmv[:, t, 0:1], trs[:, t:t + 1],
                                                    ALU.subtract, ALU.mult)
                        ins.then_inc(m_n1, 1)
                        dve.drain()
                        head_norm(X, nxt, i + (head0[l] + 2))
                        dve.wait_ge(m_qkv, i + 1)
                        src = PS[:, 1, 0:T * 192].rearrange("p (t g c) -> p t g c", t=T, g=NG)
                        dve.tensor_copy(q2[:].rearrange("p t g q d -> p t g (q d)"), src[:, :, :, 0:32])
                        for t in range(T):
                            dve.tensor_copy(KC[:, t, :, bass.ds(i, 1), :].rearrange("p g a d -> p g (a d)"),
                                            src[:, t, :, 32:40])
                            dve.tensor_copy(VC[:, t, :, :, bass.ds(i, 1)].rearrange("p g d a -> p g (d a)"),
                                            src[:, t, :, 40:48])
                        dve.drain()
                        for t in range(T):
                            for g in range(NG):
                                dve.tensor_tensor(
                                    prod[:, t * NG + g, :].rearrange("p (q s d) -> p q s d", q=4, s=NB),
                                    q2[:, t, g].unsqueeze(2).to_broadcast([P, 4, NB, HD]),
                                    KC[:, t, g].unsqueeze(1).to_broadcast([P, 4, NB, HD]), ALU.mult)
                        dve.drain()
                        dve.tensor_reduce(sc2[:].rearrange("p a s -> p (a s)"),
                                          prod.rearrange("p a (b d) -> p (a b) d", d=HD), AX.X, ALU.add)
                        dve.drain()
                        crow = w("const", "causal8").rearrange("p (a b) -> p a b", b=NB)
                        dve.tensor_scalar(sc2[:], sc2[:], SM_SCALE, None, ALU.mult)
                        dve.drain()
                        dve.tensor_tensor(sc2[:], sc2[:], crow[:, bass.ds(i, 1), :].to_broadcast([P, T * NH, NB]),
                                          ALU.add)
                        dve.drain()
                        dve.tensor_reduce(mx2[:], sc2[:], AX.X, ALU.max)
                        dve.drain()
                        dve.tensor_tensor(sc2[:], sc2[:], mx2[:].unsqueeze(2).to_broadcast([P, T * NH, NB]),
                                          ALU.subtract).then_inc(m_sc, 1)
                        dve.wait_ge(m_ex, i + 1)
                        dve.tensor_reduce(sm2[:], ex2[:], AX.X, ALU.add)
                        for t in range(T):
                            for g in range(NG):
                                a = (t * NG + g) * 4
                                dve.tensor_tensor(
                                    prod[:, t * NG + g, :].rearrange("p (q d s) -> p q d s", q=4, s=NB),
                                    ex2[:, a:a + 4, :].unsqueeze(2).to_broadcast([P, 4, HD, NB]),
                                    VC[:, t, g].unsqueeze(1).to_broadcast([P, 4, HD, NB]), ALU.mult)
                        dve.drain()
                        dve.tensor_reduce(ao[:].rearrange("p a d -> p (a d)"),
                                          prod.rearrange("p a (b s) -> p (a b) s", s=NB), AX.X, ALU.add)
                        dve.reciprocal(sm2[:], sm2[:])
                        dve.drain()
                        dve.tensor_tensor(ao[:], ao[:], sm2[:].unsqueeze(2).to_broadcast([P, T * NH, HD]),
                                          ALU.mult).then_inc(m_ao, 1)
                        dve.wait_ge(m_y, i + 1)
                        dve.tensor_tensor(H1[:, bass.ds(i * T, T), :], H1[:, bass.ds(i * T, T), :],
                                          PS[:, 3, 0:L].rearrange("p (t d) -> p t d", t=T), ALU.add).then_inc(h1_done, 1)
                        dve.drain()
                else:
                    f, GATE = FF[l], GATES[l]
                    n_chunks = {L0_FFN: 8, L1_FFN: 2, L2_MOE: 8, L3_FFN: 5}[l]
                    ne = E16 if l == L3_FFN else E8
                    with dve.Fori(0, NB) as i:
                        nxt = (i + 1) % NB
                        head_stats(src_h, nxt)
                        dve.wait_ge(f["gate"], i + 1)
                        if l == L3_FFN:
                            dve.tensor_scalar(lg[:], GATE, -80.0, None, ALU.max).then_inc(f["ge"], 1)
                            dve.wait_ge(f["gx"], i + 1)
                            dve.tensor_scalar(ex[:], ex[:], 1.0, None, ALU.add)
                            dve.drain()
                            dve.reciprocal(ex[:], ex[:])
                            dve.drain()
                            v = ex[:].rearrange("p t (g c) -> p (t g) c", c=4)
                            dve.tensor_tensor(hilo[:, 0], v[:, :, 0:2], v[:, :, 2:4], ALU.max)
                            dve.tensor_tensor(hilo[:, 1], v[:, :, 0:2], v[:, :, 2:4], ALU.min)
                            dve.drain()
                            dve.tensor_tensor(hilo[:, 2, :, 0], hilo[:, 0, :, 0], hilo[:, 0, :, 1], ALU.max)
                            dve.tensor_tensor(hilo[:, 2, :, 1], hilo[:, 0, :, 0], hilo[:, 0, :, 1], ALU.min)
                            dve.tensor_tensor(hilo[:, 3, :, 0], hilo[:, 1, :, 0], hilo[:, 1, :, 1], ALU.max)
                            dve.drain()
                            dve.tensor_tensor(hilo[:, 3, :, 1], hilo[:, 2, :, 1], hilo[:, 3, :, 0], ALU.max)
                            dve.drain()
                            dve.tensor_tensor(gsc[:].rearrange("p t g -> p (t g)"), hilo[:, 2, :, 0],
                                              hilo[:, 3, :, 1], ALU.add)
                            dve.drain()
                            top(gsc[:], NG, 2, None, gal[:], w("const", "rank4"))
                            dve.tensor_scalar(gal[:], gal[:], 2.0, None, ALU.is_lt)
                            dve.drain()
                            dve.tensor_scalar(gsc[:], gal[:], -1.0, None, ALU.add)
                            ga = gal[:].unsqueeze(3).to_broadcast([P, T, NG, 4])
                            gb = gsc[:].unsqueeze(3).to_broadcast([P, T, NG, 4])
                            m4 = msk[:].rearrange("p t (g c) -> p t g c", c=4)
                            dve.tensor_tensor(m4, ex[:].rearrange("p t (g c) -> p t g c", c=4), ga, ALU.mult)
                            dve.drain()
                            dve.tensor_tensor(m4, m4, gb, ALU.add)
                            dve.drain()
                            top(msk[:], E16, 4, msk[:], rank[:], w("const", "rank16"))
                            dve.tensor_reduce(gsm[:], msk[:], AX.X, ALU.add)
                            dve.drain()
                            dve.tensor_scalar(gsm[:], gsm[:], 1e-6, None, ALU.add)
                            dve.drain()
                            dve.reciprocal(gsm[:], gsm[:])
                            dve.drain()
                            dve.tensor_tensor(cw[:], msk[:], gsm[:].unsqueeze(2).to_broadcast([P, T, E16]),
                                              ALU.mult)
                            dve.drain()
                            for t in range(T):
                                ins = dve.tensor_copy(cwx[:, t, :, :], cw[:, t].unsqueeze(2).to_broadcast([P, E16, F16]))
                            ins.then_inc(f["c"], 1)
                        else:
                            g8, e8 = GATE[:, :, 0:E8], ex[:, :, 0:E8]
                            dve.tensor_reduce(gmx[:], g8, AX.X, ALU.max)
                            dve.drain()
                            dve.tensor_tensor(lg[:, :, 0:E8], g8, gmx[:].unsqueeze(2).to_broadcast([P, T, E8]),
                                              ALU.subtract).then_inc(f["ge"], 1)
                            dve.wait_ge(f["gx"], i + 1)
                            dve.tensor_reduce(gsm[:], e8, AX.X, ALU.add)
                            dve.drain()
                            dve.reciprocal(gsm[:], gsm[:])
                            dve.drain()
                            dve.tensor_tensor(cw[:, :, 0:E8], e8, gsm[:].unsqueeze(2).to_broadcast([P, T, E8]), ALU.mult)
                            dve.drain()
                            if l != L1_FFN:
                                top(cw[:, :, 0:E8], E8, 2, cw[:, :, 0:E8], rank[:, :, 0:E8], w("const", "rank8"))
                            if l == L2_MOE:
                                dve.tensor_reduce(gsm[:], cw[:, :, 0:E8], AX.X, ALU.add)
                                dve.tensor_scalar(mbf[:], rank[:, :, 0:E8], 2.0, None, ALU.is_lt)
                                dve.drain()
                                dve.tensor_tensor(cum1[:], cum[:], mbf[:, 0, :], ALU.add)
                                dve.reciprocal(gsm[:], gsm[:])
                                dve.drain().then_inc(f["rk"], 1)
                                dve.tensor_tensor(cw[:, :, 0:E8], cw[:, :, 0:E8],
                                                  gsm[:].unsqueeze(2).to_broadcast([P, T, E8]), ALU.mult)
                                dve.drain()
                                dve.wait_ge(f["c"], i + 1)
                                dve.scalar_tensor_tensor(cw[:, :, 0:E8], GATE[:, :, 8:16], float(CAP),
                                                         cw[:, :, 0:E8], ALU.is_lt, ALU.mult)
                                dve.tensor_tensor(cum[:], cum1[:], mbf[:, 1, :], ALU.add)
                                dve.drain()
                        if l in (L1_FFN,):
                            head_norm(src_h, nxt, i + (head0[l] + 2))

                        def combine(c):
                            dve.wait_ge(f["o"], i * n_chunks + (c + 3))
                            for t in range(T):
                                src = PS[:, 4 + c % 2, t * P:(t + 1) * P]
                                if c == 0:
                                    ins = dve.tensor_scalar(acc[:, t, :], src, cw[:, t, 0:1], None, ALU.mult)
                                else:
                                    ins = dve.scalar_tensor_tensor(acc[:, t, :], src, cw[:, t, c:c + 1], acc[:, t, :],
                                                                   ALU.mult, ALU.add)
                            ins.then_inc(f["oc"], 1)

                        if l in (L0_FFN, L3_FFN):
                            for c in range(n_chunks):
                                cols = 2 * L if not (l == L3_FFN and c == 4) else L
                                dve.wait_ge(f["sg"], i * n_chunks + (c + 1))
                                dve.wait_ge(f["o"], i * n_chunks + (2 if l == L3_FFN and c == 0 else c + 1))
                                ins = dve.tensor_tensor(y[:, c % 2, 0:cols], sg[:, c % 2, 0:cols],
                                                        PS[:, 2 * (c % 2) + 1, 0:cols], ALU.mult)
                                if l == L3_FFN and c < 4:
                                    dve.drain()
                                    dve.wait_ge(f["cT"], i * 4 + (c + 1))
                                    dve.tensor_tensor(y[:, c % 2, :], y[:, c % 2, :], PS[:, 4 + c % 2, :], ALU.mult)\
                                       .then_inc(f["y"], 1)
                                else:
                                    ins.then_inc(f["y"], 1)
                                if c == 1:
                                    head_norm(src_h, nxt, i + (head0[l] + 2))
                                if l == L0_FFN and c >= 1:
                                    combine(c - 1)
                                    dve.drain()
                            if l == L0_FFN:
                                combine(n_chunks - 1)
                                dve.drain()
                        elif l == L2_MOE:
                            for c in range(n_chunks):
                                if c == 2:
                                    head_norm(src_h, nxt, i + (head0[l] + 2))
                                combine(c)
                                dve.drain()
                            dve.tensor_tensor(acc[:], acc[:], H1[:, bass.ds(i * T, T), :], ALU.add)
                            dve.drain()
                        if l in (L0_FFN, L2_MOE):
                            tail(l, i, acc)
                        else:
                            dve.wait_ge(f["o"], i * n_chunks + (n_chunks + 2))
                            if l == L1_FFN:
                                dve.tensor_tensor(acc[:], Y, w("l1f", "b2").unsqueeze(1).to_broadcast([P, T, D]), ALU.add)
                                dve.drain()
                                for t in range(T):
                                    dve.tensor_scalar(acc[:, t, :], acc[:, t, :], cw[:, t, 7:8], None, ALU.mult)
                                dve.drain()
                                tail(l, i, acc)
                            else:
                                tail(l, i, Y)


def _pack(fields, parts):
    out = []
    for name, width in fields.at.items():
        a = np.asarray(parts[name])
        a = a.reshape(1 if a.size == width[1] else a.shape[0], width[1])
        if a.shape[0] == 1:
            a = np.broadcast_to(a, (P, width[1]))
        if a.shape[0] < P:
            a = np.concatenate([a, np.zeros((P - a.shape[0], width[1]), a.dtype)])
        out.append(a)
    return np.ascontiguousarray(np.concatenate(out, axis=1), dtype=np.float32)


def _constants():
    r = np.arange(P)
    t = np.arange(L)
    lower = lambda n: (np.arange(n)[None, :] < np.arange(n)[:, None]).astype(np.float32).reshape(1, -1)
    pos = np.where((np.repeat(np.arange(KCH), HC) < KCH - HC)[:, None], -(L - 1 - t)[None, :], -t[None, :])
    causal8 = np.where(np.arange(NB)[None, :] > np.arange(NB)[:, None], NEG, 0.0).reshape(1, -1)
    const = _pack(PACKS["const"], dict(ident=np.eye(P), rank8=lower(E8), rank16=lower(E16), rank4=lower(NG),
                                       causal8=causal8, decay_pos=pos))
    later = np.where(r[None, :] > r[:, None], NEG, 0.0)
    mask_q = np.concatenate([later, np.zeros((P, P)), later], axis=1)
    mask_k = np.concatenate([np.where(r[:, None] > t[None, :], NEG, 0.0),
                             np.where(r[:, None] > r[None, :], NEG, 0.0)], axis=1)
    cbf = _pack(PACKS_BF["cbf"], dict(ident=np.eye(P), mask_q=mask_q, mask_k=mask_k,
                                      before=(r[:, None] < r[None, :]).astype(np.float32), ones=np.ones((P, P))))
    return const, cbf


def kernel(**inputs):
    import concourse.bacc as _bacc
    from concourse.bass_utils import run_bass_kernel_spmd as _run

    v = {k: np.asarray(a) for k, a in inputs.items()}
    W_in = v["L0_attn_W_in"]
    wq = W_in[:, D + KCH:].reshape(D, KQ, HC, NM, 2)
    conv = v["L0_attn_conv_k"][:, 0, :]
    over_q = lambda a: np.broadcast_to(a.reshape(1, 1, HC, 1), (1, KQ, HC, NM)).reshape(1, -1)
    norm = v["L0_attn_norm_scale"]
    heads = lambda a: np.ascontiguousarray(a.reshape(NH, 3, HD, -1).transpose(1, 0, 2, 3)).reshape(3 * D, -1)
    halves = lambda a: a.reshape(-1, 2, P, D).transpose(2, 0, 1, 3).reshape(P, -1)
    const, cbf = _constants()
    arrays = {
        "x": np.ascontiguousarray(v["L0_attn_x"]), "const": const, "cbf": cbf,
        "l0a": _pack(PACKS["l0a"], dict(
            wk=W_in[:, :D], ws=np.repeat(W_in[:, D:D + KCH], HC, axis=1), wq_re=wq[..., 0], wq_im=wq[..., 1],
            wout=v["L0_attn_W_out"], conv_k=conv[:, :D].reshape(1, -1),
            conv_s=np.repeat(conv[:, D:], HC, axis=1).reshape(1, -1), norm_re=over_q(norm[:HC]),
            norm_im=over_q(norm[HC:]), diag_re=over_q(np.diagonal(v["L0_attn_W_re"])),
            diag_im=over_q(np.diagonal(v["L0_attn_W_im"])), theta=v["L0_attn_theta"].reshape(P, NM),
            slope=np.repeat(np.concatenate([v["L0_attn_decay_slopes"], v["L0_attn_anchor_slopes"]]), HC)[:, None],
            score=np.repeat(v["L0_attn_score_scale"], HC)[:, None])),
        "l0f": _pack(PACKS["l0f"], dict(
            router=v["L0_ffn_router_w"].T, w1=v["L0_ffn_w1"].transpose(2, 0, 1),
            w2=halves(v["L0_ffn_w2"].transpose(0, 2, 1)))),
        "l1a": _pack(PACKS["l1a"], dict(
            wqkv=heads(v["L1_attn_Wqkv"]).T, bqkv=heads(v["L1_attn_bqkv"]).reshape(1, -1), wout=v["L1_attn_Wout"].T,
            bout=v["L1_attn_bout"].reshape(1, -1))),
        "l1f": _pack(PACKS["l1f"], dict(
            router=v["L1_ffn_Wr"].T, w1=v["L1_ffn_W1"][E8 - 1], b1=v["L1_ffn_b1"][E8 - 1].reshape(4, P).T,
            w2=v["L1_ffn_W2"][E8 - 1].reshape(4, P, D).transpose(1, 0, 2), b2=v["L1_ffn_b2"][E8 - 1].reshape(1, -1))),
        "l2a": _pack(PACKS["l2a"], dict(wqkv=v["L2_attn_W_attn"], wout=v["L2_attn_W_proj"])),
        "l2f": _pack(PACKS["l2f"], dict(
            ln1w=v["L2_ffn_ln1_weight"][:, None], ln1b=v["L2_ffn_ln1_bias"][:, None],
            ln2w=v["L2_ffn_ln2_weight"][:, None], ln2b=v["L2_ffn_ln2_bias"][:, None], qkv=v["L2_ffn_qkv_weight"].T,
            proj=v["L2_ffn_proj_weight"].T, router=v["L2_ffn_router_weight"],
            w1=v["L2_ffn_moe_w1"].transpose(1, 0, 2), w2=halves(v["L2_ffn_moe_w2"]))),
        "l3a": _pack(PACKS["l3a"], dict(
            down=v["L3_attn_Wc_down"], up=np.concatenate([v["L3_attn_Wq_up"], v["L3_attn_Wkv_up"]], axis=1),
            wout=v["L3_attn_Wc_proj"])),
        "l3f": _pack(PACKS["l3f"], dict(
            router=v["L3_ffn_w_gate"].T, w1=v["L3_ffn_w1_e"].transpose(2, 0, 1), w3=v["L3_ffn_w3_e"].transpose(2, 0, 1),
            w2=v["L3_ffn_w2_e"].transpose(0, 2, 1).reshape(8, P, D).transpose(1, 0, 2), w1s=v["L3_ffn_w1_s"].T,
            w3s=v["L3_ffn_w3_s"].T, w2s=v["L3_ffn_w2_s"].T)),
    }
    nc = _bacc.Bacc("TRN2", target_bir_lowering=False, num_devices=1)
    aps = {n: nc.dram_tensor("in_" + n, a.shape, F32, kind="ExternalInput").ap()
           for n, a in arrays.items()}
    out = nc.dram_tensor("result", (NB, L, D), F32, kind="ExternalOutput").ap()
    block_program(nc, aps["x"], {n: aps[n] for n in PACKS}, {"cbf": aps["cbf"]}, out)
    r = _run(nc, [{"in_" + n: a for n, a in arrays.items()}], core_ids=[0])
    return r.results[0]["result"]
```

```python
from contextlib import ExitStack

import numpy as np

import concourse.bass as bass
from concourse import mybir

ALU = mybir.AluOpType
ACT = mybir.ActivationFunctionType
AX = mybir.AxisListType
F32 = mybir.dt.float32
BF16 = mybir.dt.bfloat16

POOL_GROUPS = 3
P = 128
NB, L = 8, 256
T = L // P
D = 128
EPS = 1e-5

(L0_ATTN, L0_FFN, L1_ATTN, L1_FFN, L2_ATTN, L2_FFN, L3_ATTN, L3_FFN) = range(8)
RUN = tuple(range(8))

KCH, HC, NM = 32, 4, 8
KQ = 4
TAPS = 4
CHUNK_M = 2
CHUNKS = NM // CHUNK_M
MAGIC = float(1.5 * 2 ** 23)
TWO_PI_LOW = 6.283185

NH, HD = 16, 8
SM_SCALE = 1.0 / float(np.sqrt(np.float32(HD)))
PARTS = 7 * HD
AUG = 3
SLOT = 64
VW = 32
HG = P // VW
NEG = -1e30

E8, F8 = 8, 256
FD1 = 512
E16, F16 = 16, 64
NSH = 128
CAP = 640
NG = 4


class Pack:

    def __init__(self, fields):
        self.at, n = {}, 0
        for name, width in fields:
            self.at[name] = (n, width)
            n += width
        self.width = n


PACKS = {
    "const": Pack([("ident", P), ("rank8", 64), ("rank16", 256), ("rank4", 16), ("causal8", 64), ("decay_pos", L)]),
    "l0a": Pack([("wk", D), ("ws", D), ("wq_re", P), ("wq_im", P), ("wout", D), ("conv_k", TAPS * D),
                 ("conv_s", TAPS * D), ("norm_re", P), ("norm_im", P), ("diag_re", P), ("diag_im", P),
                 ("theta", NM), ("slope", 1), ("score", 1)]),
    "l0f": Pack([("router", E8), ("w1", E8 * 2 * F8), ("w2", E8 * 2 * D)]),
    "l1a": Pack([("wqkv", 3 * D), ("bqkv", 3 * D), ("wout", D), ("bout", D)]),
    "l1f": Pack([("router", E8), ("w1", FD1), ("b1", 4), ("w2", 4 * D), ("b2", D)]),
    "l2a": Pack([("wqkv", 3 * D), ("wout", D)]),
    "l2f": Pack([("ln1w", 1), ("ln1b", 1), ("ln2w", 1), ("ln2b", 1), ("qkv", 192), ("proj", D),
                 ("router", E8), ("w1", E8 * F8), ("w2", E8 * 2 * D)]),
    "l3a": Pack([("down", 64), ("up", D + 2 * HD), ("wout", D)]),
    "l3f": Pack([("router", E16), ("w1", E16 * F16), ("w3", E16 * F16), ("w2", 8 * D), ("w1s", NSH),
                 ("w3s", NSH), ("w2s", D)]),
}
PACKS_BF = {"cbf": Pack([("ident", P), ("mask_q", 384), ("mask_k", 384), ("before", P), ("ones", P)])}


def block_program(nc, x, packs, packs_bf, out):
    ctx = ExitStack()
    with ctx:
        def sb(name, shape, dt=F32):
            return ctx.enter_context(nc.sbuf_tensor(name, shape, dt))

        def sem(name):
            return ctx.enter_context(nc.semaphore(name))

        W = {n: sb("w_" + n, [P, pk.width]) for n, pk in PACKS.items()}
        W["cbf"] = sb("w_cbf", [P, PACKS_BF["cbf"].width], BF16)

        def w(pack, name):
            a, n = (PACKS.get(pack) or PACKS_BF[pack]).at[name]
            return W[pack][:, a:a + n]

        X = sb("X", [P, NB * T, D])
        H1 = sb("H1", [P, NB * T, D])
        h = sb("h", [P, T, D])
        hT = sb("hT", [P, L])
        hN = sb("hN", [P, L])
        hst, hmv, hve, hrs = (sb("hst", [P, T, 6]), sb("hmv", [P, T, 2]), sb("hve", [P, T]), sb("hrs", [P, T]))
        tst, tmv, tve, trs = (sb("tst", [P, T, 6]), sb("tmv", [P, T, 2]), sb("tve", [P, T]), sb("trs", [P, T]))
        tn = sb("tn", [P, T, D])
        mhalf = sb("mhalf", [P, T])
        eps = sb("eps", [P, T])
        warm_t = sb("warm_t", [P, 1])
        half_pi = sb("half_pi", [P, 1])
        one_c = sb("one_c", [P, 1])
        hundredth = sb("hundredth", [P, 1])
        wkc, wsc = sb("wkc", [P, TAPS, D]), sb("wsc", [P, TAPS, D])
        wab = sb("wab", [P, 2, P])
        wtmp = sb("wtmp", [P, 2, P])
        coef = sb("coef", [P, 2, P])
        wA, wB = sb("wA", [P, NM, D]), sb("wB", [P, NM, D])
        slope = sb("slope", [P, 4])
        logw = sb("logw", [P, L])
        theta = sb("theta", [P, NM])
        carry = sb("carry", [P, CHUNK_M, L])
        la, pw, den = sb("la", [P, L]), sb("pw", [P, L]), sb("den", [P, L])
        inv, arg, yT = sb("inv", [P, L]), sb("arg", [P, L]), sb("yT", [P, L])
        cb = sb("cb", [P, CHUNKS, CHUNK_M, L])
        sbuf = sb("sbuf", [P, CHUNKS, CHUNK_M, L])
        qf, kf, vf = (sb("qf", [P, T * NH, HD]), sb("kf", [P, T * NH, HD]), sb("vf", [P, T * NH, HD]))
        QS, KS = sb("QS", [P, T * NH, SLOT], BF16), sb("KS", [P, T * NH, SLOT], BF16)
        QT, KT = sb("QT", [P, NH // 2, L], BF16), sb("KT", [P, NH // 2, L], BF16)
        VA = sb("VA", [P, T, NH, VW])
        mx = sb("mx", [P, NH, 3])
        PT = sb("PT", [P, 4, 2 * L])
        PG = cb[:].rearrange("p c m t -> p c (m t)")
        PN = sbuf[:].rearrange("p c m t -> p c (m t)")
        rsum = sb("rsum", [P, T, NH])
        osb = sb("osb", [P, T, D])
        oT = sb("oT", [P, L])
        latT = sb("latT", [64, L])
        cbf_f = PT[:].rearrange("p a b -> p (a b)")
        cwx = PT[:].rearrange("p a b -> p (a b)").rearrange("p (t e f) -> p t e f", t=T, e=E16)
        sg, y = sb("sg", [P, 2, 2 * L]), sb("y", [P, 2, 2 * L])
        OT = sg[:].rearrange("p a b -> p (a b)")
        acc = sb("acc", [P, T, D])
        lg, ex = sb("lg", [P, T, E16]), sb("ex", [P, T, E16])
        gmx, gsm = sb("gmx", [P, T]), sb("gsm", [P, T])
        gtb, eqb = sb("gtb", [P, T, E16 * E16]), sb("eqb", [P, T, E16 * E16])
        rank = sb("rank", [P, T, E16])
        cw, cwn = sb("cw", [P, T, E16]), sb("cwn", [P, T, E16])
        hilo = sb("hilo", [P, 4, T * NG, 2])
        gsc, gal = sb("gsc", [P, T, NG]), sb("gal", [P, T, NG])
        msk = sb("msk", [P, T, E16])
        mbf, cum = sb("mbf", [P, T, E8], BF16), sb("cum", [P, E8], BF16)
        cum1 = sb("cum1", [P, E8], BF16)
        xst, xmv, xve, xrs = (sb("xst", [P, T, 6]), sb("xmv", [P, T, 2]), sb("xve", [P, T]), sb("xrs", [P, T]))
        nst, nmv, nve, nrs = (sb("nst", [P, T, 6]), sb("nmv", [P, T, 2]), sb("nve", [P, T]), sb("nrs", [P, T]))
        n1, n1T = sb("n1", [P, T, D]), sb("n1T", [P, L])
        q2 = sb("q2", [P, T, NG, 4, HD])
        KC, VC = sb("KC", [P, T, NG, NB, HD]), sb("VC", [P, T, NG, HD, NB])
        prod = PT[:].rearrange("p a b -> p (a b)").rearrange("p (a b) -> p a b", a=T * NG)
        sc2 = sb("sc2", [P, T * NH, NB])
        ex2 = sb("ex2", [P, T * NH, NB])
        mx2, sm2 = sb("mx2", [P, T * NH]), sb("sm2", [P, T * NH])
        ao, aoT = sb("ao", [P, T * NH, HD]), sb("aoT", [P, L])

        PS = ctx.enter_context(nc.psum_tensor("PS", [P, 8, 512], F32))
        PSB = PS[:].bitcast(BF16)
        Y = PS[:, 6, 0:L].rearrange("p (t d) -> p t d", t=T)
        TR = PS[:, 7, 0:L]
        GATES = {l: PS[:, b, o:o + T * E16].rearrange("p (t e) -> p t e", t=T)
                 for l, b, o in ((L0_FFN, 6, 0), (L1_FFN, 4, 0), (L2_FFN, 6, 0), (L3_FFN, 7, L))}
        HEAD_AT = {L0_FFN: 2, L1_FFN: 1, L3_FFN: 1}
        ROUTE_AT = {L0_FFN: 3, L1_FFN: 2, L3_FFN: 1}
        EXP_AT = {L0_FFN: 4, L1_FFN: 1, L3_FFN: 1}

        x_rest = sem("x_rest")
        x_in, w_in, wb_in, st_out = sem("x_in"), {n: sem("in_" + n) for n in PACKS}, sem("in_cbf"), sem("st_out")
        consts, cbf_ready = sem("consts"), sem("cbf_ready")
        hd_stat, hd_rstd, hd_h, hd_tr, hd_hT = (sem("hd_" + n) for n in ("stat", "rstd", "h", "tr", "hT"))
        tl_stat, tl_rstd = sem("tl_stat"), sem("tl_rstd")
        y_ready, x_done = sem("y_ready"), sem("x_done")
        a_w, a_soft, a_z, a_lg, a_p, a_u, a_red, a_trig, a_pp, a_ab, a_pr, a_sum, a_arg, a_yT = (
            sem("a_" + n) for n in "w soft z lg p u red trig pp ab pr sum arg yT".split())
        AT = {l: {n: sem(f"t{l}_{n}") for n in (own + " qkv split tr eva evd m st pt pv ot otr o oT oTs").split()}
              for l, own in ((L1_ATTN, "s mx mtr mev"), (L2_ATTN, "pn pg"), (L3_ATTN, "s mx mtr mev lat lats"))}
        FF = {l: {n: sem(f"f{l}_{n}") for n in ("gate ge gx g y o oc " + own).split()}
              for l, own in ((L0_FFN, "hn sg"), (L1_FFN, "hn"), (L2_FFN, "c rk"), (L3_FFN, "hn sg cn c cT"))}
        m_ld, m_kp, m_vp = sem("m_ld"), sem("m_kp"), sem("m_vp")
        m_xst, m_xrs, m_st, m_rs, m_n1, m_tr, m_n1T, m_qkv, m_sc, m_ex, m_ao, m_aT, m_aTs, m_y = (
            sem("m_" + n) for n in "xst xrs st rs n1 tr n1T qkv sc ex ao aT aTs y".split())

        run = RUN
        order = {l: n for n, l in enumerate(run)}
        head0, k = {}, 0
        for n, l in enumerate(run):
            if n == 0 or run[n - 1] == L2_FFN:
                k += 1
            head0[l] = k - 1
            k += NB
        tail0, k = {}, 0
        for l in run:
            tail0[l] = k
            k += NB
        tails = k
        res0 = {l: NB * n for n, l in enumerate([a for a in run if a in (L0_ATTN, L1_ATTN, L2_ATTN, L3_ATTN)])}

        EARLY = {L1_ATTN: 6, L2_ATTN: 2, L3_ATTN: 4}
        PAIRS, MAX_STEPS = NH // 4, NH // 4 + NH // 2

        def own_head(l):
            n = order[l]
            return n == 0 or run[n - 1] == L2_FFN

        def key_products(engine, n):
            t, g = n // NG, n % NG
            return engine.tensor_tensor(prod[:, n, :].rearrange("p (q s d) -> p q s d", q=4, s=NB),
                                        q2[:, t, g].unsqueeze(2).to_broadcast([P, 4, NB, HD]),
                                        KC[:, t, g].unsqueeze(1).to_broadcast([P, 4, NB, HD]), ALU.mult)

        def value_products(engine, n):
            t, g = n // NG, n % NG
            return engine.tensor_tensor(prod[:, n, :].rearrange("p (q d s) -> p q d s", q=4, s=NB),
                                        ex2[:, 4 * n:4 * n + 4, :].unsqueeze(2).to_broadcast([P, 4, HD, NB]),
                                        VC[:, t, g].unsqueeze(1).to_broadcast([P, 4, HD, NB]), ALU.mult)

        block = ctx.enter_context(nc.Block())

        @block.sync
        def _(sp):
            xt = x.rearrange("b (t p) d -> p (b t) d", p=P)
            first = 2 * T
            sp.dma_start(X[:, 0:first, :], xt[:, 0:first, :]).then_inc(x_in, 16)
            for n in PACKS:
                sp.dma_start(W[n][:], packs[n]).then_inc(w_in[n], 16)
                if n == "l0a":
                    sp.dma_start(X[:, first:, :], xt[:, first:, :]).then_inc(x_rest, 16)
                    sp.dma_start(cbf_f[:, 0:PACKS_BF["cbf"].width], packs_bf["cbf"]).then_inc(wb_in, 16)
            yt = out.rearrange("b (t p) d -> p (b t) d", p=P)
            early_tiles = (NB - 1) * T
            sp.wait_ge(x_done, tails)
            sp.dma_start(yt[:, 0:early_tiles, :], X[:, 0:early_tiles, :]).then_inc(st_out, 16)
            sp.wait_ge(x_done, 1 + tails)
            sp.dma_start(yt[:, early_tiles:, :], X[:, early_tiles:, :]).then_inc(st_out, 16)
            sp.wait_ge(st_out, 32)

        @block.gpsimd
        def _(pool):
            def rstd(stat, ready, count, mv, ve, rs):
                pool.wait_ge(stat, count)
                pool.tensor_tensor(ve[:], mv[:, :, 1], eps[:], ALU.add)
                pool.drain()
                pool.tensor_tensor(rs[:], ve[:], mhalf[:], ALU.pow).then_inc(ready, 1)

            def head_rstd(count):
                rstd(hd_stat, hd_rstd, count, hmv, hve, hrs)

            def tail_rstd(count):
                rstd(tl_stat, tl_rstd, count, tmv, tve, trs)

            pool.memset(mhalf[:], -0.5)
            pool.memset(eps[:], EPS)
            pool.memset(half_pi[:], float(np.pi / 2))
            pool.memset(one_c[:], 1.0)
            pool.memset(hundredth[:], 0.01)
            pool.memset(carry[:], 1.0)
            pool.memset(QS[:], 0.0)
            pool.memset(KS[:], 0.0)
            pool.memset(VA[:], 0.0)
            pool.memset(KC[:], 0.0)
            pool.memset(VC[:], 0.0)
            pool.memset(cum[:], 0.0)
            pool.drain()
            pool.memset(carry[:, :, 0:1], 0.0)
            pool.memset(KS[:, :, PARTS:PARTS + AUG], 1.0)
            pool.memset(VA[:, :, :, HD:HD + 1], 1.0)
            pool.drain().then_inc(consts, 1)

            for l in run:
                if own_head(l):
                    head_rstd(head0[l] + 1)
                if l in AT:
                    def squares(u):
                        if l == L2_ATTN:
                            for n, hh in enumerate(range(3, NH, 4)):
                                pool.wait_ge(AT[l]["pt"], u * NH + (hh + 1))
                                pool.tensor_tensor(PG[:, 3, 0:384], PT[:, 3, 0:384],
                                                   hundredth[:].to_broadcast([P, 384]), ALU.add)
                                pool.drain()
                                pool.tensor_tensor(PG[:, 3, 0:384], PG[:, 3, 0:384],
                                                   PT[:, 3, 0:384], ALU.mult).then_inc(AT[l]["pg"], 1)

                    head_rstd(head0[l] + 2)
                    with pool.Fori(0, NB - 1) as i:
                        head_rstd(i + (head0[l] + 3))
                        squares(i)
                        tail_rstd(i + (tail0[l] + 1))
                    squares(NB - 1)
                    tail_rstd(NB + tail0[l])
                    continue
                if l == L2_FFN:
                    def inner_rstd(u):
                        rstd(m_st, m_rs, u + 1, nmv, nve, nrs)

                    def products(u):
                        mine = range(T * NG - POOL_GROUPS, T * NG)
                        pool.wait_ge(m_ld, u + 1)
                        for n in mine:
                            ins = key_products(pool, n)
                        ins.then_inc(m_kp, 1)
                        pool.wait_ge(m_ex, u + 1)
                        for n in mine:
                            ins = value_products(pool, n)
                        ins.then_inc(m_vp, 1)

                    inner_rstd(0)
                    rstd(m_xst, m_xrs, 1, xmv, xve, xrs)
                    inner_rstd(1)
                    products(0)
                    head_rstd(head0[l] + 2)
                    with pool.Fori(0, NB - 1) as i:
                        rstd(m_xst, m_xrs, i + 2, xmv, xve, xrs)
                        products(i + 1)
                        inner_rstd(i + 2)
                        head_rstd(i + (head0[l] + 3))
                        tail_rstd(i + (tail0[l] + 1))
                    tail_rstd(NB + tail0[l])
                    continue
                if l in FF:
                    head_rstd(head0[l] + 2)
                    with pool.Fori(0, NB - 1) as i:
                        tail_rstd(i + (tail0[l] + 1))
                        head_rstd(i + (head0[l] + 3))
                    tail_rstd(NB + tail0[l])
                    continue
                with pool.Fori(0, NB) as i:
                    if l == L0_ATTN:
                        for c in range(CHUNKS):
                            pool.wait_ge(a_trig, i * CHUNKS + (c + 1))
                            if c == 0:
                                pool.wait_ge(a_p, i + 1)
                            for b in (cb, sbuf):
                                ins = pool.tensor_tensor(b[:, c], b[:, c],
                                                         pw[:].unsqueeze(1).to_broadcast([P, CHUNK_M, L]), ALU.mult)
                            ins.then_inc(a_pp, 1)
                            if c == 1:
                                head_rstd(i + (head0[l] + 2))
                    tail_rstd(i + (tail0[l] + 1))

        @block.scalar
        def _(act):
            def warm(func):
                act.drain()
                act.activation(warm_t[:], one_c[:], func)

            def head_copy(l, count, plain=False):
                act.wait_ge(hd_tr, count)
                if l == L2_FFN and not plain:
                    act.activation(hT[:], TR, ACT.Identity, scale=w("l2f", "ln2w"),
                                   bias=w("l2f", "ln2b")).then_inc(hd_hT, 1)
                else:
                    act.activation(hT[:], TR, ACT.Copy).then_inc(hd_hT, 1)

            act.wait_ge(consts, 1)
            for l in run:
                if own_head(l):
                    head_copy(l, head0[l] + 1, plain=True)
                if l == L0_ATTN:
                    act.wait_ge(w_in["l0a"], 16)
                    act.activation(slope[:, 0:1], w("l0a", "slope"), ACT.Abs)
                    act.drain()
                    act.activation(slope[:, 1:2], slope[:, 0:1], ACT.Exp, scale=-1.0)
                    act.drain()
                    act.activation(slope[:, 2:3], slope[:, 1:2], ACT.Ln, bias=one_c[:], scale=1.0)
                    act.activation(slope[:, 3:4], w("l0a", "slope"), ACT.Relu)
                    act.drain().then_inc(a_soft, 1)
                    act.wait_ge(a_w, 1)
                    act.sem_inc(a_sum, CHUNKS)
                    warm(ACT.Silu)

                    def turns(u, c):
                        act.wait_ge(a_sum, u * CHUNKS + (c + 1))
                        for m in range(CHUNK_M):
                            j = c * CHUNK_M + m
                            ins = act.activation(cb[:, c, m], PS[:, 0, 0:L], ACT.Identity, scale=theta[:, j:j + 1])
                        ins.then_inc(a_u, 1)

                    def trig(u, c):
                        act.wait_ge(a_red, u * CHUNKS + (c + 1))
                        act.activation(cb[:, c], sbuf[:, c], ACT.Abs)
                        act.drain()
                        act.activation(cb[:, c], cb[:, c], ACT.Sin, scale=-TWO_PI_LOW, bias=half_pi[:])
                        act.activation(sbuf[:, c], sbuf[:, c], ACT.Sin, scale=-TWO_PI_LOW).then_inc(a_trig, 1)

                    def first_turns(u):
                        act.wait_ge(a_z, u + 1)
                        turns(u, 0)
                        turns(u, 1)

                    def weights(u):
                        act.wait_ge(a_lg, u + 1)
                        act.activation(pw[:], la[:], ACT.Exp).then_inc(a_p, 1)

                    def unit(i, more):
                        trig(i, 0)
                        turns(i, 2)
                        trig(i, 1)
                        turns(i, 3)
                        trig(i, 2)
                        trig(i, 3)
                        head_copy(l, i + (head0[l] + 2))
                        if more:
                            first_turns(i + 1)
                        act.wait_ge(a_arg, i + 1)
                        act.activation(yT[:], arg[:], ACT.Silu).then_inc(a_yT, 1)
                        if more:
                            act.wait_ge(a_pp, i * CHUNKS + CHUNKS)
                            weights(i + 1)
                            warm(ACT.Silu)

                    first_turns(0)
                    weights(0)
                    warm(ACT.Silu)
                    with act.Fori(0, NB - 1) as i:
                        unit(i, True)
                    unit(NB - 1, False)
                elif l in AT:
                    a = AT[l]
                    width = 2 * L if l == L1_ATTN else 384
                    ntr = 3 if l == L3_ATTN else 4
                    early = EARLY[l]
                    half = NH // 4

                    def latent(u):
                        act.wait_ge(a["lat"], u + 1)
                        act.activation(latT[:], PS[0:64, 2, 0:L], ACT.Copy).then_inc(a["lats"], 1)

                    def parts_copy(u):
                        act.wait_ge(a["tr"], u * ntr + 1)
                        if l == L3_ATTN:
                            act.activation(KT[:, 0, :], PSB[:, 2, 0:L], ACT.Copy).then_inc(a["eva"], 1)
                        else:
                            act.activation(KT[:, :, 0:P], PSB[:, 2, :].rearrange("p (a b) -> p a b", b=P),
                                           ACT.Copy).then_inc(a["eva"], 1)
                        act.wait_ge(a["tr"], u * ntr + (ntr - 1))
                        act.activation(QT[:, :, 0:P], PSB[:, 0, :].rearrange("p (a b) -> p a b", b=P),
                                       ACT.Copy).then_inc(a["eva"], 1)

                    def maxima_copy(u, k):
                        act.wait_ge(a["mtr"], u * 2 + (k + 1))
                        act.activation(QT[:, k * half:(k + 1) * half, :],
                                       PSB[:, 7, :].rearrange("p (a b) -> p a b", b=L), ACT.Copy).then_inc(a["mev"], 1)

                    def outputs(u):
                        act.wait_ge(a["pv"], u * NH + (NH + 4))
                        act.activation(OT, PS[:, 4:6, :].rearrange("p a b -> p (a b)"), ACT.Copy).then_inc(a["ot"], 1)

                    def outputs_copy(u):
                        act.wait_ge(a["oT"], u + 1)
                        act.activation(oT[:], PS[:, 6, L:2 * L], ACT.Copy).then_inc(a["oTs"], 1)

                    def weigh(u, hh):
                        act.wait_ge(a["st"], u * NH + (hh + 1))
                        act.wait_ge(a["pv"], u * NH + (hh + 1))
                        src, dst = PS[:, hh % 2, 0:width], PT[:, hh % 4, 0:width]
                        if l == L2_ATTN:
                            act.activation(PN[:, hh % 4, 0:width], src, ACT.Identity, scale=-0.01 * SM_SCALE,
                                           bias=one_c[:]).then_inc(a["pn"], 1)
                            act.activation(dst, src, ACT.Relu, scale=SM_SCALE).then_inc(a["pt"], 1)
                        else:
                            act.activation(dst, src, ACT.Exp, scale=SM_SCALE).then_inc(a["pt"], 1)

                    def weigh_all(u, more):
                        if l == L3_ATTN and more:
                            latent(u + 1)
                        for hh in range(early, NH):
                            weigh(u, hh)
                            if hh == early and l != L2_ATTN:
                                maxima_copy(u, 1)

                    warm(ACT.Exp)
                    if l == L3_ATTN:
                        latent(0)
                    head_copy(l, head0[l] + 2)
                    parts_copy(0)
                    if l != L2_ATTN:
                        maxima_copy(0, 0)
                    for hh in range(early):
                        weigh(0, hh)
                    with act.Fori(0, NB - 1) as i:
                        weigh_all(i, True)
                        head_copy(l, i + (head0[l] + 3))
                        parts_copy(i + 1)
                        outputs(i)
                        if l != L2_ATTN:
                            outputs_copy(i)
                            maxima_copy(i + 1, 0)
                        for hh in range(early):
                            weigh(i + 1, hh)
                        if l == L2_ATTN:
                            outputs_copy(i)
                    weigh_all(NB - 1, False)
                    outputs(NB - 1)
                    outputs_copy(NB - 1)
                elif l == L2_FFN:
                    f = FF[l]
                    act.wait_ge(w_in["l2f"], 16)

                    def inner_copy(u):
                        act.wait_ge(m_tr, u + 1)
                        act.activation(n1T[:], PS[:, 1, 0:L], ACT.Identity, scale=w("l2f", "ln1w"),
                                       bias=w("l2f", "ln1b")).then_inc(m_n1T, 1)

                    def short_exp(u):
                        act.wait_ge(m_sc, u + 1)
                        act.activation(ex2[:], sc2[:], ACT.Exp).then_inc(m_ex, 1)

                    def short_copy(u):
                        act.wait_ge(m_aT, u + 1)
                        act.activation(aoT[:], PS[:, 1, 0:L], ACT.Copy).then_inc(m_aTs, 1)

                    def gate_exp(u):
                        act.wait_ge(f["ge"], u + 1)
                        act.activation(ex[:, :, 0:E8], lg[:, :, 0:E8], ACT.Exp).then_inc(f["gx"], 1)

                    def hidden(u, c):
                        act.wait_ge(f["g"], u * E8 + (c + 1))
                        act.wait_ge(f["o"], u * E8 + (c + 1))
                        act.activation(y[:, c % 2, :], PS[:, 2 * (c % 2), :], ACT.Gelu_apprx_tanh).then_inc(f["y"], 1)

                    inner_copy(0)
                    short_exp(0)
                    short_copy(0)
                    head_copy(l, head0[l] + 2)
                    inner_copy(1)
                    gate_exp(0)
                    warm(ACT.Gelu_apprx_tanh)
                    with act.Fori(0, NB - 1) as i:
                        for c in range(E8):
                            hidden(i, c)
                            if c == 3:
                                short_exp(i + 1)
                            if c == 5:
                                short_copy(i + 1)
                        head_copy(l, i + (head0[l] + 3))
                        inner_copy(i + 2)
                        gate_exp(i + 1)
                    for c in range(E8):
                        hidden(NB - 1, c)
                else:
                    f, GATE = FF[l], GATES[l]
                    func = {L0_FFN: ACT.Silu, L3_FFN: ACT.Silu, L1_FFN: ACT.Gelu}[l]
                    n_chunks = {L0_FFN: 8, L1_FFN: 2, L3_FFN: 5}[l]
                    ne = E16 if l == L3_FFN else E8
                    if l in (L1_FFN, L3_FFN):
                        act.wait_ge(w_in["l1f" if l == L1_FFN else "l3f"], 16)

                    def gate_exp(u):
                        act.wait_ge(f["ge"], u + 1)
                        act.activation(ex[:, :, 0:ne], lg[:, :, 0:ne], ACT.Exp,
                                       scale=-1.0 if l == L3_FFN else 1.0).then_inc(f["gx"], 1)

                    gate_exp(0)
                    warm(func)
                    with act.Fori(0, NB) as i:
                        for c in range(n_chunks):
                            cols = L if l == L3_FFN and c == 0 else 2 * L
                            gate = PS[:, 2 * (c % 2), 0:cols]
                            act.wait_ge(f["g"], i * n_chunks + (c + 1))
                            if l in (L0_FFN, L3_FFN):
                                act.activation(sg[:, c % 2, 0:cols], gate, func).then_inc(f["sg"], 1)
                            else:
                                act.wait_ge(f["o"], i * n_chunks + (c + 1))
                                for b in range(2):
                                    j = 2 * c + b
                                    ins = act.activation(y[:, c % 2, b * L:(b + 1) * L],
                                                         PS[:, 2 * (c % 2), b * L:(b + 1) * L], func,
                                                         bias=w("l1f", "b1")[:, j:j + 1])
                                ins.then_inc(f["y"], 1)
                            if l == L3_FFN and c == 0:
                                act.wait_ge(f["cn"], i + 1)
                                for t in range(T):
                                    ins = act.activation(cwx[:, t, :, :],
                                                         cwn[:, t].unsqueeze(2).to_broadcast([P, E16, F16]), ACT.Copy)
                                ins.then_inc(f["c"], 1)
                            if c == HEAD_AT[l]:
                                act.wait_ge(hd_tr, i + (head0[l] + 2))
                                act.activation(hN[:], TR, ACT.Copy).then_inc(f["hn"], 1)
                                if l == L1_FFN:
                                    act.drain()
                                    act.activation(hT[:], hN[:], ACT.Copy).then_inc(hd_hT, 1)
                            if c == EXP_AT[l]:
                                gate_exp(i + 1)
                        if l != L1_FFN:
                            act.activation(hT[:], hN[:], ACT.Copy).then_inc(hd_hT, 1)

        @block.tensor
        def _(pe):
            ident = w("const", "ident")
            identb = w("cbf", "ident")

            def head_transpose(l, i):
                pe.wait_ge(hd_h, i + (head0[l] + 2))
                for t in range(T):
                    ins = pe.transpose(TR[:, t * P:(t + 1) * P], h[:, t, :], ident)
                ins.then_inc(hd_tr, 1)

            pe.wait_ge(w_in["const"], 16)
            pe.sem_inc(x_done, 1)
            for l in run:
                if own_head(l):
                    pe.wait_ge(hd_h, head0[l] + 1)
                    if head0[l]:
                        pe.wait_ge(hd_hT, head0[l])
                    for t in range(T):
                        ins = pe.transpose(TR[:, t * P:(t + 1) * P], h[:, t, :], ident)
                    ins.then_inc(hd_tr, 1)
                if order[l] == 0 and l in AT or order[l] == 1:
                    pe.wait_ge(cbf_ready, 1)
                if order[l]:
                    pe.wait_ge(x_done, 1 + tail0[l])

                def unit_ready(i):
                    pe.wait_ge(hd_hT, i + (head0[l] + 1))

                def y_free(i):
                    pe.wait_ge(x_done, i + (tail0[l] + 1))

                if l == L0_ATTN:
                    pe.wait_ge(w_in["l0a"], 16)
                    pe.wait_ge(a_w, 1)
                    pe.sem_inc(a_pr, 2)

                    def convolve(u):
                        pe.wait_ge(hd_hT, u + (head0[l] + 1))
                        for dst, wt in ((PS[:, 0, 0:L], wkc), (PS[:, 7, L:2 * L], wsc)):
                            for j in range(TAPS - 1, -1, -1):
                                back = TAPS - 1 - j
                                ins = pe.matmul(dst[:, back:L], wt[:, j, :], hT[:, 0:L - back],
                                                start=back == 0, stop=back == TAPS - 1)
                        ins.then_inc(a_z, 1)

                    def factors(u, c):
                        pe.wait_ge(a_pr, u * CHUNKS + (c + 1))
                        for g, wt in ((0, wA), (1, wB)):
                            for m in range(CHUNK_M):
                                ins = pe.matmul(PS[:, 1 + 2 * (c % 2) + g, m * L:(m + 1) * L],
                                                wt[:, c * CHUNK_M + m, :], hT[:], start=True, stop=True)
                        ins.then_inc(a_ab, 1)

                    def sums(u, c):
                        pe.wait_ge(a_pr, u * CHUNKS + (c + 3))
                        for b in (cb, sbuf):
                            for m in range(CHUNK_M):
                                first = c == 0 and m == 0 and b is cb
                                last = c == CHUNKS - 1 and m == CHUNK_M - 1 and b is sbuf
                                ins = pe.matmul(PS[:, 5, 0:L], ident, b[:, c, m], start=first, stop=last)
                        ins.then_inc(a_sum, 1)

                    def unit(i, more):
                        factors(i, 0)
                        factors(i, 1)
                        sums(i, 0)
                        factors(i, 2)
                        sums(i, 1)
                        factors(i, 3)
                        head_transpose(l, i)
                        if more:
                            convolve(i + 1)
                        sums(i, 2)
                        sums(i, 3)
                        pe.wait_ge(a_yT, i + 1)
                        y_free(i)
                        for t in range(T):
                            ins = pe.matmul(Y[:, t, :], yT[:, t * P:(t + 1) * P], w("l0a", "wout"), start=True, stop=True)
                        ins.then_inc(y_ready, 1)

                    convolve(0)
                    with pe.Fori(0, NB - 1) as i:
                        unit(i, True)
                    unit(NB - 1, False)
                elif l in AT:
                    a = AT[l]
                    name = {L1_ATTN: "l1a", L2_ATTN: "l2a", L3_ATTN: "l3a"}[l]
                    causal = l != L1_ATTN
                    ntr = 3 if l == L3_ATTN else 4
                    early = EARLY[l]
                    rows = PARTS if l == L2_ATTN else PARTS + AUG
                    lead = 3 if l == L2_ATTN else 2

                    def project(u):
                        pe.wait_ge(hd_hT, u + (head0[l] + 1))
                        if l == L3_ATTN:
                            pe.matmul(PS[0:64, 2, 0:L], w(name, "down"), hT[:], start=True, stop=True).then_inc(a["lat"], 1)
                        else:
                            for t in range(T):
                                ins = pe.matmul(PS[:, 2 + t, 0:3 * D], hT[:, t * P:(t + 1) * P], w(name, "wqkv"),
                                                start=True, stop=True)
                            ins.then_inc(a["qkv"], 1)

                    def project_up(u):
                        pe.wait_ge(a["lats"], u + 1)
                        for t in range(T):
                            ins = pe.matmul(PS[:, 2 + t, 0:D + 2 * HD], latT[:, t * P:(t + 1) * P],
                                            w(name, "up")[0:64], start=True, stop=True)
                        ins.then_inc(a["qkv"], 1)

                    def parts_transpose(u, last):
                        pe.wait_ge(a["split"], u + 1)
                        if l == L3_ATTN:
                            for t in range(T):
                                ins = pe.transpose(PSB[:, 2, t * P:(t + 1) * P],
                                                   KS[:, t * NH:t * NH + 2, :].rearrange("p a b -> p (a b)"), identb)
                            ins.then_inc(a["tr"], 1)
                        for src, bank in (((QS, 0),) if l == L3_ATTN else ((KS, 2), (QS, 0))):
                            if src is QS and last is not None:
                                pe.wait_ge(a["pt"], last * NH + NH)
                            for t in range(T):
                                for b in range(NH // 2):
                                    s = t * NH + 2 * b
                                    ins = pe.transpose(PSB[:, bank + t, b * P:(b + 1) * P],
                                                       src[:, s:s + 2, :].rearrange("p a b -> p (a b)"), identb)
                                ins.then_inc(a["tr"], 1)

                    def parts_ready(u):
                        pe.wait_ge(a["eva"], u * 2 + 2)
                        pe.wait_ge(a["evd"], u * (ntr - 2) + (ntr - 2))

                    def maxima_transpose(u, k):
                        pe.wait_ge(a["m"], u * 2 + (k + 1))
                        for b in range(NH // 4):
                            for t in range(T):
                                s = t * NH + k * (NH // 2) + 2 * b
                                ins = pe.transpose(PSB[:, 7, b * L + t * P:b * L + (t + 1) * P],
                                                   QS[:, s:s + 2, :].rearrange("p a b -> p (a b)"), identb)
                        ins.then_inc(a["mtr"], 1)

                    def scores_for_maximum(u, hh):
                        b, r = (hh % 4 if hh < 2 * PAIRS else 2 + hh % 2), 64 * (hh % 2)
                        if causal:
                            pe.matmul(PS[:, b, 0:384], identb, w("cbf", "mask_q"), start=True, stop=False,
                                      skip_group_check=True)
                        for t in range(T):
                            o = slice(0, P) if causal and t == 0 else slice(P, 384) if causal else slice(t * L, (t + 1) * L)
                            ins = pe.matmul(PS[:, b, o], QT[r:r + PARTS, hh // 2, t * P:(t + 1) * P],
                                            KT[r:r + PARTS, 0 if l == L3_ATTN else hh // 2, 0:o.stop - o.start],
                                            start=not causal, stop=True, skip_group_check=causal)
                        return ins

                    def pair_for_maxima(u, pair):
                        if pair >= 2:
                            pe.wait_ge(a["mx"], u * MAX_STEPS + (pair - 1))
                        scores_for_maximum(u, 2 * pair)
                        scores_for_maximum(u, 2 * pair + 1).then_inc(a["s"], 1)

                    def single_for_maximum(u, hh):
                        n = hh - 2 * PAIRS
                        pe.wait_ge(a["mx"], u * MAX_STEPS + (PAIRS + max(n - 1, 0)))
                        scores_for_maximum(u, hh).then_inc(a["s"], 1)

                    def maxima(u, done):
                        for pair in range(PAIRS):
                            pair_for_maxima(u, pair)
                            if pair == 1 and done is not None:
                                outputs_transpose(done)
                        if done is not None:
                            outputs_back(done)
                        single_for_maximum(u, 8)
                        single_for_maximum(u, 9)
                        if done is not None:
                            project_out(done)
                        maxima_transpose(u, 0)
                        single_for_maximum(u, 10)
                        single_for_maximum(u, 11)
                        pe.wait_ge(a["mev"], u * 2 + 1)
                        scores(u, 0)
                        scores(u, 1)
                        for n in range(4):
                            single_for_maximum(u, 12 + n)
                            if 2 + n < early:
                                scores(u, 2 + n)
                                values(u, n)

                    def scores(u, hh):
                        r, kh = 64 * (hh % 2), 0 if l == L3_ATTN else hh // 2
                        if hh >= 2:
                            pe.wait_ge(a["pt"], u * NH + (hh - 1))
                        b = hh % 2
                        if causal:
                            pe.matmul(PS[:, b, 0:384], identb, w("cbf", "mask_k"), start=True, stop=False,
                                      skip_group_check=True)
                            pe.matmul(PS[:, b, 0:L], KT[r:r + rows, kh, 0:P], QT[r:r + rows, hh // 2, :],
                                      start=False, stop=True, skip_group_check=True)
                            ins = pe.matmul(PS[:, b, L:384], KT[r:r + rows, kh, P:L],
                                            QT[r:r + rows, hh // 2, P:L], start=False, stop=True,
                                            skip_group_check=True)
                        else:
                            for t in range(T):
                                ins = pe.matmul(PS[:, b, t * L:(t + 1) * L], KT[r:r + rows, kh, t * P:(t + 1) * P],
                                                QT[r:r + rows, hh // 2, :], start=True, stop=True)
                        ins.then_inc(a["st"], 1)

                    def values(u, hh):
                        vh, j, g = 0 if l == L3_ATTN else hh, hh % HG, hh // HG
                        if l == L2_ATTN:
                            pe.wait_ge(a["m"], u * NH + (hh + 1))
                            if hh % 4 == 3:
                                pe.wait_ge(a["pg"], u * (NH // 4) + (hh // 4 + 1))
                            srcs = (PG, PN)
                        else:
                            pe.wait_ge(a["pt"], u * NH + (hh + 1))
                            srcs = (PT,)
                        at = (g % 2) * L
                        for n, s in enumerate(srcs):
                            for kt in range(T):
                                q0 = P if causal and kt == 1 else 0
                                ins = pe.matmul(PS[j * VW:(j + 1) * VW, 4 + g // 2, at + q0:at + L], VA[:, kt, vh, :],
                                                s[:, hh % 4, kt * L:(kt + 1) * L - q0],
                                                start=n == 0 and kt == 0, stop=n == len(srcs) - 1 and kt == 1,
                                                tile_position=(0, j * VW), skip_group_check=True)
                        ins.then_inc(a["pv"], 1)

                    def outputs_transpose(u):
                        pe.wait_ge(a["ot"], u + 1)
                        for n in range(T * NH // HG):
                            ins = pe.transpose(PS[:, 4 + n // 4, (n % 4) * P:(n % 4 + 1) * P],
                                               OT[:, n * P:(n + 1) * P], ident)
                        ins.then_inc(a["otr"], 1)

                    def outputs_back(u):
                        pe.wait_ge(a["o"], u + 1)
                        y_free(u)
                        for t in range(T):
                            ins = pe.transpose(PS[:, 6, L + t * P:L + (t + 1) * P], osb[:, t, :], ident)
                        ins.then_inc(a["oT"], 1)

                    def project_out(u):
                        pe.wait_ge(a["oTs"], u + 1)
                        for t in range(T):
                            ins = pe.matmul(Y[:, t, :], oT[:, t * P:(t + 1) * P], w(name, "wout"), start=True, stop=True)
                        ins.then_inc(y_ready, 1)

                    def attend(u, more):
                        if l != L2_ATTN:
                            pe.wait_ge(a["mx"], (u + 1) * MAX_STEPS)
                            if more:
                                project(u + 1)
                        for hh in range(early, NH + lead):
                            if hh == NH // 2 and l != L2_ATTN:
                                pe.wait_ge(a["mev"], u * 2 + 2)
                            if hh < NH:
                                scores(u, hh)
                            if hh == early and l == L2_ATTN and more:
                                project(u + 1)
                            if hh == early and l == L3_ATTN and more:
                                project_up(u + 1)
                            if hh == early and l != L2_ATTN:
                                maxima_transpose(u, 1)
                            if hh == NH - 1 and more:
                                head_transpose(l, u + 1)
                            if hh >= lead:
                                values(u, hh - lead)

                    def finish(u):
                        outputs_transpose(u)
                        outputs_back(u)
                        project_out(u)

                    pe.wait_ge(w_in[name], 16)
                    pe.sem_inc(a["pv"], 4)
                    project(0)
                    if l == L3_ATTN:
                        project_up(0)
                    head_transpose(l, 0)
                    parts_transpose(0, None)
                    parts_ready(0)
                    if l == L2_ATTN:
                        for hh in range(early):
                            scores(0, hh)
                    else:
                        maxima(0, None)
                    with pe.Fori(0, NB - 1) as i:
                        attend(i, True)
                        parts_transpose(i + 1, i)
                        if l == L2_ATTN:
                            outputs_transpose(i)
                            parts_ready(i + 1)
                            for hh in range(early):
                                scores(i + 1, hh)
                            outputs_back(i)
                            project_out(i)
                        else:
                            parts_ready(i + 1)
                            maxima(i + 1, i)
                    attend(NB - 1, False)
                    finish(NB - 1)
                elif l == L2_FFN:
                    f, GATE = FF[l], GATES[l]
                    pe.wait_ge(w_in["l2f"], 16)
                    pe.sem_inc(f["y"], 2)
                    pe.sem_inc(f["o"], 2)
                    pe.sem_inc(f["oc"], 2)

                    def inner_transpose(u):
                        pe.wait_ge(m_n1, u + 1)
                        for t in range(T):
                            ins = pe.transpose(PS[:, 1, t * P:(t + 1) * P], n1[:, t, :], ident)
                        ins.then_inc(m_tr, 1)

                    def short_qkv(u):
                        pe.wait_ge(m_n1T, u + 1)
                        for t in range(T):
                            ins = pe.matmul(PS[:, 3, t * 192:(t + 1) * 192], n1T[:, t * P:(t + 1) * P],
                                            w("l2f", "qkv"), start=True, stop=True)
                        ins.then_inc(m_qkv, 1)

                    def short_transpose(u):
                        pe.wait_ge(m_ao, u + 1)
                        for t in range(T):
                            ins = pe.transpose(PS[:, 1, t * P:(t + 1) * P],
                                               ao[:, t * NH:(t + 1) * NH, :].rearrange("p a b -> p (a b)"), ident)
                        ins.then_inc(m_aT, 1)

                    def short_project(u):
                        pe.wait_ge(m_aTs, u + 1)
                        for t in range(T):
                            ins = pe.matmul(PS[:, 3, t * P:(t + 1) * P], aoT[:, t * P:(t + 1) * P],
                                            w("l2f", "proj"), start=True, stop=True)
                        ins.then_inc(m_y, 1)

                    def router(u):
                        pe.wait_ge(hd_hT, u + (head0[l] + 2))
                        for t in range(T):
                            ins = pe.matmul(GATE[:, t, 0:E8], hT[:, t * P:(t + 1) * P], w("l2f", "router"),
                                            start=True, stop=True)
                        ins.then_inc(f["gate"], 1)

                    def earlier(u):
                        pe.wait_ge(f["rk"], u + 1)
                        for t in range(T):
                            pe.matmul(GATE[:, t, 8:16], w("cbf", "before"), mbf[:, t, :], start=True, stop=False)
                            ins = pe.matmul(GATE[:, t, 8:16], w("cbf", "ones"), (cum if t == 0 else cum1)[:],
                                            start=False, stop=True)
                        ins.then_inc(f["c"], 1)

                    def up(u, c):
                        pe.wait_ge(f["y"], u * E8 + (c + 1))
                        for b in range(2):
                            ins = pe.matmul(PS[:, 2 * (c % 2), b * L:(b + 1) * L],
                                            w("l2f", "w1")[:, (2 * c + b) * P:(2 * c + b + 1) * P], hT[:],
                                            start=True, stop=True)
                        ins.then_inc(f["g"], 1)

                    def down(u, c):
                        pe.wait_ge(f["y"], u * E8 + (c + 3))
                        pe.wait_ge(f["oc"], u * E8 + (c + 1))
                        for t in range(T):
                            for b in range(2):
                                ins = pe.matmul(PS[:, 4 + c % 2, t * P:(t + 1) * P],
                                                y[:, c % 2, b * L + t * P:b * L + (t + 1) * P],
                                                w("l2f", "w2")[:, (2 * c + b) * D:(2 * c + b + 1) * D],
                                                start=b == 0, stop=b == 1)
                        ins.then_inc(f["o"], 1)

                    inner_transpose(0)
                    short_qkv(0)
                    short_transpose(0)
                    short_project(0)
                    head_transpose(l, 0)
                    router(0)
                    inner_transpose(1)
                    short_qkv(1)
                    up(0, 0)
                    earlier(0)
                    with pe.Fori(0, NB - 1) as i:
                        for c in range(1, E8):
                            up(i, c)
                            if c == 6:
                                short_project(i + 1)
                            down(i, c - 1)
                            if c == 5:
                                short_transpose(i + 1)
                        head_transpose(l, i + 1)
                        down(i, E8 - 1)
                        router(i + 1)
                        inner_transpose(i + 2)
                        short_qkv(i + 2)
                        up(i + 1, 0)
                        earlier(i + 1)
                    for c in range(1, E8):
                        up(NB - 1, c)
                        down(NB - 1, c - 1)
                    down(NB - 1, E8 - 1)
                else:
                    f, GATE = FF[l], GATES[l]
                    name = {L0_FFN: "l0f", L1_FFN: "l1f", L3_FFN: "l3f"}[l]
                    n_chunks = {L0_FFN: 8, L1_FFN: 2, L3_FFN: 5}[l]
                    experts = E16 if l == L3_FFN else E8
                    pe.wait_ge(w_in[name], 16)
                    pe.sem_inc(f["y"], 2)
                    pe.sem_inc(f["o"], 2)
                    pe.sem_inc(f["oc"], 2)

                    def router(src):
                        for t in range(T):
                            ins = pe.matmul(GATE[:, t, 0:experts], src[:, t * P:(t + 1) * P], w(name, "router"),
                                            start=True, stop=True)
                        ins.then_inc(f["gate"], 1)

                    unit_ready(0)
                    router(hT)
                    with pe.Fori(0, NB) as i:
                        unit_ready(i)

                        def up(c):
                            pe.wait_ge(f["y"], i * n_chunks + (2 if l == L3_FFN and c == 0 else c + 1))
                            if l == L0_FFN:
                                srcs = [(g, w(name, "w1")[:, ((c * 2 + g) * 2 + b) * P:((c * 2 + g) * 2 + b + 1) * P], b)
                                        for g in range(2) for b in range(2)]
                            elif l == L3_FFN and c > 0:
                                srcs = [(g, w(name, n)[:, (2 * c - 2 + b) * P:(2 * c - 1 + b) * P], b)
                                        for g, n in ((0, "w1"), (1, "w3")) for b in range(2)]
                            elif l == L3_FFN:
                                srcs = [(0, w(name, "w1s"), 0), (1, w(name, "w3s"), 0)]
                            else:
                                srcs = [(0, w(name, "w1")[:, (2 * c + b) * P:(2 * c + b + 1) * P], b) for b in range(2)]
                            for g, wt, b in srcs:
                                ins = pe.matmul(PS[:, 2 * (c % 2) + g, b * L:(b + 1) * L], wt, hT[:], start=True, stop=True)
                            ins.then_inc(f["g"], 1)

                        def share(c):
                            if c == 1:
                                pe.wait_ge(f["c"], i + 1)
                            for b in range(2):
                                for t in range(T):
                                    e = 2 * (2 * (c - 1) + b)
                                    ins = pe.transpose(
                                        PS[:, 4 + c % 2, b * L + t * P:b * L + (t + 1) * P],
                                        cwx[:, t, e:e + 2, :].rearrange("p e f -> p (e f)"), ident)
                            ins.then_inc(f["cT"], 1)

                        def down(c):
                            pe.wait_ge(f["y"], i * n_chunks + (c + 3))
                            if l == L0_FFN:
                                pe.wait_ge(f["oc"], i * n_chunks + (c + 1))
                                for t in range(T):
                                    for b in range(2):
                                        ins = pe.matmul(
                                            PS[:, 4 + c % 2, t * P:(t + 1) * P],
                                            y[:, c % 2, b * L + t * P:b * L + (t + 1) * P],
                                            w(name, "w2")[:, (2 * c + b) * D:(2 * c + b + 1) * D],
                                            start=b == 0, stop=b == 1)
                            else:
                                if c == 0 and l == L1_FFN:
                                    pe.wait_ge(f["oc"], i + 2)
                                elif c == 0:
                                    y_free(i)
                                nb = 1 if l == L3_FFN and c == 0 else 2
                                k = c - 1 if l == L3_FFN else c
                                for b in range(nb):
                                    for t in range(T):
                                        w2 = (w(name, "w2s") if nb == 1 else
                                              w(name, "w2")[:, (2 * k + b) * D:(2 * k + b + 1) * D])
                                        ins = pe.matmul(Y[:, t, :], y[:, c % 2, b * L + t * P:b * L + (t + 1) * P], w2,
                                                        start=c == 0 and b == 0 and t == 0,
                                                        stop=c == n_chunks - 1 and b == nb - 1,
                                                        skip_group_check=True)
                            ins.then_inc(f["o"], 1)

                        for c in range(n_chunks + 1):
                            if c < n_chunks:
                                up(c)
                            if c == HEAD_AT[l]:
                                head_transpose(l, i)
                            if l == L3_FFN and 2 <= c < n_chunks:
                                share(c)
                            if c == ROUTE_AT[l] and l == L0_FFN:
                                pe.wait_ge(f["hn"], i + 1)
                                router(hN)
                            if c >= 1:
                                down(c - 1)
                            if c == 1 and l == L3_FFN:
                                pe.wait_ge(f["hn"], i + 1)
                                router(hN)
                                share(1)
                            if c == ROUTE_AT[l] == n_chunks:
                                pe.wait_ge(f["hn"], i + 1)
                                router(hN)

        @block.vector
        def _(dve):
            def head_stats(src, u):
                for t in range(T):
                    dve.bn_stats(hst[:, t, :], src[:, bass.ds(u * T + t, 1), :].rearrange("p a b -> p (a b)"))
                dve.drain()
                for t in range(T):
                    ins = dve.bn_aggr(hmv[:, t, :], hst[:, t, :])
                ins.then_inc(hd_stat, 1)

            def head_norm(src, u, count):
                dve.wait_ge(hd_tr, count - 1)
                dve.wait_ge(hd_rstd, count)
                for t in range(T):
                    ins = dve.tensor_scalar(h[:, t, :], src[:, bass.ds(u * T + t, 1), :].rearrange("p a b -> p (a b)"),
                                            hmv[:, t, 0:1], hrs[:, t:t + 1], ALU.subtract, ALU.mult)
                ins.then_inc(hd_h, 1)

            def tail_stats(src):
                for t in range(T):
                    dve.bn_stats(tst[:, t, :], src[:, t, :])
                dve.drain()
                for t in range(T):
                    ins = dve.bn_aggr(tmv[:, t, :], tst[:, t, :])
                ins.then_inc(tl_stat, 1)

            def tail_add(l, i, src):
                dve.wait_ge(tl_rstd, i + (tail0[l] + 1))
                for t in range(T):
                    dve.tensor_scalar(tn[:, t, :], src[:, t, :], tmv[:, t, 0:1], trs[:, t:t + 1],
                                      ALU.subtract, ALU.mult)
                dve.drain()
                dve.tensor_tensor(X[:, bass.ds(i * T, T), :], X[:, bass.ds(i * T, T), :], tn[:], ALU.add)\
                   .then_inc(x_done, 1)
                dve.drain()

            def tail(l, i, src):
                tail_stats(src)
                tail_add(l, i, src)

            def gate_less_max(f, GATE, u):
                dve.wait_ge(f["gate"], u + 1)
                g8 = GATE[:, :, 0:E8]
                dve.tensor_reduce(gmx[:], g8, AX.X, ALU.max)
                dve.drain()
                dve.tensor_tensor(lg[:, :, 0:E8], g8, gmx[:].unsqueeze(2).to_broadcast([P, T, E8]),
                                  ALU.subtract).then_inc(f["ge"], 1)

            def gate_share(f, u, cw):
                e8 = ex[:, :, 0:E8]
                dve.wait_ge(f["gx"], u + 1)
                dve.tensor_reduce(gsm[:], e8, AX.X, ALU.add)
                dve.drain()
                dve.reciprocal(gsm[:], gsm[:])
                dve.drain()
                dve.tensor_tensor(cw[:, :, 0:E8], e8, gsm[:].unsqueeze(2).to_broadcast([P, T, E8]), ALU.mult)
                dve.drain()

            def top(p, n, k, weighted, scratch_rank, lower):
                top_compare(p, n, lower)
                top_rank(p, n, k, weighted, scratch_rank)

            def top_compare(p, n, lower):
                gt = gtb[:, :, 0:n * n].rearrange("p t (j i) -> p t j i", i=n)
                eq = eqb[:, :, 0:n * n].rearrange("p t (j i) -> p t j i", i=n)
                other = p.unsqueeze(2).to_broadcast([P, T, n, n])
                own = p.unsqueeze(3).to_broadcast([P, T, n, n])
                dve.tensor_tensor(eq, other, own, ALU.is_equal)
                dve.tensor_tensor(gt, other, own, ALU.is_gt)
                dve.drain()
                dve.tensor_tensor(eq, eq, lower.rearrange("p (a j i) -> p a j i", a=1, i=n).to_broadcast([P, T, n, n]),
                                  ALU.mult)
                dve.drain()
                dve.tensor_tensor(gt, gt, eq, ALU.add)
                dve.drain()

            def top_rank(p, n, k, weighted, scratch_rank):
                gt = gtb[:, :, 0:n * n].rearrange("p t (j i) -> p t j i", i=n)
                dve.tensor_reduce(scratch_rank, gt, AX.X, ALU.add)
                dve.drain()
                if weighted is not None:
                    dve.scalar_tensor_tensor(weighted, scratch_rank, float(k), p, ALU.is_lt, ALU.mult)
                    dve.drain()

            dve.wait_ge(x_in, 16)
            dve.wait_ge(consts, 1)
            dve.wait_ge(w_in["const"], 16)
            for l in run:
                if own_head(l):
                    head_stats(X, 0)
                    dve.wait_ge(hd_rstd, head0[l] + 1)
                    if head0[l]:
                        dve.wait_ge(hd_tr, head0[l])
                    for t in range(T):
                        ins = dve.tensor_scalar(h[:, t, :], X[:, t, :], hmv[:, t, 0:1], hrs[:, t:t + 1],
                                                ALU.subtract, ALU.mult)
                    ins.then_inc(hd_h, 1)
                    dve.drain()
                if order[l] == 0:
                    dve.wait_ge(x_rest, 16)
                    dve.wait_ge(wb_in, 16)
                    dve.tensor_copy(W["cbf"][:], cbf_f[:, 0:PACKS_BF["cbf"].width]).then_inc(cbf_ready, 1)

                if l == L0_ATTN:
                    dve.wait_ge(w_in["l0a"], 16)
                    for dst, wt, cv in ((wkc, "wk", "conv_k"), (wsc, "ws", "conv_s")):
                        dve.tensor_tensor(dst[:], w("l0a", wt).unsqueeze(1).to_broadcast([P, TAPS, D]),
                                          w("l0a", cv).rearrange("p (j d) -> p j d", j=TAPS), ALU.mult)
                    dve.tensor_tensor(coef[:, 0, :], w("l0a", "norm_re"), w("l0a", "diag_re"), ALU.mult)
                    dve.tensor_tensor(coef[:, 1, :], w("l0a", "norm_im"), w("l0a", "diag_im"), ALU.mult)
                    dve.drain()
                    dve.tensor_tensor(wab[:, 0, :], w("l0a", "wq_re"), coef[:, 0, :], ALU.mult)
                    dve.tensor_tensor(wab[:, 1, :], w("l0a", "wq_im"), coef[:, 0, :], ALU.mult)
                    dve.tensor_tensor(wtmp[:, 0, :], w("l0a", "wq_im"), coef[:, 1, :], ALU.mult)
                    dve.tensor_tensor(wtmp[:, 1, :], w("l0a", "wq_re"), coef[:, 1, :], ALU.mult)
                    dve.drain()
                    dve.tensor_tensor(wab[:, 0, :], wab[:, 0, :], wtmp[:, 0, :], ALU.subtract)
                    dve.tensor_tensor(wab[:, 1, :], wab[:, 1, :], wtmp[:, 1, :], ALU.add)
                    dve.drain()
                    rep = KCH // KQ
                    for g, dst in ((0, wA), (1, wB)):
                        for m in range(NM):
                            dve.tensor_copy(
                                dst[:, m, :].rearrange("p (q r h) -> p q r h", q=KQ, r=rep),
                                wab[:, g, :].rearrange("p (q a h m) -> p q a h m", q=KQ, a=1, h=HC)[:, :, :, :, m]
                                .to_broadcast([P, KQ, rep, HC]))
                    dve.tensor_scalar(theta[:], w("l0a", "theta"), float(1.0 / (2 * np.pi)), None, ALU.mult)
                    dve.wait_ge(a_soft, 1)
                    dve.tensor_tensor(slope[:, 0:1], slope[:, 2:3], slope[:, 3:4], ALU.add)
                    dve.drain()
                    dve.tensor_scalar(logw[:], w("const", "decay_pos"), slope[:, 0:1], None, ALU.mult)
                    dve.drain().then_inc(a_w, 1)

                    def exponents(u):
                        dve.wait_ge(a_z, u + 1)
                        dve.tensor_scalar(la[:], PS[:, 7, L:2 * L], w("l0a", "score"), 20.0, ALU.mult, ALU.min)
                        dve.drain()
                        dve.scalar_tensor_tensor(la[:], la[:], -20.0, logw[:], ALU.max, ALU.add).then_inc(a_lg, 1)

                    def reduce_turns(u, c):
                        dve.wait_ge(a_u, u * CHUNKS + (c + 1))
                        dve.tensor_scalar(sbuf[:, c], cb[:, c], MAGIC, None, ALU.add)
                        dve.drain()
                        dve.scalar_tensor_tensor(sbuf[:, c], sbuf[:, c], MAGIC, cb[:, c],
                                                 ALU.subtract, ALU.subtract).then_inc(a_red, 1)

                    def cumulate(u, c):
                        dve.wait_ge(a_pp, u * CHUNKS + (c + 1))
                        cf = carry[:].rearrange("p m t -> p (m t)")
                        for b in (cb, sbuf):
                            flat = b[:, c].rearrange("p m t -> p (m t)")
                            dve.tensor_tensor_scan(flat, cf, flat, 0.0, ALU.mult, ALU.add)
                        dve.drain()
                        dve.wait_ge(a_ab, u * CHUNKS + (c + 1))
                        for g, b in ((0, cb), (1, sbuf)):
                            flat = b[:, c].rearrange("p m t -> p (m t)")
                            ins = dve.tensor_tensor(flat, flat, PS[:, 1 + 2 * (c % 2) + g, :], ALU.mult)
                        ins.then_inc(a_pr, 1)

                    def unit(i, nxt, more):
                        head_stats(X, nxt)
                        reduce_turns(i, 2)
                        cumulate(i, 0)
                        reduce_turns(i, 3)
                        cumulate(i, 1)
                        head_norm(X, nxt, i + (head0[l] + 2))
                        dve.wait_ge(a_p, i + 1)
                        dve.tensor_tensor_scan(den[:], one_c[:].to_broadcast([P, L]), pw[:], 0.0, ALU.mult, ALU.add)
                        dve.drain()
                        dve.tensor_scalar(den[:], den[:], 1e-4, None, ALU.max)
                        dve.drain()
                        dve.reciprocal(inv[:], den[:])
                        cumulate(i, 2)
                        cumulate(i, 3)
                        if more:
                            exponents(i + 1)
                            reduce_turns(i + 1, 0)
                        dve.wait_ge(a_sum, i * CHUNKS + 2 * CHUNKS)
                        dve.tensor_tensor(arg[:], inv[:], PS[:, 5, 0:L], ALU.mult).then_inc(a_arg, 1)
                        if more:
                            reduce_turns(i + 1, 1)
                        dve.wait_ge(y_ready, i + (res0[l] + 1))
                        tail(l, i, Y)

                    exponents(0)
                    reduce_turns(0, 0)
                    reduce_turns(0, 1)
                    with dve.Fori(0, NB - 1) as i:
                        unit(i, i + 1, True)
                    unit(NB - 1, 0, False)
                elif l in AT:
                    a = AT[l]
                    name = {L1_ATTN: "l1a", L2_ATTN: "l2a", L3_ATTN: "l3a"}[l]
                    ntr = 3 if l == L3_ATTN else 4
                    early = EARLY[l]
                    nk = 1 if l == L3_ATTN else NH
                    nm = 2 if l == L1_ATTN else 3
                    result = acc if l == L1_ATTN else Y
                    QSv = QS[:].rearrange("p n (s d) -> p n s d", d=HD)
                    KSv = KS[:].rearrange("p n (s d) -> p n s d", d=HD)
                    kn = slice(0, T * NH, NH) if nk == 1 else slice(0, T * NH)

                    def load_qkv(u, last):
                        dve.wait_ge(a["qkv"], u + 1)
                        at = 0
                        for dst, width in ((qf, D), (kf, nk * HD), (vf, nk * HD)):
                            src = PS[:, 2:4, at:at + width]
                            dstv = dst[:].rearrange("p n d -> p (n d)")[:, 0:T * width].rearrange("p (t f) -> p t f", t=T)
                            if l == L1_ATTN:
                                dve.tensor_tensor(dstv, src, w(name, "bqkv")[:, at:at + width].unsqueeze(1)
                                                  .to_broadcast([P, T, width]), ALU.add)
                            else:
                                dve.tensor_copy(dstv, src)
                            at += width
                        dve.drain()
                        if last is not None and l != L2_ATTN:
                            dve.wait_ge(a["mtr"], last * 2 + 2)

                    def split(part):
                        for cur, dst, slots in ((qf[:], QSv, ((0, 7, 3), (1, 6, 3), (2, 6, 3))),
                                                (kf[:, 0:T * nk], KSv[:, kn], ((0, 3, 1), (3, 6, 1), (6, 7, 1)))):
                            s0, s1, st = slots[part]
                            n, cnt = cur.shape[1], len(range(s0, s1, st))
                            dve.tensor_copy(dst[:, :, s0:s1:st, :], cur.unsqueeze(2).to_broadcast([P, n, cnt, HD]))
                        dve.drain()
                        if part < 2:
                            for cur, dst, s0 in ((qf[:], QSv, part), (kf[:, 0:T * nk], KSv[:, kn], 3 * part)):
                                dve.tensor_tensor(cur, cur, dst[:, :, s0, :], ALU.subtract)
                            dve.drain()
                        elif l == L3_ATTN:
                            dve.tensor_copy(KS[:, 1:T * NH:NH, 0:PARTS], KS[:, 0:T * NH:NH, 0:PARTS])
                            dve.drain().then_inc(a["split"], 1)
                        else:
                            dve.drain().then_inc(a["split"], 1)

                    def load_values():
                        dve.tensor_scalar(VA[:, :, 0:nk, 0:HD],
                                          vf[:, 0:T * nk].rearrange("p (t a) d -> p t a d", t=T),
                                          1e-3 if l == L2_ATTN else 1.0, None, ALU.mult)

                    def parts_copy(u, last):
                        if last is not None:
                            dve.wait_ge(a["st"], last * NH + NH)
                        if l != L3_ATTN:
                            dve.wait_ge(a["tr"], u * ntr + 2)
                            dve.tensor_copy(KT[:, :, P:L], PSB[:, 3, :].rearrange("p (a b) -> p a b", b=P))\
                               .then_inc(a["evd"], 1)
                        dve.wait_ge(a["tr"], u * ntr + ntr)
                        dve.tensor_copy(QT[:, :, P:L], PSB[:, 1, :].rearrange("p (a b) -> p a b", b=P))\
                           .then_inc(a["evd"], 1)

                    def maximum(u, step):
                        dve.wait_ge(a["s"], u * MAX_STEPS + (step + 1))
                        keys = L if l == L1_ATTN else P
                        b, hh, n = ((2 * (step % 2), 2 * step, 2) if step < PAIRS else
                                    (2 + (step - PAIRS) % 2, step + PAIRS, 1))
                        dve.tensor_reduce(mx[:, hh:hh + n, 0:nm],
                                          PS[:, b:b + n, 0:nm * keys].rearrange("p a (t k) -> p a t k", t=nm),
                                          AX.X, ALU.max).then_inc(a["mx"], 1)

                    def maximum_parts(k):
                        hs = slice(k * NH // 2, (k + 1) * NH // 2)
                        dve.drain()
                        dve.tensor_scalar(mx[:, hs, 0:nm], mx[:, hs, 0:nm], -1.0, None, ALU.mult)
                        dve.drain()
                        if nm == 3:
                            dve.tensor_tensor(mx[:, hs, 1], mx[:, hs, 1], mx[:, hs, 2], ALU.min)
                            dve.drain()
                        m = mx[:, hs, 0:T].rearrange("p a t -> p t a")
                        QM = QS[:].rearrange("p (t a) c -> p t a c", t=T)[:, :, hs]
                        for part in range(AUG):
                            dve.tensor_copy(QM[:, :, :, PARTS + part], m)
                            dve.drain()
                            if part < AUG - 1:
                                dve.tensor_tensor(m, m, QM[:, :, :, PARTS + part], ALU.subtract)
                                dve.drain()
                        dve.drain().then_inc(a["m"], 1)

                    def normalise(u):
                        dve.wait_ge(a["otr"], u + 1)
                        O = PS[:, 4:6, :].rearrange("p b (g t j r) -> p t (b g) j r", g=2, t=T, j=HG)
                        ov = osb[:].rearrange("p t (g j d) -> p t g j d", g=NH // HG, j=HG)
                        if l == L2_ATTN:
                            for t in range(T):
                                ins = dve.tensor_copy(ov[:, t], O[:, t, :, :, 0:HD])
                        else:
                            rv = rsum[:].rearrange("p t (g j) -> p t g j", j=HG)
                            for t in range(T):
                                dve.reciprocal(rv[:, t], O[:, t, :, :, HD])
                            dve.drain()
                            for t in range(T):
                                ins = dve.tensor_tensor(ov[:, t], O[:, t, :, :, 0:HD],
                                                        rv[:, t].unsqueeze(3).to_broadcast([P, NH // HG, HG, HD]),
                                                        ALU.mult)
                        ins.then_inc(a["o"], 1)

                    def result_stats(u):
                        dve.wait_ge(y_ready, u + (res0[l] + 1))
                        if l == L1_ATTN:
                            dve.tensor_tensor(acc[:], Y, w(name, "bout").unsqueeze(1).to_broadcast([P, T, D]), ALU.add)
                            dve.drain()
                        tail_stats(result)

                    def linear(u, hh):
                        pn = PN[:, hh % 4, 0:384]
                        dve.wait_ge(a["pn"], u * NH + (hh + 1))
                        ins = dve.scalar_tensor_tensor(pn, pn, 2.0, pn, ALU.is_le, ALU.mult)
                        if hh % 4 < 3:
                            pt = PT[:, hh % 4, 0:384]
                            dve.wait_ge(a["pt"], u * NH + (hh + 1))
                            ins = dve.scalar_tensor_tensor(PG[:, hh % 4, 0:384], pt, 0.01, pt, ALU.add, ALU.mult)
                        ins.then_inc(a["m"], 1)

                    dve.wait_ge(w_in[name], 16)
                    head_stats(X, 1)
                    load_qkv(0, None)
                    for part in range(3):
                        split(part)
                    load_values()
                    head_norm(X, 1, head0[l] + 2)
                    parts_copy(0, None)
                    if l != L2_ATTN:
                        for step in range(MAX_STEPS):
                            maximum(0, step)
                            if step == PAIRS - 1:
                                maximum_parts(0)
                        maximum_parts(1)
                    if l == L2_ATTN:
                        for hh in range(early):
                            linear(0, hh)
                    with dve.Fori(0, NB - 1) as i:
                        nxt = (i + 2) % NB
                        head_stats(X, nxt)
                        if l == L2_ATTN:
                            for hh in range(early, NH):
                                linear(i, hh)
                                if hh == 2:
                                    load_qkv(i + 1, i)
                                if hh in (4, 6, 8):
                                    split((hh - 4) // 2)
                                if hh == 10:
                                    head_norm(X, nxt, i + (head0[l] + 3))
                            parts_copy(i + 1, i)
                            normalise(i)
                            load_values()
                            for hh in range(early):
                                linear(i + 1, hh)
                            result_stats(i)
                        else:
                            load_qkv(i + 1, i)
                            for part in range(3):
                                split(part)
                            head_norm(X, nxt, i + (head0[l] + 3))
                            parts_copy(i + 1, i)
                            for step in range(MAX_STEPS):
                                maximum(i + 1, step)
                                if step == 1:
                                    normalise(i)
                                    load_values()
                                if step == PAIRS - 1:
                                    maximum_parts(0)
                                if step == PAIRS + 2:
                                    result_stats(i)
                            maximum_parts(1)
                        tail_add(l, i, result)
                    if l == L2_ATTN:
                        for hh in range(early, NH):
                            linear(NB - 1, hh)
                    normalise(NB - 1)
                    result_stats(NB - 1)
                    tail_add(l, NB - 1, result)
                elif l == L2_FFN:
                    f, GATE = FF[l], GATES[l]
                    crow = w("const", "causal8").rearrange("p (a b) -> p a b", b=NB)
                    flat = lambda a: a.rearrange("p a b -> p (a b)")

                    def x_stats(u):
                        for t in range(T):
                            dve.bn_stats(xst[:, t, :], flat(X[:, bass.ds(u * T + t, 1), :]))
                        dve.drain()
                        for t in range(T):
                            ins = dve.bn_aggr(xmv[:, t, :], xst[:, t, :])
                        ins.then_inc(m_xst, 1)

                    def hidden_state(count, u):
                        dve.wait_ge(m_xrs, count)
                        for t in range(T):
                            dve.tensor_scalar(flat(H1[:, bass.ds(u * T + t, 1), :]), flat(X[:, bass.ds(u * T + t, 1), :]),
                                              xmv[:, t, 0:1], xrs[:, t:t + 1], ALU.subtract, ALU.mult)
                        dve.drain()

                    def inner_stats(u):
                        for t in range(T):
                            dve.bn_stats(nst[:, t, :], flat(H1[:, bass.ds(u * T + t, 1), :]))
                        dve.drain()
                        for t in range(T):
                            ins = dve.bn_aggr(nmv[:, t, :], nst[:, t, :])
                        ins.then_inc(m_st, 1)

                    def inner_norm(count, u):
                        dve.wait_ge(m_rs, count)
                        for t in range(T):
                            ins = dve.tensor_scalar(n1[:, t, :], flat(H1[:, bass.ds(u * T + t, 1), :]), nmv[:, t, 0:1],
                                                    nrs[:, t:t + 1], ALU.subtract, ALU.mult)
                        ins.then_inc(m_n1, 1)

                    def short_load(u):
                        dve.wait_ge(m_qkv, u + 1)
                        src = PS[:, 3, 0:T * 192].rearrange("p (t g c) -> p t g c", t=T, g=NG)
                        dve.tensor_scalar(q2[:].rearrange("p t g q d -> p t g (q d)"), src[:, :, :, 0:32], SM_SCALE, None,
                                          ALU.mult)
                        for t in range(T):
                            dve.tensor_copy(KC[:, t, :, bass.ds(u, 1), :].rearrange("p g a d -> p g (a d)"),
                                            src[:, t, :, 32:40])
                            dve.tensor_copy(VC[:, t, :, :, bass.ds(u, 1)].rearrange("p g d a -> p g (d a)"),
                                            src[:, t, :, 40:48])
                        dve.drain().then_inc(m_ld, 1)

                    def short_scores(u):
                        for n in range(T * NG - POOL_GROUPS):
                            key_products(dve, n)
                        dve.drain()
                        dve.wait_ge(m_kp, u + 1)
                        dve.tensor_reduce(flat(sc2[:]), prod.rearrange("p a (b d) -> p (a b) d", d=HD), AX.X, ALU.add)
                        dve.drain()

                    def short_less_max(u):
                        dve.tensor_tensor(sc2[:], sc2[:], crow[:, bass.ds(u, 1), :].to_broadcast([P, T * NH, NB]),
                                          ALU.add)
                        dve.drain()
                        dve.tensor_reduce(mx2[:], sc2[:], AX.X, ALU.max)
                        dve.drain()
                        dve.tensor_tensor(sc2[:], sc2[:], mx2[:].unsqueeze(2).to_broadcast([P, T * NH, NB]),
                                          ALU.subtract).then_inc(m_sc, 1)

                    def short_values(u):
                        dve.wait_ge(m_ex, u + 1)
                        dve.tensor_reduce(sm2[:], ex2[:], AX.X, ALU.add)
                        for n in range(T * NG - POOL_GROUPS):
                            value_products(dve, n)
                        dve.drain()
                        dve.reciprocal(sm2[:], sm2[:])
                        dve.wait_ge(m_vp, u + 1)
                        dve.tensor_reduce(flat(ao[:]), prod.rearrange("p a (b s) -> p (a b) s", s=NB), AX.X, ALU.add)
                        dve.drain()
                        dve.tensor_tensor(ao[:], ao[:], sm2[:].unsqueeze(2).to_broadcast([P, T * NH, HD]),
                                          ALU.mult).then_inc(m_ao, 1)

                    def short_add(u):
                        dve.wait_ge(m_y, u + 1)
                        dve.tensor_tensor(H1[:, bass.ds(u * T, T), :], H1[:, bass.ds(u * T, T), :],
                                          PS[:, 3, 0:L].rearrange("p (t d) -> p t d", t=T), ALU.add)
                        dve.drain()

                    def choose(u):
                        gate_share(f, u, cw)
                        top(cw[:, :, 0:E8], E8, 2, cw[:, :, 0:E8], rank[:, :, 0:E8], w("const", "rank8"))
                        dve.tensor_reduce(gsm[:], cw[:, :, 0:E8], AX.X, ALU.add)
                        dve.tensor_scalar(mbf[:], rank[:, :, 0:E8], 2.0, None, ALU.is_lt)
                        dve.drain()
                        dve.tensor_tensor(cum1[:], cum[:], mbf[:, 0, :], ALU.add)
                        dve.reciprocal(gsm[:], gsm[:])
                        dve.drain().then_inc(f["rk"], 1)
                        dve.tensor_tensor(cw[:, :, 0:E8], cw[:, :, 0:E8],
                                          gsm[:].unsqueeze(2).to_broadcast([P, T, E8]), ALU.mult)
                        dve.drain()

                    def within_capacity(u):
                        dve.wait_ge(f["c"], u + 1)
                        dve.scalar_tensor_tensor(cw[:, :, 0:E8], GATE[:, :, 8:16], float(CAP),
                                                 cw[:, :, 0:E8], ALU.is_lt, ALU.mult)
                        dve.tensor_tensor(cum[:], cum1[:], mbf[:, 1, :], ALU.add)
                        dve.drain()

                    def combine(u, c):
                        dve.wait_ge(f["o"], u * E8 + (c + 3))
                        for t in range(T):
                            src = PS[:, 4 + c % 2, t * P:(t + 1) * P]
                            if c == 0:
                                ins = dve.tensor_scalar(acc[:, t, :], src, cw[:, t, 0:1], None, ALU.mult)
                            else:
                                ins = dve.scalar_tensor_tensor(acc[:, t, :], src, cw[:, t, c:c + 1], acc[:, t, :],
                                                               ALU.mult, ALU.add)
                        ins.then_inc(f["oc"], 1)
                        dve.drain()

                    def add_hidden(u):
                        dve.tensor_tensor(acc[:], acc[:], H1[:, bass.ds(u * T, T), :], ALU.add)
                        dve.drain()

                    dve.tensor_copy(H1[:, 0:T, :], h[:])
                    dve.drain()
                    inner_stats(0)
                    x_stats(1)
                    inner_norm(1, 0)
                    hidden_state(1, 1)
                    inner_stats(1)
                    short_load(0)
                    short_scores(0)
                    short_less_max(0)
                    short_values(0)
                    inner_norm(2, 1)
                    short_add(0)
                    head_stats(H1, 0)
                    head_norm(H1, 0, head0[l] + 2)
                    gate_less_max(f, GATE, 0)
                    choose(0)
                    within_capacity(0)
                    with dve.Fori(0, NB - 1) as i:
                        u, nxt = i + 1, (i + 2) % NB
                        short_load(u)
                        x_stats(nxt)
                        combine(i, 0)
                        short_scores(u)
                        combine(i, 1)
                        short_less_max(u)
                        combine(i, 2)
                        short_values(u)
                        combine(i, 3)
                        hidden_state(i + 2, nxt)
                        inner_stats(nxt)
                        combine(i, 4)
                        inner_norm(i + 3, nxt)
                        short_add(u)
                        head_stats(H1, u)
                        combine(i, 5)
                        head_norm(H1, u, i + (head0[l] + 3))
                        combine(i, 6)
                        combine(i, 7)
                        add_hidden(i)
                        tail_stats(acc)
                        gate_less_max(f, GATE, u)
                        tail_add(l, i, acc)
                        choose(u)
                        within_capacity(u)
                    for c in range(E8):
                        combine(NB - 1, c)
                    add_hidden(NB - 1)
                    tail(l, NB - 1, acc)
                else:
                    f, GATE = FF[l], GATES[l]
                    n_chunks = {L0_FFN: 8, L1_FFN: 2, L3_FFN: 5}[l]

                    def group_scores(u):
                        dve.wait_ge(f["gx"], u + 1)
                        dve.tensor_scalar(ex[:], ex[:], 1.0, None, ALU.add)
                        dve.drain()
                        dve.reciprocal(ex[:], ex[:])
                        dve.drain()
                        v = ex[:].rearrange("p t (g c) -> p (t g) c", c=4)
                        dve.tensor_tensor(hilo[:, 0], v[:, :, 0:2], v[:, :, 2:4], ALU.max)
                        dve.tensor_tensor(hilo[:, 1], v[:, :, 0:2], v[:, :, 2:4], ALU.min)
                        dve.drain()
                        dve.tensor_tensor(hilo[:, 2, :, 0], hilo[:, 0, :, 0], hilo[:, 0, :, 1], ALU.max)
                        dve.tensor_tensor(hilo[:, 2, :, 1], hilo[:, 0, :, 0], hilo[:, 0, :, 1], ALU.min)
                        dve.tensor_tensor(hilo[:, 3, :, 0], hilo[:, 1, :, 0], hilo[:, 1, :, 1], ALU.max)
                        dve.drain()
                        dve.tensor_tensor(hilo[:, 3, :, 1], hilo[:, 2, :, 1], hilo[:, 3, :, 0], ALU.max)
                        dve.drain()
                        dve.tensor_tensor(gsc[:].rearrange("p t g -> p (t g)"), hilo[:, 2, :, 0],
                                          hilo[:, 3, :, 1], ALU.add)
                        dve.drain()

                    def group_choice():
                        top(gsc[:], NG, 2, None, gal[:], w("const", "rank4"))
                        dve.tensor_scalar(gal[:], gal[:], 2.0, None, ALU.is_lt)
                        dve.drain()
                        dve.tensor_scalar(gsc[:], gal[:], -1.0, None, ALU.add)
                        ga = gal[:].unsqueeze(3).to_broadcast([P, T, NG, 4])
                        gb = gsc[:].unsqueeze(3).to_broadcast([P, T, NG, 4])
                        m4 = msk[:].rearrange("p t (g c) -> p t g c", c=4)
                        dve.tensor_tensor(m4, ex[:].rearrange("p t (g c) -> p t g c", c=4), ga, ALU.mult)
                        dve.drain()
                        dve.tensor_tensor(m4, m4, gb, ALU.add)
                        dve.drain()

                    def expert_shares():
                        top_rank(msk[:], E16, 4, msk[:], rank[:])
                        dve.tensor_reduce(gsm[:], msk[:], AX.X, ALU.add)
                        dve.drain()
                        dve.tensor_scalar(gsm[:], gsm[:], 1e-6, None, ALU.add)
                        dve.drain()
                        dve.reciprocal(gsm[:], gsm[:])
                        dve.drain()
                        dve.tensor_tensor(cwn[:], msk[:], gsm[:].unsqueeze(2).to_broadcast([P, T, E16]),
                                          ALU.mult).then_inc(f["cn"], 1)

                    def logits(u):
                        if l == L3_FFN:
                            dve.wait_ge(f["gate"], u + 1)
                            dve.tensor_scalar(lg[:], GATE, -80.0, None, ALU.max).then_inc(f["ge"], 1)
                        else:
                            gate_less_max(f, GATE, u)

                    def shares(u):
                        gate_share(f, u, cwn)
                        if l == L0_FFN:
                            top(cwn[:, :, 0:E8], E8, 2, cwn[:, :, 0:E8], rank[:, :, 0:E8], w("const", "rank8"))

                    def take_shares():
                        dve.tensor_copy(cw[:, :, 0:E8], cwn[:, :, 0:E8])
                        dve.drain()

                    def combine(u, c):
                        dve.wait_ge(f["o"], u * n_chunks + (c + 3))
                        for t in range(T):
                            src = PS[:, 4 + c % 2, t * P:(t + 1) * P]
                            if c == 0:
                                ins = dve.tensor_scalar(acc[:, t, :], src, cw[:, t, 0:1], None, ALU.mult)
                            else:
                                ins = dve.scalar_tensor_tensor(acc[:, t, :], src, cw[:, t, c:c + 1], acc[:, t, :],
                                                               ALU.mult, ALU.add)
                        ins.then_inc(f["oc"], 1)

                    def gated(u, c):
                        cols = L if l == L3_FFN and c == 0 else 2 * L
                        dve.wait_ge(f["sg"], u * n_chunks + (c + 1))
                        dve.wait_ge(f["o"], u * n_chunks + (2 if l == L3_FFN and c == 0 else c + 1))
                        ins = dve.tensor_tensor(y[:, c % 2, 0:cols], sg[:, c % 2, 0:cols],
                                                PS[:, 2 * (c % 2) + 1, 0:cols], ALU.mult)
                        if l == L3_FFN and c > 0:
                            dve.drain()
                            dve.wait_ge(f["cT"], u * 4 + c)
                            ins = dve.tensor_tensor(y[:, c % 2, :], y[:, c % 2, :], PS[:, 4 + c % 2, :], ALU.mult)
                        ins.then_inc(f["y"], 1)

                    logits(0)
                    if l == L3_FFN:
                        group_scores(0)
                        group_choice()
                        top_compare(msk[:], E16, w("const", "rank16"))
                        expert_shares()
                    else:
                        shares(0)
                        take_shares()


                    def unit(i, nxt, more):
                        def ahead():
                            if more:
                                head_stats(X, (i + 2) % NB)
                                if l != L1_FFN:
                                    gated(i + 1, 0)

                        if l == L0_FFN:
                            for c in range(1, n_chunks):
                                gated(i, c)
                                if c == 1:
                                    head_norm(X, nxt, i + (head0[l] + 2))
                                combine(i, c - 1)
                                dve.drain()
                                if c == 3:
                                    logits(i + 1)
                                if c == 5:
                                    gate_share(f, i + 1, cwn)
                                if c == 6:
                                    top_compare(cwn[:, :, 0:E8], E8, w("const", "rank8"))
                            combine(i, n_chunks - 1)
                            dve.drain()
                            tail_stats(acc)
                            ahead()
                            top_rank(cwn[:, :, 0:E8], E8, 2, cwn[:, :, 0:E8], rank[:, :, 0:E8])
                            take_shares()
                            tail_add(l, i, acc)
                        elif l == L1_FFN:
                            head_norm(X, nxt, i + (head0[l] + 2))
                            dve.wait_ge(f["o"], i * n_chunks + (n_chunks + 2))
                            dve.tensor_tensor(acc[:], Y, w("l1f", "b2").unsqueeze(1).to_broadcast([P, T, D]), ALU.add)\
                               .then_inc(f["oc"], 1)
                            dve.drain()
                            for t in range(T):
                                dve.tensor_scalar(acc[:, t, :], acc[:, t, :], cw[:, t, 7:8], None, ALU.mult)
                            dve.drain()
                            tail_stats(acc)
                            ahead()
                            logits(i + 1)
                            tail_add(l, i, acc)
                            shares(i + 1)
                            take_shares()
                        else:
                            head_norm(X, nxt, i + (head0[l] + 2))
                            gated(i, 1)
                            logits(i + 1)
                            group_scores(i + 1)
                            gated(i, 2)
                            group_choice()
                            gated(i, 3)
                            top_compare(msk[:], E16, w("const", "rank16"))
                            gated(i, 4)
                            expert_shares()
                            dve.wait_ge(f["o"], i * n_chunks + (n_chunks + 2))
                            tail_stats(Y)
                            ahead()
                            tail_add(l, i, Y)

                    head_stats(X, 1)
                    if l != L1_FFN:
                        gated(0, 0)
                    with dve.Fori(0, NB - 1) as i:
                        unit(i, i + 1, True)
                    unit(NB - 1, 0, False)


def _pack(fields, parts):
    out = []
    for name, width in fields.at.items():
        a = np.asarray(parts[name])
        a = a.reshape(1 if a.size == width[1] else a.shape[0], width[1])
        if a.shape[0] == 1:
            a = np.broadcast_to(a, (P, width[1]))
        if a.shape[0] < P:
            a = np.concatenate([a, np.zeros((P - a.shape[0], width[1]), a.dtype)])
        out.append(a)
    return np.ascontiguousarray(np.concatenate(out, axis=1), dtype=np.float32)


def _constants():
    r = np.arange(P)
    t = np.arange(L)
    lower = lambda n: (np.arange(n)[None, :] < np.arange(n)[:, None]).astype(np.float32).reshape(1, -1)
    pos = np.where((np.repeat(np.arange(KCH), HC) < KCH - HC)[:, None], -(L - 1 - t)[None, :], -t[None, :])
    causal8 = np.where(np.arange(NB)[None, :] > np.arange(NB)[:, None], NEG, 0.0).reshape(1, -1)
    const = _pack(PACKS["const"], dict(ident=np.eye(P), rank8=lower(E8), rank16=lower(E16), rank4=lower(NG),
                                       causal8=causal8, decay_pos=pos))
    later = np.where(r[None, :] > r[:, None], NEG, 0.0)
    mask_q = np.concatenate([later, np.zeros((P, P)), later], axis=1)
    mask_k = np.concatenate([np.where(r[:, None] > t[None, :], NEG, 0.0),
                             np.where(r[:, None] > r[None, :], NEG, 0.0)], axis=1)
    cbf = _pack(PACKS_BF["cbf"], dict(ident=np.eye(P), mask_q=mask_q, mask_k=mask_k,
                                      before=(r[:, None] < r[None, :]).astype(np.float32), ones=np.ones((P, P))))
    return const, cbf


def kernel(**inputs):
    import concourse.bacc as _bacc
    from concourse.bass_utils import run_bass_kernel_spmd as _run

    v = {k: np.asarray(a) for k, a in inputs.items()}
    W_in = v["L0_attn_W_in"]
    wq = W_in[:, D + KCH:].reshape(D, KQ, HC, NM, 2)
    conv = v["L0_attn_conv_k"][:, 0, :]
    over_q = lambda a: np.broadcast_to(a.reshape(1, 1, HC, 1), (1, KQ, HC, NM)).reshape(1, -1)
    norm = v["L0_attn_norm_scale"]
    heads = lambda a: np.ascontiguousarray(a.reshape(NH, 3, HD, -1).transpose(1, 0, 2, 3)).reshape(3 * D, -1)
    halves = lambda a: a.reshape(-1, 2, P, D).transpose(2, 0, 1, 3).reshape(P, -1)
    const, cbf = _constants()
    arrays = {
        "x": np.ascontiguousarray(v["L0_attn_x"]), "const": const, "cbf": cbf,
        "l0a": _pack(PACKS["l0a"], dict(
            wk=W_in[:, :D], ws=np.repeat(W_in[:, D:D + KCH], HC, axis=1), wq_re=wq[..., 0], wq_im=wq[..., 1],
            wout=v["L0_attn_W_out"], conv_k=conv[:, :D].reshape(1, -1),
            conv_s=np.repeat(conv[:, D:], HC, axis=1).reshape(1, -1), norm_re=over_q(norm[:HC]),
            norm_im=over_q(norm[HC:]), diag_re=over_q(np.diagonal(v["L0_attn_W_re"])),
            diag_im=over_q(np.diagonal(v["L0_attn_W_im"])), theta=v["L0_attn_theta"].reshape(P, NM),
            slope=np.repeat(np.concatenate([v["L0_attn_decay_slopes"], v["L0_attn_anchor_slopes"]]), HC)[:, None],
            score=np.repeat(v["L0_attn_score_scale"], HC)[:, None])),
        "l0f": _pack(PACKS["l0f"], dict(
            router=v["L0_ffn_router_w"].T, w1=v["L0_ffn_w1"].transpose(2, 0, 1),
            w2=halves(v["L0_ffn_w2"].transpose(0, 2, 1)))),
        "l1a": _pack(PACKS["l1a"], dict(
            wqkv=heads(v["L1_attn_Wqkv"]).T, bqkv=heads(v["L1_attn_bqkv"]).reshape(1, -1), wout=v["L1_attn_Wout"].T,
            bout=v["L1_attn_bout"].reshape(1, -1))),
        "l1f": _pack(PACKS["l1f"], dict(
            router=v["L1_ffn_Wr"].T, w1=v["L1_ffn_W1"][E8 - 1], b1=v["L1_ffn_b1"][E8 - 1].reshape(4, P).T,
            w2=v["L1_ffn_W2"][E8 - 1].reshape(4, P, D).transpose(1, 0, 2), b2=v["L1_ffn_b2"][E8 - 1].reshape(1, -1))),
        "l2a": _pack(PACKS["l2a"], dict(wqkv=v["L2_attn_W_attn"], wout=v["L2_attn_W_proj"])),
        "l2f": _pack(PACKS["l2f"], dict(
            ln1w=v["L2_ffn_ln1_weight"][:, None], ln1b=v["L2_ffn_ln1_bias"][:, None],
            ln2w=v["L2_ffn_ln2_weight"][:, None], ln2b=v["L2_ffn_ln2_bias"][:, None], qkv=v["L2_ffn_qkv_weight"].T,
            proj=v["L2_ffn_proj_weight"].T, router=v["L2_ffn_router_weight"],
            w1=v["L2_ffn_moe_w1"].transpose(1, 0, 2), w2=halves(v["L2_ffn_moe_w2"]))),
        "l3a": _pack(PACKS["l3a"], dict(
            down=v["L3_attn_Wc_down"], up=np.concatenate([v["L3_attn_Wq_up"], v["L3_attn_Wkv_up"]], axis=1),
            wout=v["L3_attn_Wc_proj"])),
        "l3f": _pack(PACKS["l3f"], dict(
            router=v["L3_ffn_w_gate"].T, w1=v["L3_ffn_w1_e"].transpose(2, 0, 1), w3=v["L3_ffn_w3_e"].transpose(2, 0, 1),
            w2=v["L3_ffn_w2_e"].transpose(0, 2, 1).reshape(8, P, D).transpose(1, 0, 2), w1s=v["L3_ffn_w1_s"].T,
            w3s=v["L3_ffn_w3_s"].T, w2s=v["L3_ffn_w2_s"].T)),
    }
    nc = _bacc.Bacc("TRN2", target_bir_lowering=False, num_devices=1)
    aps = {n: nc.dram_tensor("in_" + n, a.shape, F32, kind="ExternalInput").ap()
           for n, a in arrays.items()}
    out = nc.dram_tensor("result", (NB, L, D), F32, kind="ExternalOutput").ap()
    block_program(nc, aps["x"], {n: aps[n] for n in PACKS}, {"cbf": aps["cbf"]}, out)
    r = _run(nc, [{"in_" + n: a for n, a in arrays.items()}], core_ids=[0])
    return r.results[0]["result"]
```
